# Optimizing a Trainium2 kernel written in Bass

```python
import numpy as np
import jax
import jax.numpy as jnp

def _softmax(x, axis=-1):
    return jax.nn.softmax(x, axis=axis)

def _gelu(x):
    return jax.nn.gelu(x, approximate=True)

def _silu(x):
    return jax.nn.silu(x)

def _sigmoid(x):
    return jax.nn.sigmoid(x)

def _layernorm(x, axis=-1, eps=1e-05):
    m = jnp.mean(x, axis=axis, keepdims=True)
    v = jnp.var(x, axis=axis, keepdims=True)
    return (x - m) / jnp.sqrt(v + eps)

def _scatter_add(tgt, idx, src, axis=0):
    return tgt.at[idx].add(src)

def _segment_sum(src, seg, n):
    return jax.ops.segment_sum(src, seg, n)
kernel_name = 'mk_macaron_d2_jaxref_r4_4a4f8f'

def setup_inputs(seed: int=0):
    np.random.seed(seed)
    _w = jnp.asarray

    def _L0_attn_setup():
        import jax, jax.numpy as jnp
        import numpy as np
        B, S, D, H = (1, 1024, 256, 16)
        DH = D // H

        def _positional_encoding(seq_len, d_model, dtype):
            pos = jnp.arange(seq_len, dtype=dtype)[:, None]
            div = jnp.exp(jnp.arange(0, d_model, 2, dtype=dtype) * (-np.log(10000.0) / d_model))
            pe = jnp.zeros((seq_len, d_model), dtype=dtype)
            pe = pe.at[:, 0::2].set(jnp.sin(pos * div))
            pe = pe.at[:, 1::2].set(jnp.cos(pos * div))
            return pe
        key = jax.random.key(seed)
        ks = jax.random.split(key, 11)
        s = 1.0 / np.sqrt(D)
        return {'x': jax.random.normal(ks[0], (B, S, D), dtype=jnp.float32), 'Wq': jax.random.normal(ks[1], (D, D), dtype=jnp.float32) * s, 'bq': jnp.zeros((D,), dtype=jnp.float32), 'Wk': jax.random.normal(ks[2], (D, D), dtype=jnp.float32) * s, 'bk': jnp.zeros((D,), dtype=jnp.float32), 'Wv': jax.random.normal(ks[3], (D, D), dtype=jnp.float32) * s, 'bv': jnp.zeros((D,), dtype=jnp.float32), 'Wo': jax.random.normal(ks[4], (D, D), dtype=jnp.float32) * s, 'bo': jnp.zeros((D,), dtype=jnp.float32), 'gamma': jnp.ones((D,), dtype=jnp.float32), 'beta': jnp.zeros((D,), dtype=jnp.float32)}
    _L0_attn_in = _L0_attn_setup()

    def _L0_ffn_setup():
        import jax, jax.numpy as jnp
        import numpy as np
        B, N, D = (4, 512, 256)
        SPARSITY = 0.01
        key = jax.random.key(seed)
        k1, k2, k3 = jax.random.split(key, 3)
        x = jax.random.normal(k1, (B, N, D), dtype=jnp.float32)
        spatial = jax.random.normal(k2, (D, D), dtype=jnp.float32) * 0.02
        freq = jnp.fft.fft(spatial, axis=-1)
        k = int(D * SPARSITY)
        mag = jnp.abs(freq)
        kth = jax.lax.top_k(mag, k)[0][:, -1:]
        w_sparse = jnp.where(mag >= kth, freq, 0.0 + 0j)
        bias = jax.random.normal(k3, (D,), dtype=jnp.float32) * 0.01
        return {'x': x, 'w_freq_real': jnp.real(w_sparse).astype(jnp.float32), 'w_freq_imag': jnp.imag(w_sparse).astype(jnp.float32), 'bias': bias}
    _L0_ffn_in = _L0_ffn_setup()

    def _L1_attn_setup():
        import jax, jax.numpy as jnp
        import numpy as np
        LN_EPS = 1e-05

        def _silu(x):
            return x * jax.nn.sigmoid(x)
        key = jax.random.key(seed)
        ks = jax.random.split(key, 12)
        B, L, d_model = (2, 512, 256)
        d_inner, d_state, d_conv = (512, 16, 4)
        s = lambda fan: 1.0 / np.sqrt(fan)
        A = jnp.arange(1, d_state + 1, dtype=jnp.float32)[None, :] * jnp.ones((d_inner, 1), jnp.float32)
        return {'x': jax.random.normal(ks[0], (B, L, d_model), jnp.float32), 'w_in': jax.random.normal(ks[1], (d_model, 2 * d_inner), jnp.float32) * s(d_model), 'conv_w': jax.random.normal(ks[2], (d_inner, 1, d_conv), jnp.float32) * s(d_conv), 'conv_b': jax.random.normal(ks[3], (d_inner,), jnp.float32) * 0.02, 'w_xproj': jax.random.normal(ks[4], (d_inner, 2 * d_state), jnp.float32) * s(d_inner), 'w_dt': jax.random.normal(ks[5], (d_inner, d_inner), jnp.float32) * s(d_inner), 'b_dt': jax.random.normal(ks[6], (d_inner,), jnp.float32) * 0.02, 'A_log': jnp.log(A), 'D': jnp.ones((d_inner,), jnp.float32), 'w_out': jax.random.normal(ks[7], (d_inner, d_model), jnp.float32) * s(d_inner), 'ln_g': jnp.ones((d_model,), jnp.float32), 'ln_b': jnp.zeros((d_model,), jnp.float32)}
    _L1_attn_in = _L1_attn_setup()

    def _L1_ffn_setup():
        import jax, jax.numpy as jnp
        import numpy as np
        E, TOP_K, D, H = (8, 2, 256, 512)
        B, S = (2, 512)
        key = jax.random.key(seed)
        ks = jax.random.split(key, 10)
        s = 0.02
        return {'x': jax.random.normal(ks[0], (B, S, D), dtype=jnp.float32), 'gate_w': jax.random.normal(ks[1], (E, D), dtype=jnp.float32) * s, 'gate_b': jnp.zeros((E,), dtype=jnp.float32), 'w0': jax.random.normal(ks[2], (E, H, D), dtype=jnp.float32) * s, 'b0': jnp.zeros((E, H), dtype=jnp.float32), 'w1': jax.random.normal(ks[3], (E, H, D), dtype=jnp.float32) * s, 'b1': jnp.zeros((E, H), dtype=jnp.float32), 'w2': jax.random.normal(ks[4], (E, D, H), dtype=jnp.float32) * s, 'b2': jnp.zeros((E, D), dtype=jnp.float32)}
    _L1_ffn_in = _L1_ffn_setup()
    _d = {'L0_attn_x': _L0_attn_in['x'], 'L0_attn_Wq': _L0_attn_in['Wq'], 'L0_attn_bq': _L0_attn_in['bq'], 'L0_attn_Wk': _L0_attn_in['Wk'], 'L0_attn_bk': _L0_attn_in['bk'], 'L0_attn_Wv': _L0_attn_in['Wv'], 'L0_attn_bv': _L0_attn_in['bv'], 'L0_attn_Wo': _L0_attn_in['Wo'], 'L0_attn_bo': _L0_attn_in['bo'], 'L0_attn_gamma': _L0_attn_in['gamma'], 'L0_attn_beta': _L0_attn_in['beta'], 'L0_ffn_w_freq_real': _L0_ffn_in['w_freq_real'], 'L0_ffn_w_freq_imag': _L0_ffn_in['w_freq_imag'], 'L0_ffn_bias': _L0_ffn_in['bias'], 'L1_attn_w_in': _L1_attn_in['w_in'], 'L1_attn_conv_w': _L1_attn_in['conv_w'], 'L1_attn_conv_b': _L1_attn_in['conv_b'], 'L1_attn_w_xproj': _L1_attn_in['w_xproj'], 'L1_attn_w_dt': _L1_attn_in['w_dt'], 'L1_attn_b_dt': _L1_attn_in['b_dt'], 'L1_attn_A_log': _L1_attn_in['A_log'], 'L1_attn_D': _L1_attn_in['D'], 'L1_attn_w_out': _L1_attn_in['w_out'], 'L1_attn_ln_g': _L1_attn_in['ln_g'], 'L1_attn_ln_b': _L1_attn_in['ln_b'], 'L1_ffn_gate_w': _L1_ffn_in['gate_w'], 'L1_ffn_gate_b': _L1_ffn_in['gate_b'], 'L1_ffn_w0': _L1_ffn_in['w0'], 'L1_ffn_b0': _L1_ffn_in['b0'], 'L1_ffn_w1': _L1_ffn_in['w1'], 'L1_ffn_b1': _L1_ffn_in['b1'], 'L1_ffn_w2': _L1_ffn_in['w2'], 'L1_ffn_b2': _L1_ffn_in['b2']}
    _x0 = _d['L0_attn_x']
    _d['L0_attn_x'] = jax.random.normal(jax.random.fold_in(jax.random.key(seed), 1), (8, 512, 256), dtype=_x0.dtype)
    del _x0
    return _d

def reference(L0_attn_x, L0_attn_Wq, L0_attn_bq, L0_attn_Wk, L0_attn_bk, L0_attn_Wv, L0_attn_bv, L0_attn_Wo, L0_attn_bo, L0_attn_gamma, L0_attn_beta, L0_ffn_w_freq_real, L0_ffn_w_freq_imag, L0_ffn_bias, L1_attn_w_in, L1_attn_conv_w, L1_attn_conv_b, L1_attn_w_xproj, L1_attn_w_dt, L1_attn_b_dt, L1_attn_A_log, L1_attn_D, L1_attn_w_out, L1_attn_ln_g, L1_attn_ln_b, L1_ffn_gate_w, L1_ffn_gate_b, L1_ffn_w0, L1_ffn_b0, L1_ffn_w1, L1_ffn_b1, L1_ffn_w2, L1_ffn_b2):

    def _L0_attn_ref(x, Wq, bq, Wk, bk, Wv, bv, Wo, bo, gamma, beta):
        import jax, jax.numpy as jnp
        import numpy as np
        B, S, D, H = (1, 1024, 256, 16)
        DH = D // H

        def _positional_encoding(seq_len, d_model, dtype):
            pos = jnp.arange(seq_len, dtype=dtype)[:, None]
            div = jnp.exp(jnp.arange(0, d_model, 2, dtype=dtype) * (-np.log(10000.0) / d_model))
            pe = jnp.zeros((seq_len, d_model), dtype=dtype)
            pe = pe.at[:, 0::2].set(jnp.sin(pos * div))
            pe = pe.at[:, 1::2].set(jnp.cos(pos * div))
            return pe
        b, s, d = x.shape
        h = x + _positional_encoding(s, d, x.dtype)[None, :, :]
        q = (h @ Wq + bq).reshape(b, s, H, DH)
        k = (h @ Wk + bk).reshape(b, s, H, DH)
        v = (h @ Wv + bv).reshape(b, s, H, DH)
        scores = jnp.einsum('bshd,bthd->bhst', q, k) / np.sqrt(DH)
        attn = jax.nn.softmax(scores, axis=-1)
        out = jnp.einsum('bhst,bthd->bshd', attn, v).reshape(b, s, d)
        out = out @ Wo + bo
        y = h + out
        mu = jnp.mean(y, axis=-1, keepdims=True)
        var = jnp.var(y, axis=-1, keepdims=True)
        return (y - mu) * jax.lax.rsqrt(var + 1e-05) * gamma + beta

    def _L0_ffn_ref(x, w_freq_real, w_freq_imag, bias):
        import jax, jax.numpy as jnp
        import numpy as np
        B, N, D = (4, 512, 256)
        SPARSITY = 0.01
        w = jax.lax.complex(w_freq_real, w_freq_imag)
        x_freq = jnp.fft.fft(x, axis=-1)
        y_freq = jnp.einsum('bnd,do->bno', x_freq, w)
        y = jnp.real(jnp.fft.ifft(y_freq, axis=-1))
        return y + bias

    def _L1_attn_ref(x, w_in, conv_w, conv_b, w_xproj, w_dt, b_dt, A_log, D, w_out, ln_g, ln_b):
        import jax, jax.numpy as jnp
        import numpy as np
        LN_EPS = 1e-05

        def _silu(x):
            return x * jax.nn.sigmoid(x)
        B, L, d_model = x.shape
        d_inner = conv_w.shape[0]
        d_state = A_log.shape[1]
        d_conv = conv_w.shape[2]
        residual = x
        mu = x.mean(-1, keepdims=True)
        var = ((x - mu) ** 2).mean(-1, keepdims=True)
        xn = (x - mu) * jax.lax.rsqrt(var + LN_EPS) * ln_g + ln_b
        xz = xn @ w_in
        x_b, z = jnp.split(xz, 2, axis=-1)
        xc = jnp.transpose(x_b, (0, 2, 1))
        xc = jax.lax.conv_general_dilated(xc, conv_w, window_strides=(1,), padding=[(d_conv - 1, 0)], dimension_numbers=('NCH', 'OIH', 'NCH'), feature_group_count=d_inner)
        xc = xc + conv_b[None, :, None]
        x_b = _silu(jnp.transpose(xc, (0, 2, 1)))
        A = -jnp.exp(A_log)
        x_dbl = x_b @ w_xproj
        B_mat, C_mat = jnp.split(x_dbl, 2, axis=-1)
        dt = jax.nn.softplus(x_b @ w_dt + b_dt)

        def step(h, ins):
            dt_t, B_t, C_t, x_t = ins
            A_bar = jnp.exp(dt_t[:, :, None] * A[None])
            B_bar = dt_t[:, :, None] * B_t[:, None, :]
            h = A_bar * h + B_bar * x_t[:, :, None]
            y_t = jnp.einsum('bdn,bn->bd', h, C_t)
            return (h, y_t)
        tm = lambda a: jnp.transpose(a, (1, 0, 2))
        h0 = jnp.zeros((B, d_inner, d_state), x.dtype)
        _, y = jax.lax.scan(step, h0, (tm(dt), tm(B_mat), tm(C_mat), tm(x_b)))
        y = jnp.transpose(y, (1, 0, 2)) + D * x_b
        y = y * _silu(z)
        return y @ w_out + residual

    def _L1_ffn_ref(x, gate_w, gate_b, w0, b0, w1, b1, w2, b2):
        import jax, jax.numpy as jnp
        import numpy as np
        E, TOP_K, D, H = (8, 2, 256, 512)
        B, S = (2, 512)
        Bn, Sq, Dv = x.shape
        xt = x.reshape(-1, Dv)
        logits = xt @ gate_w.T + gate_b
        top_v, top_i = jax.lax.top_k(logits, TOP_K)
        h0 = jnp.einsum('td,ehd->eth', xt, w0) + b0[:, None, :]
        h1 = jnp.einsum('td,ehd->eth', xt, w1) + b1[:, None, :]
        act = h0 * jax.nn.silu(h1)
        out_all = jnp.einsum('eth,edh->etd', act, w2) + b2[:, None, :]
        out_te = jnp.transpose(out_all, (1, 0, 2))
        sel = jnp.take_along_axis(out_te, top_i[:, :, None], axis=1)
        w = jax.nn.softmax(top_v, axis=-1)[:, :, None]
        out = (w * sel).sum(axis=1)
        return out.reshape(Bn, Sq, Dv)
    x = L0_attn_x
    x = x + 0.5 * _L0_ffn_ref(_layernorm(x, axis=-1), L0_ffn_w_freq_real, L0_ffn_w_freq_imag, L0_ffn_bias)
    x = x + _L0_attn_ref(_layernorm(x, axis=-1), L0_attn_Wq, L0_attn_bq, L0_attn_Wk, L0_attn_bk, L0_attn_Wv, L0_attn_bv, L0_attn_Wo, L0_attn_bo, L0_attn_gamma, L0_attn_beta)
    x = x + 0.5 * _L0_ffn_ref(_layernorm(x, axis=-1), L0_ffn_w_freq_real, L0_ffn_w_freq_imag, L0_ffn_bias)
    x = x + 0.5 * _L1_ffn_ref(_layernorm(x, axis=-1), L1_ffn_gate_w, L1_ffn_gate_b, L1_ffn_w0, L1_ffn_b0, L1_ffn_w1, L1_ffn_b1, L1_ffn_w2, L1_ffn_b2)
    x = x + _L1_attn_ref(_layernorm(x, axis=-1), L1_attn_w_in, L1_attn_conv_w, L1_attn_conv_b, L1_attn_w_xproj, L1_attn_w_dt, L1_attn_b_dt, L1_attn_A_log, L1_attn_D, L1_attn_w_out, L1_attn_ln_g, L1_attn_ln_b)
    x = x + 0.5 * _L1_ffn_ref(_layernorm(x, axis=-1), L1_ffn_gate_w, L1_ffn_gate_b, L1_ffn_w0, L1_ffn_b0, L1_ffn_w1, L1_ffn_b1, L1_ffn_w2, L1_ffn_b2)
    return x

_drawn_inputs = setup_inputs


def setup_inputs(seed=0):
    import zlib

    import numpy as np

    out = dict(_drawn_inputs(seed))
    spreads = {'L0_attn_bq': (0.0, 0.8),
     'L0_attn_bk': (0.0, 0.8),
     'L0_attn_bv': (0.0, 0.1),
     'L0_attn_bo': (0.0, 0.1),
     'L0_attn_gamma': (1.0, 0.2),
     'L0_attn_beta': (0.0, 0.1),
     'L1_attn_D': (1.0, 0.6),
     'L1_attn_ln_g': (1.0, 0.2),
     'L1_attn_ln_b': (0.0, 0.1),
     'L1_ffn_gate_b': (0.0, 0.687),
     'L1_ffn_b0': (0.0, 0.8),
     'L1_ffn_b1': (0.0, 0.8),
     'L1_ffn_b2': (0.0, 0.289)}
    factors = {'L0_ffn_bias': 7.6,
     'L1_attn_conv_b': 8.0,
     'L1_attn_b_dt': 8.0,
     'L1_ffn_w0': 8.0,
     'L1_ffn_w1': 8.0,
     'L1_ffn_w2': 7.734}
    for name, (base, spread) in spreads.items():
        noise = np.random.default_rng([zlib.crc32(name.encode()), seed]).standard_normal(out[name].shape)
        drawn = base * np.exp(spread * noise) if base else spread * noise
        out[name] = jnp.asarray(drawn.astype(out[name].dtype))
    for name, factor in factors.items():
        out[name] = (out[name] * factor).astype(out[name].dtype)
    return out
```

```python
from contextlib import ExitStack

import numpy as np

import concourse.bass as bass
from concourse import mybir

F32 = mybir.dt.float32
BF16 = mybir.dt.bfloat16
ALU = mybir.AluOpType
ACT = mybir.ActivationFunctionType
AX = mybir.AxisListType

P = 128
NB, S, D = 8, 512, 256
TT = S // P
DC = D // P
H, DH = 16, 16
HG = 4
NG = H // HG
DI, NS, KC = 512, 16, 4
IC = DI // P
E, HID = 8, 512
HC = HID // P
EPS = 1e-5
NPIECE = 6


def semaphores(nc, ctx, names):
    return {n: ctx.enter_context(nc.semaphore(n)) for n in names}


def end_turn(nc, sems):
    numbers = sorted(s.num for s in sems.values())
    assert numbers == list(range(numbers[0], numbers[-1] + 1))
    nc.all_engine_barrier(sems_to_clear=range(numbers[0], numbers[-1] + 1))


def linker(engine, sem):
    count = [0]

    def link(instruction):
        count[0] += 1
        instruction.then_inc(sem, 1)
        engine.wait_ge(sem, count[0])

    return link


def token_major(dram_rows):
    return dram_rows.rearrange("(q p) d -> p q d", p=P)


def dve_layernorm(nc, dve, link, src, dst, ln, var_ready, rstd_ready, turn):
    for q in range(TT):
        last = nc.vector.bn_stats(ln["stats"][:, q, :], src[:, q, :])
    link(last)
    for q in range(TT):
        last = nc.vector.bn_aggr(ln["mv"][:, q, :], ln["stats"][:, q, :])
    link(last)
    nc.vector.tensor_scalar(ln["vareps"][:, :], ln["mv"][:, :, 1], EPS, None, ALU.add).then_inc(var_ready, 1)
    dve.wait_ge(rstd_ready, turn)
    for q in range(TT):
        last = nc.vector.tensor_scalar(dst[:, q, :], src[:, q, :], ln["mv"][:, q, 0:1],
                                       ln["rstd"][:, q:q + 1], ALU.subtract, ALU.mult)
    return last


def pool_rstd(nc, pool, ln, var_ready, rstd_ready, turn):
    pool.wait_ge(var_ready, turn)
    nc.gpsimd.tensor_tensor(ln["rstd"][:, :], ln["vareps"][:, :], ln["neghalf"][:, :], ALU.pow).then_inc(rstd_ready, 1)


def ln_buffers(sb):
    return {"stats": sb("ln_stats", [P, TT, 6], F32), "mv": sb("ln_mv", [P, TT, 2], F32),
            "vareps": sb("ln_vareps", [P, TT], F32), "rstd": sb("ln_rstd", [P, TT], F32),
            "neghalf": sb("ln_neghalf", [P, TT], F32)}


def pe_transpose_tokens(nc, banks, src, ident, done):
    for c in range(DC):
        for q in range(TT):
            last = nc.tensor.transpose(banks[c][:, q * P:(q + 1) * P], src[:, q, c * P:(c + 1) * P], ident[:, :])
        last.then_inc(done, 1)


def pe_project_tokens(nc, banks, lhs_t, weights, chunks, done):
    for q in range(TT):
        for c in range(chunks):
            last = nc.tensor.matmul(banks[q // 2][:, (q % 2) * D:(q % 2 + 1) * D], lhs_t[:, c, q * P:(q + 1) * P],
                                    weights[:, c, :], start=(c == 0), stop=(c == chunks - 1))
        if q % 2:
            last.then_inc(done, 1)


def mixer_matrix(nc, cos_d, sin_d, ncos_d, wr_d, wi_d, mix_d):
    with ExitStack() as ctx:
        sb = lambda n, s, t: ctx.enter_context(nc.sbuf_tensor(n, s, t))
        pb = lambda n: ctx.enter_context(nc.psum_tensor(n, [P, DC, D], F32))
        cos, sin, ncos, wr, wi = [sb(n, [P, DC, D], F32) for n in ("cos", "sin", "ncos", "wr", "wi")]
        pt, nqt, mix = [sb(n, [P, DC, D], F32) for n in ("pt", "nqt", "mix_build")]
        pt_ps, nqt_ps, mix_ps = pb("pt_ps"), pb("nqt_ps"), pb("mix_ps")
        t = semaphores(nc, ctx, ["mix_loaded", "parts_done", "parts_copied", "mix_done", "mix_copied", "mix_stored"])
        with nc.Block() as block:

            @block.sync
            def _(sp):
                for dst, src in ((cos, cos_d), (sin, sin_d), (ncos, ncos_d), (wr, wr_d), (wi, wi_d)):
                    sp.dma_start(dst[:, :, :], src.rearrange("(c p) n -> p c n", p=P)).then_inc(t["mix_loaded"], 16)
                sp.wait_ge(t["mix_copied"], 1)
                sp.dma_start(mix_d.rearrange("(c p) n -> p c n", p=P), mix[:, :, :]).then_inc(t["mix_stored"], 16)
                sp.wait_ge(t["mix_stored"], 16)

            @block.tensor
            def _(pe):
                pe.wait_ge(t["mix_loaded"], 5 * 16)
                for out, a, b in ((pt_ps, cos, sin), (nqt_ps, sin, ncos)):
                    for m in range(DC):
                        for c in range(DC):
                            nc.tensor.matmul(out[:, m, :], wr[:, c, m * P:(m + 1) * P], a[:, c, :], start=(c == 0), stop=False)
                            last = nc.tensor.matmul(out[:, m, :], wi[:, c, m * P:(m + 1) * P], b[:, c, :], start=False,
                                                    stop=(c == DC - 1))
                    last.then_inc(t["parts_done"], 1)
                pe.wait_ge(t["parts_copied"], 2)
                for m in range(DC):
                    for c in range(DC):
                        nc.tensor.matmul(mix_ps[:, m, :], pt[:, c, m * P:(m + 1) * P], cos[:, c, :], start=(c == 0), stop=False)
                        last = nc.tensor.matmul(mix_ps[:, m, :], nqt[:, c, m * P:(m + 1) * P], sin[:, c, :], start=False,
                                                stop=(c == DC - 1))
                last.then_inc(t["mix_done"], 1)

            @block.vector
            def _(dve):
                for i, (dst, src) in enumerate(((pt, pt_ps), (nqt, nqt_ps))):
                    dve.wait_ge(t["parts_done"], i + 1)
                    nc.vector.tensor_copy(dst[:, :, :], src[:, :, :]).then_inc(t["parts_copied"], 1)
                dve.wait_ge(t["mix_done"], 1)
                nc.vector.tensor_scalar(mix[:, :, :], mix_ps[:, :, :], 0.5 / D, None, ALU.mult).then_inc(t["mix_copied"], 1)

        end_turn(nc, t)


def attention_stage(nc, x_d, x_out_d, w, tag="att"):
    with ExitStack() as ctx:
        sb = lambda n, s, t: ctx.enter_context(nc.sbuf_tensor(f"{tag}_{n}", s, t))
        pb = lambda n, s: ctx.enter_context(nc.psum_tensor(f"{tag}_{n}", s, F32))
        ident = sb("ident", [P, P], F32)
        pos = sb("pos", [P, TT, D], F32)
        mix, wq, wk, wv, wo = [sb(n, [P, DC, D], F32) for n in ("mix", "wq", "wk", "wv", "wo")]
        rows = {n: sb(n, [P, D], F32) for n in ("half_bias", "bv", "bo", "gamma", "beta")}
        bqc, bkc = sb("bqc", [P, DC], F32), sb("bkc", [P, DC], F32)
        ln = ln_buffers(sb)

        x0, xn, x0b, x1, h, hb, x1b, x2, x2b, o_tok = [
            sb(n, [P, TT, D], F32) for n in ("x0", "xn", "x0b", "x1", "h", "hb", "x1b", "x2", "x2b", "o_tok")]
        x_t = sb("x_t", [P, DC, S], F32)
        qk_f = sb("qk_f", [P, 2 * DC, S], F32)
        res = sb("res", [P, 2 * DC, S], F32)
        parts = [sb(f"part{i}", [P, 2 * DC, S], BF16) for i in range(3)]
        q_st, k_st = sb("q_st", [P, H, S], BF16), sb("k_st", [P, H, S], BF16)
        v_aug = sb("v_aug", [P, TT, H, 32], F32)
        probs = sb("probs", [P, 4, 2 * S], F32)
        negmax = sb("negmax", [P, NG, HG, TT], F32)
        nm_hi, nm_lo = sb("nm_hi", [P, NG, P], BF16), sb("nm_lo", [P, NG, P], BF16)
        o_t = sb("o_t", [P, 2, S], F32)
        rden = sb("rden", [P, TT, HG], F32)

        sc = pb("sc", [P, 2, S])
        st = pb("st", [P, 4, S])
        ob = pb("ob", [P, S])
        tb = pb("tb", [P, S])
        sc_banks = [sc[:, i, :] for i in range(2)]
        st_banks = [st[:, i, :] for i in range(4)]

        setup = semaphores(nc, ctx, ["a_loaded", "pool_filled", "dve_filled"])
        loads = [(ident[:, :], w["ident"]), (pos[:, :, :], token_major(w["pos"]))]
        loads += [(dst[:, :, :], w[n].rearrange("(c p) n -> p c n", p=P))
                  for dst, n in ((mix, "mix"), (wq, "Wq"), (wk, "Wk"), (wv, "Wv"), (wo, "Wo"))]
        loads += [(rows[n][:, :], w[src].partition_broadcast(P))
                  for n, src in (("half_bias", "ffn_bias"), ("bv", "bv"), ("bo", "bo"), ("gamma", "gamma"), ("beta", "beta"))]
        loads += [(bqc[:, :], w["bq"]), (bkc[:, :], w["bk"])]
        with nc.Block() as block:

            @block.sync
            def _(sp):
                for dst, src in loads:
                    sp.dma_start(dst, src).then_inc(setup["a_loaded"], 16)
                sp.wait_ge(setup["a_loaded"], 16 * len(loads))

            @block.gpsimd
            def _(pool):
                nc.gpsimd.memset(ln["neghalf"][:, :], -0.5).then_inc(setup["pool_filled"], 1)
                nc.gpsimd.memset(v_aug[:, :, :, 16:32], 0.0).then_inc(setup["pool_filled"], 1)
                pool.wait_ge(setup["pool_filled"], 2)
                nc.gpsimd.memset(v_aug[:, :, :, 16:17], 1.0).then_inc(setup["pool_filled"], 1)
                pool.wait_ge(setup["pool_filled"], 3)

            @block.vector
            def _(dve):
                nc.vector.memset(k_st[96:98, :, :], 1.0).then_inc(setup["dve_filled"], 1)
                dve.wait_ge(setup["a_loaded"], 16 * len(loads))
                nc.vector.tensor_scalar(rows["half_bias"][:, :], rows["half_bias"][:, :], 0.5, None,
                                        ALU.mult).then_inc(setup["dve_filled"], 1)

        end_turn(nc, setup)

        t = semaphores(nc, ctx, ["x_loaded", "x_stored", "dve_step", "act_step", "pool_step", "var_ready", "rstd_ready",
                           "biased", "norm_ready", "tr_done", "xt_ready", "tok_done", "tok_used",
                           "qk_done", "q_in", "k_in", "hi_ready", "mid_ready", "lo_ready", "stacked",
                           "v_done", "v_ready", "sc_done", "sc_used", "negmax_ready", "nmt_done", "nm_ready", *(f"nm_placed{g}" for g in range(NG)),
                           "st_done", "probs_ready", "pv_done", "ot_ready", "otr_done", "o_ready"])
        nm_placed = [t["nm_placed0"], t["nm_placed1"], t["nm_placed2"], t["nm_placed3"]]

        def bc(row):
            return row[:, :].rearrange("p (a d) -> p a d", a=1).broadcast_to([P, TT, D])
        q_piece, k_piece = (0, 0, 1, 1, 0, 2), (0, 1, 0, 1, 2, 0)

        with nc.Fori(0, NB) as b:
            with nc.Block() as block:

                @block.sync
                def _(sp):
                    sp.dma_start(x0[:, :, :], token_major(x_d[bass.ds(b * S, S), :])).then_inc(t["x_loaded"], 16)
                    ready = (t["hi_ready"], t["mid_ready"], t["lo_ready"])
                    for part in range(3):
                        sp.wait_ge(ready[part], 2)
                        for i in range(NPIECE):
                            for which, (piece, stack) in enumerate(((q_piece, q_st), (k_piece, k_st))):
                                if piece[i] == part:
                                    sp.dma_start(stack[DH * i:DH * i + DH, :, :],
                                                 parts[part][:, DC * which:DC * which + DC, :]).then_inc(t["stacked"], 16)
                    for g in range(NG):
                        sp.wait_ge(t["nm_ready"], 2 * (g + 1))
                        for row, src in ((96, nm_hi), (97, nm_lo)):
                            sp.dma_start(q_st[row:row + 1, HG * g:HG * g + HG, :], src[0:HG * TT, g, :]).then_inc(nm_placed[g], 16)
                    sp.wait_ge(t["norm_ready"], 4)
                    sp.dma_start(token_major(x_out_d[bass.ds(b * S, S), :]), x2b[:, :, :]).then_inc(t["x_stored"], 16)
                    sp.wait_ge(t["x_stored"], 16)

                @block.gpsimd
                def _(pool):
                    pool.wait_ge(t["x_loaded"], 16)
                    nc.gpsimd.tensor_tensor(x0b[:, :, :], x0[:, :, :], bc(rows["half_bias"]), ALU.add).then_inc(t["biased"], 1)
                    pool_rstd(nc, pool, ln, t["var_ready"], t["rstd_ready"], 1)
                    pool_rstd(nc, pool, ln, t["var_ready"], t["rstd_ready"], 2)
                    pool.wait_ge(t["norm_ready"], 2)
                    nc.gpsimd.tensor_tensor(hb[:, :, :], h[:, :, :], bc(rows["bo"]), ALU.add).then_inc(t["biased"], 1)
                    nc.gpsimd.tensor_tensor(x1b[:, :, :], x1[:, :, :], bc(rows["beta"]), ALU.add).then_inc(t["biased"], 1)
                    pool_rstd(nc, pool, ln, t["var_ready"], t["rstd_ready"], 3)
                    pool_rstd(nc, pool, ln, t["var_ready"], t["rstd_ready"], 4)
                    nc.gpsimd.tensor_tensor(x2b[:, :, :], x2[:, :, :], bc(rows["half_bias"]), ALU.add).then_inc(t["biased"], 1)

                @block.scalar
                def _(act):
                    def copy_transposed(turn):
                        for c in range(DC):
                            act.wait_ge(t["tr_done"], DC * (turn - 1) + c + 1)
                            nc.scalar.copy(x_t[:, c, :], st_banks[c]).then_inc(t["xt_ready"], 1)

                    copy_transposed(1)
                    copy_transposed(2)
                    for i in range(2 * DC):
                        act.wait_ge(t["qk_done"], i + 1)
                        bias = (bqc if i < DC else bkc)[:, i % DC:i % DC + 1]
                        last = nc.scalar.activation(qk_f[:, i, :], st_banks[(DC + i) % 4], ACT.Identity, bias=bias)
                        last.then_inc(t["q_in"], 1)
                    act.wait_ge(t["q_in"], 4)
                    for i in range(2):
                        nc.scalar.copy(parts[0][:, DC * i:DC * i + DC, :], qk_f[:, DC * i:DC * i + DC, :]).then_inc(t["hi_ready"], 1)
                    for n in range(2 * H):
                        g, hh = n // (2 * HG), n // 2
                        act.wait_ge(t["st_done"], n + 1)
                        if n >= 4:
                            act.wait_ge(t["pv_done"], n - 3)
                        pair = st[:, 2 * (n % 2):2 * (n % 2) + 2, :].rearrange("p a s -> p (a s)")
                        nc.scalar.activation(probs[:, n % 4, :], pair, ACT.Exp, scale=DH ** -0.5).then_inc(t["probs_ready"], 1)
                        if n % (2 * HG) == 0 and g >= 1:
                            act.wait_ge(t["pv_done"], n)
                            if g >= 3:
                                act.wait_ge(t["otr_done"], g - 2)
                            nc.scalar.copy(o_t[:, (g - 1) % 2, :], ob[:, :]).then_inc(t["ot_ready"], 1)
                    act.wait_ge(t["pv_done"], 2 * H)
                    act.wait_ge(t["otr_done"], NG - 2)
                    nc.scalar.copy(o_t[:, (NG - 1) % 2, :], ob[:, :]).then_inc(t["ot_ready"], 1)
                    copy_transposed(3)
                    copy_transposed(4)

                @block.vector
                def _(dve):
                    link = linker(dve, t["dve_step"])
                    dve.wait_ge(t["x_loaded"], 16)
                    dve_layernorm(nc, dve, link, x0, xn, ln, t["var_ready"], t["rstd_ready"], 1).then_inc(t["norm_ready"], 1)
                    dve.wait_ge(t["biased"], 1)
                    for i in range(2):
                        dve.wait_ge(t["tok_done"], i + 1)
                        last = nc.vector.tensor_tensor(x1[:, 2 * i:2 * i + 2, :], sc_banks[i].rearrange("p (a d) -> p a d", a=2),
                                                       x0b[:, 2 * i:2 * i + 2, :], ALU.add)
                    link(last)
                    link(dve_layernorm(nc, dve, link, x1, h, ln, t["var_ready"], t["rstd_ready"], 2))
                    nc.vector.tensor_tensor(h[:, :, :], h[:, :, :], pos[:, :, :], ALU.add).then_inc(t["norm_ready"], 1)
                    for i in range(2):
                        sl = slice(DC * i, DC * i + DC)
                        dve.wait_ge(t["hi_ready"], i + 1)
                        link(nc.vector.tensor_tensor(res[:, sl, :], qk_f[:, sl, :], parts[0][:, sl, :], ALU.subtract))
                        nc.vector.tensor_copy(parts[1][:, sl, :], res[:, sl, :]).then_inc(t["mid_ready"], 1)
                        dve.wait_ge(t["mid_ready"], i + 1)
                        nc.vector.tensor_tensor(parts[2][:, sl, :], res[:, sl, :], parts[1][:, sl, :], ALU.subtract).then_inc(t["lo_ready"], 1)
                    bv3 = rows["bv"][:, :].rearrange("p (h e) -> p h e", h=H)
                    for q in range(TT):
                        dve.wait_ge(t["v_done"], q // 2 + 1)
                        last = nc.vector.tensor_tensor(v_aug[:, q, :, 0:DH],
                                                       sc[:, q // 2, (q % 2) * D:(q % 2 + 1) * D].rearrange("p (h e) -> p h e", h=H),
                                                       bv3, ALU.add)
                    last.then_inc(t["v_ready"], 1)

                    def group_max(g):
                        for i in range(HG * TT):
                            n = HG * TT * g + i
                            dve.wait_ge(t["sc_done"], n + 1)
                            last = nc.vector.tensor_reduce(negmax[:, g, i // TT, i % TT:i % TT + 1], sc_banks[n % 2], axis=AX.X,
                                                           op=ALU.max, negate=True)
                            last.then_inc(t["sc_used"], 1)

                    def place_max(g):
                        dve.wait_ge(t["nmt_done"], g + 1)
                        nc.vector.tensor_copy(nm_hi[0:HG * TT, g, :], tb[0:HG * TT, 0:P]).then_inc(t["nm_ready"], 1)
                        dve.wait_ge(t["nm_ready"], 2 * g + 1)
                        nc.vector.tensor_tensor(nm_lo[0:HG * TT, g, :], tb[0:HG * TT, 0:P], nm_hi[0:HG * TT, g, :],
                                                ALU.subtract).then_inc(t["nm_ready"], 1)

                    def normalise(g):
                        dve.wait_ge(t["otr_done"], g + 1)
                        view = tb[:, :].rearrange("p (q h e) -> p q h e", q=TT, h=HG)
                        link(nc.vector.reciprocal(rden[:, :, :], view[:, :, :, DH]))
                        for q in range(TT):
                            last = nc.vector.tensor_tensor(
                                o_tok[:, q, g * HG * DH:(g + 1) * HG * DH].rearrange("p (h e) -> p h e", h=HG),
                                view[:, q, :, 0:DH],
                                rden[:, q, :].rearrange("p (h e) -> p h e", e=1).broadcast_to([P, HG, DH]), ALU.mult)
                        last.then_inc(t["o_ready"], 1)

                    group_max(0)
                    place_max(0)
                    group_max(1)
                    place_max(1)
                    for g in range(NG):
                        if g + 2 < NG:
                            group_max(g + 2)
                            place_max(g + 2)
                        normalise(g)
                    dve.wait_ge(t["biased"], 3)
                    for i in range(2):
                        dve.wait_ge(t["tok_done"], 2 + i + 1)
                        last = nc.vector.tensor_tensor(h[:, 2 * i:2 * i + 2, :], sc_banks[i].rearrange("p (a d) -> p a d", a=2),
                                                       hb[:, 2 * i:2 * i + 2, :], ALU.add)
                    link(last)
                    link(dve_layernorm(nc, dve, link, h, xn, ln, t["var_ready"], t["rstd_ready"], 3))
                    link(nc.vector.tensor_tensor(xn[:, :, :], xn[:, :, :], bc(rows["gamma"]), ALU.mult))
                    link(nc.vector.tensor_tensor(x2[:, :, :], xn[:, :, :], x1b[:, :, :], ALU.add))
                    dve_layernorm(nc, dve, link, x2, xn, ln, t["var_ready"], t["rstd_ready"], 4).then_inc(t["norm_ready"], 1)
                    dve.wait_ge(t["biased"], 4)
                    for i in range(2):
                        dve.wait_ge(t["tok_done"], 4 + i + 1)
                        last = nc.vector.tensor_tensor(x2b[:, 2 * i:2 * i + 2, :], sc_banks[i].rearrange("p (a d) -> p a d", a=2),
                                                       x2b[:, 2 * i:2 * i + 2, :], ALU.add)
                    last.then_inc(t["norm_ready"], 1)

                @block.tensor
                def _(pe):
                    pe.wait_ge(t["norm_ready"], 1)
                    pe_transpose_tokens(nc, st_banks, xn, ident, t["tr_done"])
                    pe.wait_ge(t["xt_ready"], DC)
                    pe_project_tokens(nc, sc_banks, x_t, mix, DC, t["tok_done"])
                    pe.wait_ge(t["norm_ready"], 2)
                    pe_transpose_tokens(nc, st_banks, h, ident, t["tr_done"])
                    pe.wait_ge(t["xt_ready"], 2 * DC)
                    for i in range(2 * DC):
                        wgt = wq if i < DC else wk
                        for c in range(DC):
                            last = nc.tensor.matmul(st_banks[(DC + i) % 4], wgt[:, c, (i % DC) * P:(i % DC + 1) * P], x_t[:, c, :],
                                                    start=(c == 0), stop=(c == DC - 1))
                        last.then_inc(t["qk_done"], 1)
                    pe_project_tokens(nc, sc_banks, x_t, wv, DC, t["v_done"])

                    def score(n):
                        hh, q = n // TT, n % TT
                        if n >= 2:
                            pe.wait_ge(t["sc_used"], n - 1)
                        nc.tensor.matmul(sc_banks[n % 2], q_st[0:96, hh, q * P:(q + 1) * P], k_st[0:96, hh, :],
                                         start=True, stop=True).then_inc(t["sc_done"], 1)

                    def transpose_max(g):
                        pe.wait_ge(t["sc_used"], HG * TT * (g + 1))
                        if g >= 1:
                            pe.wait_ge(t["nm_ready"], 2 * g)
                        if g >= 3:
                            pe.wait_ge(t["o_ready"], g - 2)
                        nc.tensor.transpose(tb[0:HG * TT, 0:P], negmax[:, g, :, :].rearrange("p h q -> p (h q)"),
                                            ident[:, :]).then_inc(t["nmt_done"], 1)

                    def scores_t(n):
                        if n == 0:
                            pe.wait_ge(t["q_in"], 2 * DC)
                        if n % (2 * HG) == 0:
                            pe.wait_ge(nm_placed[n // (2 * HG)], 32)
                        if n >= 2:
                            pe.wait_ge(t["probs_ready"], n - 1)
                        for j in range(2):
                            kb = 2 * (n % 2) + j
                            last = nc.tensor.matmul(st_banks[2 * (n % 2) + j], k_st[0:98, n // 2, kb * P:(kb + 1) * P],
                                                    q_st[0:98, n // 2, :], start=True, stop=True)
                        last.then_inc(t["st_done"], 1)

                    def weighted_values(n):
                        hh = n // 2
                        hg = hh % HG
                        pe.wait_ge(t["probs_ready"], n + 1)
                        for j in range(2):
                            kb = 2 * (n % 2) + j
                            last = nc.tensor.matmul(ob[32 * hg:32 * hg + 32, :], v_aug[:, kb, hh, :], probs[:, n % 4, j * S:(j + 1) * S],
                                                    start=(kb == 0), stop=(kb == TT - 1))
                        last.then_inc(t["pv_done"], 1)

                    def transpose_out(g):
                        pe.wait_ge(t["ot_ready"], g + 1)
                        pe.wait_ge(t["nm_ready"], 2 * min(g + 3, NG))
                        if g:
                            pe.wait_ge(t["o_ready"], g)
                        for q in range(TT):
                            last = nc.tensor.transpose(tb[:, q * P:(q + 1) * P], o_t[:, g % 2, q * P:(q + 1) * P], ident[:, :])
                        last.then_inc(t["otr_done"], 1)

                    pe.wait_ge(t["v_ready"], 1)
                    pe.wait_ge(t["stacked"], 16 * 2 * NPIECE)
                    for g in range(2):
                        for i in range(HG * TT):
                            score(HG * TT * g + i)
                        transpose_max(g)
                    scores_t(0)
                    for n in range(2 * H):
                        g = n // (2 * HG)
                        if g + 2 < NG:
                            score(HG * TT * (g + 2) + 2 * (n % (2 * HG)))
                        if n + 1 < 2 * H:
                            scores_t(n + 1)
                        if n % (2 * HG) == 0 and g:
                            transpose_out(g - 1)
                        if g + 2 < NG:
                            score(HG * TT * (g + 2) + 2 * (n % (2 * HG)) + 1)
                        weighted_values(n)
                        if n % (2 * HG) == 2 * HG - 1 and g + 2 < NG:
                            transpose_max(g + 2)
                    transpose_out(NG - 1)
                    pe.wait_ge(t["o_ready"], NG)
                    pe_transpose_tokens(nc, st_banks, o_tok, ident, t["tr_done"])
                    pe.wait_ge(t["xt_ready"], 3 * DC)
                    pe_project_tokens(nc, sc_banks, x_t, wo, DC, t["tok_done"])
                    pe.wait_ge(t["norm_ready"], 3)
                    pe_transpose_tokens(nc, st_banks, xn, ident, t["tr_done"])
                    pe.wait_ge(t["xt_ready"], 4 * DC)
                    pe_project_tokens(nc, sc_banks, x_t, mix, DC, t["tok_done"])

            end_turn(nc, t)


def mamba_stage(nc, x_d, x_out_d, w, tag="mamba"):
    with ExitStack() as ctx:
        sb = lambda n, s, t: ctx.enter_context(nc.sbuf_tensor(f"{tag}_{n}", s, t))
        pb = lambda n, s: ctx.enter_context(nc.psum_tensor(f"{tag}_{n}", s, F32))
        ident = sb("ident", [P, P], F32)
        w_in, w_dt = sb("w_in", [P, DC, 2 * DI], F32), sb("w_dt", [P, IC, DI], F32)
        w_out, w_x = sb("w_out", [P, IC, D], F32), sb("w_x", [P, IC, 96], F32)
        ln_g, ln_b = sb("ln_g", [P, D], F32), sb("ln_b", [P, D], F32)
        conv_w, a_neg = sb("conv_w", [P, IC, KC], F32), sb("a_neg", [P, IC, NS], F32)
        cols = {n: sb(n, [P, IC], F32) for n in ("conv_b", "b_dt", "skip")}
        pick = sb("pick", [96, 2 * NS, P], BF16)
        ln = ln_buffers(sb)
        x0, xm, xs, out = [sb(n, [P, TT, D], F32) for n in ("m_x0", "m_xm", "m_xs", "m_out")]
        x_t = sb("m_xt", [P, DC, S], F32)
        xpad = sb("xpad", [P, IC, KC - 1 + S], F32)
        cv, xb, zs, u, ex, dt, dtx, yv = [sb("m_" + n, [P, IC, S], F32) for n in ("cv", "xb", "zs", "u", "ex", "dt", "dtx", "yv")]
        bc_st = sb("bc_st", [96, S], BF16)
        bc_res, bc_mid = sb("bc_res", [96, S], F32), sb("bc_mid", [96, S], BF16)
        b_bc = sb("b_bc", [P, 2, S], F32)
        decay, drive, state, read = [sb(n, [P, 2, IC, S], F32) for n in ("decay", "drive", "state", "read")]

        ya, bb, cb = pb("ya", [P, IC, S]), pb("bb", [P, 2, S]), pb("cb", [P, 2, S])
        banks = {"ya": [ya[:, i, :] for i in range(IC)], "b": [bb[:, i, :] for i in range(2)], "c": [cb[:, i, :] for i in range(2)]}

        setup = semaphores(nc, ctx, ["m_loaded", "pool_filled", "dve_filled", "act_filled"])
        loads = [(ident[:, :], w["ident"]), (pick[:, :, :], w["pick"]),
                 (w_in[:, :, :], w["w_in"].rearrange("(c p) n -> p c n", p=P)),
                 (w_dt[:, :, :], w["w_dt"].rearrange("(c p) n -> p c n", p=P)),
                 (w_out[:, :, :], w["w_out"].rearrange("(c p) n -> p c n", p=P)),
                 (w_x[:, :, :], w["w_xproj3"].rearrange("(c p) n -> p c n", p=P)),
                 (ln_g[:, :], w["ln_g"].partition_broadcast(P)), (ln_b[:, :], w["ln_b"].partition_broadcast(P)),
                 (conv_w[:, :, :], w["conv_w"]), (a_neg[:, :, :], w["A_log"])]
        loads += [(cols[n][:, :], w[n]) for n in cols]
        with nc.Block() as block:

            @block.sync
            def _(sp):
                for dst, src in loads:
                    sp.dma_start(dst, src).then_inc(setup["m_loaded"], 16)
                sp.wait_ge(setup["m_loaded"], 16 * len(loads))

            @block.gpsimd
            def _(pool):
                nc.gpsimd.memset(ln["neghalf"][:, :], -0.5).then_inc(setup["pool_filled"], 1)
                nc.gpsimd.memset(xpad[:, :, 0:KC - 1], 0.0).then_inc(setup["pool_filled"], 1)
                nc.gpsimd.memset(decay[:, :, :, 0:1], 0.0).then_inc(setup["pool_filled"], 1)

            @block.scalar
            def _(act):
                act.wait_ge(setup["m_loaded"], 16 * len(loads))
                nc.scalar.activation(a_neg[:, :, :], a_neg[:, :, :], ACT.Exp).then_inc(setup["act_filled"], 1)

            @block.vector
            def _(dve):
                dve.wait_ge(setup["act_filled"], 1)
                nc.vector.tensor_scalar(a_neg[:, :, :], a_neg[:, :, :], -1.0, None, ALU.mult).then_inc(setup["dve_filled"], 1)

        end_turn(nc, setup)

        t = semaphores(nc, ctx, ["x_loaded", "x_stored", "dve_step", "act_step", "var_ready", "rstd_ready", "norm_ready", "sum_ready",
                           "tr_done", "xt_ready", "in_done", "in_used", "conv_ready", "xb_ready", "xd_done", "bc_ready",
                           "dt_done", "u_ready", "abs_ready", "ln_ready", "dtx_ready", "b_done", "c_done", "b_ready",
                           "decay_ready", "drive_ready", "scan_done", "read_ready", "sum_done", "y_ready", "tok_done", "out_ready"])

        def row(r):
            return r[:, :].rearrange("p (a d) -> p a d", a=1).broadcast_to([P, TT, D])

        def over_blocks(one):
            return one.rearrange("p (a s) -> p a s", a=1).broadcast_to([P, IC, S])

        def flat(x):
            return x.rearrange("p c s -> p (c s)")

        with nc.Fori(0, NB) as b:
            with nc.Block() as block:

                @block.sync
                def _(sp):
                    sp.dma_start(x0[:, :, :], token_major(x_d[bass.ds(b * S, S), :])).then_inc(t["x_loaded"], 16)
                    sp.wait_ge(t["out_ready"], 1)
                    sp.dma_start(token_major(x_out_d[bass.ds(b * S, S), :]), out[:, :, :]).then_inc(t["x_stored"], 16)
                    sp.wait_ge(t["x_stored"], 16)

                @block.gpsimd
                def _(pool):
                    pool_rstd(nc, pool, ln, t["var_ready"], t["rstd_ready"], 1)
                    pool_rstd(nc, pool, ln, t["var_ready"], t["rstd_ready"], 2)
                    pool.wait_ge(t["norm_ready"], 1)
                    nc.gpsimd.tensor_tensor(xs[:, :, :], x0[:, :, :], xm[:, :, :], ALU.add).then_inc(t["sum_ready"], 1)
                    pool.wait_ge(t["dtx_ready"], 1)
                    for n in range(NS):
                        pool.wait_ge(t["b_ready"], n + 1)
                        if n >= 2:
                            pool.wait_ge(t["scan_done"], n - 1)
                        nc.gpsimd.tensor_tensor(drive[:, n % 2, :, :], dtx[:, :, :], over_blocks(b_bc[:, n % 2, :]),
                                                ALU.mult).then_inc(t["drive_ready"], 1)

                @block.scalar
                def _(act):
                    for c in range(DC):
                        act.wait_ge(t["tr_done"], c + 1)
                        nc.scalar.copy(x_t[:, c, :], banks["ya"][c]).then_inc(t["xt_ready"], 1)
                    for i in range(IC):
                        act.wait_ge(t["in_done"], i + 1)
                        nc.scalar.copy(xpad[:, i, KC - 1:], (banks["b"] + banks["c"])[i]).then_inc(t["in_used"], 1)
                    for i in range(IC):
                        act.wait_ge(t["in_done"], IC + i + 1)
                        nc.scalar.activation(zs[:, i, :], banks["ya"][(2 + i) % IC], ACT.Silu).then_inc(t["in_used"], 1)
                    for i in range(IC):
                        act.wait_ge(t["conv_ready"], i + 1)
                        nc.scalar.activation(xb[:, i, :], cv[:, i, :], ACT.Silu, bias=cols["conv_b"][:, i:i + 1]).then_inc(t["xb_ready"], 1)
                    for i in range(IC):
                        act.wait_ge(t["dt_done"], i + 1)
                        nc.scalar.activation(u[:, i, :], banks["ya"][i], ACT.Identity, bias=cols["b_dt"][:, i:i + 1]).then_inc(t["u_ready"], 1)
                    act.wait_ge(t["u_ready"], IC)
                    nc.scalar.activation(ex[:, :, :], u[:, :, :], ACT.Abs).then_inc(t["abs_ready"], 1)
                    act.wait_ge(t["abs_ready"], 1)
                    nc.scalar.activation(ex[:, :, :], ex[:, :, :], ACT.Exp, scale=-1.0).then_inc(t["act_step"], 1)
                    act.wait_ge(t["act_step"], 1)
                    nc.scalar.activation(ex[:, :, :], ex[:, :, :], ACT.Ln, bias=1.0).then_inc(t["ln_ready"], 1)
                    act.wait_ge(t["dtx_ready"], 1)
                    for n in range(NS):
                        act.wait_ge(t["b_done"], n + 1)
                        if n >= 2:
                            act.wait_ge(t["drive_ready"], n - 1)
                        nc.scalar.copy(b_bc[:, n % 2, :], banks["b"][n % 2]).then_inc(t["b_ready"], 1)
                        if n >= 2:
                            act.wait_ge(t["scan_done"], n - 1)
                        for i in range(IC):
                            last = nc.scalar.activation(decay[:, n % 2, i, 1:], dt[:, i, 1:], ACT.Exp, scale=a_neg[:, i, n:n + 1])
                        last.then_inc(t["decay_ready"], 1)

                @block.vector
                def _(dve):
                    link = linker(dve, t["dve_step"])
                    dve.wait_ge(t["x_loaded"], 16)
                    dve_layernorm(nc, dve, link, x0, xm, ln, t["var_ready"], t["rstd_ready"], 1).then_inc(t["norm_ready"], 1)
                    dve.wait_ge(t["norm_ready"], 1)
                    link(dve_layernorm(nc, dve, link, xm, out, ln, t["var_ready"], t["rstd_ready"], 2))
                    link(nc.vector.tensor_tensor(out[:, :, :], out[:, :, :], row(ln_g), ALU.mult))
                    nc.vector.tensor_tensor(out[:, :, :], out[:, :, :], row(ln_b), ALU.add).then_inc(t["norm_ready"], 1)
                    for i in range(IC):
                        dve.wait_ge(t["in_used"], i + 1)
                        link(nc.vector.tensor_scalar(cv[:, i, :], xpad[:, i, 0:S], conv_w[:, i, 0:1], None, ALU.mult))
                        for k in range(1, KC):
                            last = nc.vector.scalar_tensor_tensor(cv[:, i, :], xpad[:, i, k:k + S], conv_w[:, i, k:k + 1], cv[:, i, :],
                                                                  ALU.mult, ALU.add)
                            link(last) if k < KC - 1 else last.then_inc(t["conv_ready"], 1)
                    dve.wait_ge(t["xd_done"], 1)
                    link(nc.vector.tensor_copy(bc_st[:, :], cb[0:96, 0, :]))
                    link(nc.vector.tensor_tensor(bc_res[:, :], cb[0:96, 0, :], bc_st[:, :], ALU.subtract))
                    nc.vector.tensor_copy(bc_mid[:, :], bc_res[:, :])
                    link(nc.vector.tensor_copy(bc_st[32:64, :], bc_res[32:64, :]))
                    nc.vector.tensor_tensor(bc_st[64:96, :], bc_res[64:96, :], bc_mid[64:96, :], ALU.subtract).then_inc(t["bc_ready"], 1)
                    dve.wait_ge(t["u_ready"], IC)
                    link(nc.vector.tensor_scalar(flat(dt[:, :, :]), flat(u[:, :, :]), 0.0, None, ALU.max))
                    dve.wait_ge(t["ln_ready"], 1)
                    link(nc.vector.tensor_tensor(flat(dt[:, :, :]), flat(dt[:, :, :]), flat(ex[:, :, :]), ALU.add))
                    nc.vector.tensor_tensor(flat(dtx[:, :, :]), flat(dt[:, :, :]), flat(xb[:, :, :]), ALU.mult).then_inc(t["dtx_ready"], 1)

                    def scan(n):
                        dve.wait_ge(t["decay_ready"], n + 1)
                        dve.wait_ge(t["drive_ready"], n + 1)
                        nc.vector.tensor_tensor_scan(flat(state[:, n % 2, :, :]), flat(decay[:, n % 2, :, :]),
                                                     flat(drive[:, n % 2, :, :]), 0.0, ALU.mult, ALU.add).then_inc(t["scan_done"], 1)

                    def read_out(n):
                        dve.wait_ge(t["scan_done"], n + 1)
                        dve.wait_ge(t["c_done"], n + 1)
                        if n >= 2:
                            dve.wait_ge(t["sum_done"], n - 1)
                        nc.vector.tensor_tensor(read[:, n % 2, :, :], state[:, n % 2, :, :], over_blocks(banks["c"][n % 2]),
                                                ALU.mult).then_inc(t["read_ready"], 1)

                    scan(0)
                    for n in range(NS):
                        if n + 1 < NS:
                            if n >= 1:
                                dve.wait_ge(t["read_ready"], n)
                            scan(n + 1)
                        read_out(n)
                    dve.wait_ge(t["sum_done"], NS)
                    for i in range(IC):
                        last = nc.vector.scalar_tensor_tensor(yv[:, i, :], xb[:, i, :], cols["skip"][:, i:i + 1], banks["ya"][i],
                                                              ALU.mult, ALU.add)
                    link(last)
                    nc.vector.tensor_tensor(flat(yv[:, :, :]), flat(yv[:, :, :]), flat(zs[:, :, :]), ALU.mult).then_inc(t["y_ready"], 1)
                    dve.wait_ge(t["sum_ready"], 1)
                    for i in range(2):
                        dve.wait_ge(t["tok_done"], i + 1)
                        last = nc.vector.tensor_tensor(out[:, 2 * i:2 * i + 2, :], banks["b"][i].rearrange("p (a d) -> p a d", a=2),
                                                       xs[:, 2 * i:2 * i + 2, :], ALU.add)
                    last.then_inc(t["out_ready"], 1)

                @block.tensor
                def _(pe):
                    pe.wait_ge(t["norm_ready"], 2)
                    pe_transpose_tokens(nc, banks["ya"], out, ident, t["tr_done"])
                    pe.wait_ge(t["xt_ready"], DC)
                    targets = banks["b"] + banks["c"] + banks["ya"][2:] + banks["ya"][:2]
                    for i in range(2 * IC):
                        for c in range(DC):
                            last = nc.tensor.matmul(targets[i], w_in[:, c, i * P:(i + 1) * P], x_t[:, c, :], start=(c == 0), stop=(c == DC - 1))
                        last.then_inc(t["in_done"], 1)
                    pe.wait_ge(t["xb_ready"], IC)
                    for k in range(IC):
                        last = nc.tensor.matmul(cb[0:96, 0, :], w_x[:, k, :], xb[:, k, :], start=(k == 0), stop=(k == IC - 1))
                    last.then_inc(t["xd_done"], 1)
                    pe.wait_ge(t["in_used"], 2 * IC)
                    for i in range(IC):
                        for k in range(IC):
                            last = nc.tensor.matmul(banks["ya"][i], w_dt[:, k, i * P:(i + 1) * P], xb[:, k, :], start=(k == 0), stop=(k == IC - 1))
                        last.then_inc(t["dt_done"], 1)

                    def spread(n):
                        if n >= 2:
                            pe.wait_ge(t["b_ready"], n - 1)
                            pe.wait_ge(t["read_ready"], n - 1)
                        nc.tensor.matmul(banks["b"][n % 2], pick[:, n, :], bc_st[:, :], start=True, stop=True).then_inc(t["b_done"], 1)
                        nc.tensor.matmul(banks["c"][n % 2], pick[:, NS + n, :], bc_st[:, :], start=True, stop=True).then_inc(t["c_done"], 1)

                    pe.wait_ge(t["bc_ready"], 1)
                    spread(0)
                    spread(1)
                    pe.wait_ge(t["u_ready"], IC)
                    for n in range(NS):
                        pe.wait_ge(t["read_ready"], n + 1)
                        if n + 2 < NS:
                            spread(n + 2)
                        for i in range(IC):
                            last = nc.tensor.matmul(banks["ya"][i], ident[:, :], read[:, n % 2, i, :], start=(n == 0), stop=(n == NS - 1))
                        last.then_inc(t["sum_done"], 1)
                    pe.wait_ge(t["y_ready"], 1)
                    pe_project_tokens(nc, banks["b"], yv, w_out, IC, t["tok_done"])

            end_turn(nc, t)


def dense_moe_stage(nc, x_d, x_out_d, w, tag="moe"):
    with ExitStack() as ctx:
        sb = lambda n, s, t: ctx.enter_context(nc.sbuf_tensor(f"{tag}_{n}", s, t))
        pb = lambda n, s: ctx.enter_context(nc.psum_tensor(f"{tag}_{n}", s, F32))
        ident = sb("ident", [P, P], F32)
        w0, w1 = sb("w0", [P, DC, E, HID], F32), sb("w1", [P, DC, E, HID], F32)
        w2 = sb("w2", [P, HC, E, D], F32)
        b0, b1 = sb("b0", [P, E, HC], F32), sb("b1", [P, E, HC], F32)
        b2 = sb("b2", [E, D], F32)
        gate_w, gate_b = sb("gate_w", [P, DC, E], F32), sb("gate_b", [P, E], F32)
        lower = sb("lower", [P, E, E], F32)
        ln = ln_buffers(sb)
        x0, xn, acc = [sb(n, [P, TT, D], F32) for n in ("d_x0", "d_xn", "d_acc")]
        x_t = sb("d_xt", [P, DC, S], F32)
        logit, expl, gates = [sb(n, [P, TT, E], F32) for n in ("logit", "expl", "gates")]
        ahead, tie = sb("ahead", [P, TT, E, E], F32), sb("tie", [P, TT, E, E], F32)
        rank, top, den = sb("rank", [P, TT, E], F32), sb("top", [P, TT], F32), sb("den", [P, TT], F32)
        gates_t = sb("gates_t", [E, S], F32)
        sil, hid = sb("sil", [P, 2, S], F32), sb("hid", [P, 2, HC, S], F32)

        hp = pb("hp", [P, 4, S])
        op = pb("op", [P, 2, S])
        tp = pb("tp", [P, 2, S])
        op_banks, tp_banks = [op[:, i, :] for i in range(2)], [tp[:, i, :] for i in range(2)]

        setup = semaphores(nc, ctx, ["d_loaded", "pool_filled"])
        loads = [(ident[:, :], w["ident"]), (w0[:, :, :, :], w["w0"]), (w1[:, :, :, :], w["w1"]), (w2[:, :, :, :], w["w2"]),
                 (b0[:, :, :], w["b0"]), (b1[:, :, :], w["b1"]), (b2[:, :], w["b2"]), (gate_w[:, :, :], w["gate_w"]),
                 (gate_b[:, :], w["gate_b"].partition_broadcast(P)), (lower[:, :, :], w["lower"].partition_broadcast(P))]
        with nc.Block() as block:

            @block.sync
            def _(sp):
                for dst, src in loads:
                    sp.dma_start(dst, src).then_inc(setup["d_loaded"], 16)
                sp.wait_ge(setup["d_loaded"], 16 * len(loads))

            @block.gpsimd
            def _(pool):
                nc.gpsimd.memset(ln["neghalf"][:, :], -0.5).then_inc(setup["pool_filled"], 1)

        end_turn(nc, setup)

        t = semaphores(nc, ctx, ["x_loaded", "x_stored", "dve_step", "var_ready", "rstd_ready", "norm_ready", "tr_done", "xt_ready",
                           "logit_done", "shift_ready", "exp_ready", "gate_ready", "gt_done", "gt_ready", "b2_done", "acc_ready",
                           "h_done", "sil_ready", "hid_ready", "out_done", "comb_done", "out_ready"])

        with nc.Fori(0, NB) as b:
            with nc.Block() as block:

                @block.sync
                def _(sp):
                    sp.dma_start(x0[:, :, :], token_major(x_d[bass.ds(b * S, S), :])).then_inc(t["x_loaded"], 16)
                    sp.wait_ge(t["comb_done"], E)
                    sp.dma_start(token_major(x_out_d[bass.ds(b * S, S), :]), acc[:, :, :]).then_inc(t["x_stored"], 16)
                    sp.wait_ge(t["x_stored"], 16)

                @block.gpsimd
                def _(pool):
                    pool_rstd(nc, pool, ln, t["var_ready"], t["rstd_ready"], 1)

                @block.scalar
                def _(act):
                    for c in range(DC):
                        act.wait_ge(t["tr_done"], c + 1)
                        nc.scalar.copy(x_t[:, c, :], tp_banks[c]).then_inc(t["xt_ready"], 1)
                    act.wait_ge(t["shift_ready"], 1)
                    nc.scalar.activation(expl[:, :, :], logit[:, :, :], ACT.Exp).then_inc(t["exp_ready"], 1)
                    act.wait_ge(t["gt_done"], 1)
                    nc.scalar.copy(gates_t[:, :], tp[0:E, 1, :]).then_inc(t["gt_ready"], 1)
                    for n in range(E * HC):
                        act.wait_ge(t["h_done"], n + 1)
                        if n >= 2:
                            act.wait_ge(t["hid_ready"], n - 1)
                        nc.scalar.activation(sil[:, n % 2, :], hp[:, 2 * (n % 2) + 1, :], ACT.Silu,
                                             bias=b1[:, n // HC, n % HC:n % HC + 1]).then_inc(t["sil_ready"], 1)

                @block.vector
                def _(dve):
                    link = linker(dve, t["dve_step"])
                    dve.wait_ge(t["x_loaded"], 16)
                    dve_layernorm(nc, dve, link, x0, xn, ln, t["var_ready"], t["rstd_ready"], 1).then_inc(t["norm_ready"], 1)
                    dve.wait_ge(t["logit_done"], 1)
                    link(nc.vector.tensor_tensor(logit[:, :, :], tp[:, 0, 0:TT * E].rearrange("p (q e) -> p q e", q=TT),
                                                 gate_b[:, :].rearrange("p (a e) -> p a e", a=1).broadcast_to([P, TT, E]), ALU.add))
                    for q in range(TT):
                        mine = logit[:, q, :].rearrange("p (e a) -> p e a", a=1).broadcast_to([P, E, E])
                        others = logit[:, q, :].rearrange("p (a e) -> p a e", a=1).broadcast_to([P, E, E])
                        nc.vector.tensor_tensor(ahead[:, q, :, :], others, mine, ALU.is_gt)
                        last = nc.vector.tensor_tensor(tie[:, q, :, :], others, mine, ALU.is_equal)
                    link(nc.vector.tensor_reduce(top[:, :], logit[:, :, :], axis=AX.X, op=ALU.max))
                    for q in range(TT):
                        last = nc.vector.tensor_tensor(tie[:, q, :, :], tie[:, q, :, :], lower[:, :, :], ALU.mult)
                    link(last)
                    nc.vector.tensor_tensor(logit[:, :, :], logit[:, :, :],
                                            top[:, :].rearrange("p (q a) -> p q a", a=1).broadcast_to([P, TT, E]),
                                            ALU.subtract).then_inc(t["shift_ready"], 1)
                    for q in range(TT):
                        last = nc.vector.tensor_tensor(ahead[:, q, :, :], ahead[:, q, :, :], tie[:, q, :, :], ALU.add)
                    link(last)
                    link(nc.vector.tensor_reduce(rank[:, :, :], ahead[:, :, :, :], axis=AX.X, op=ALU.add))
                    link(nc.vector.tensor_scalar(rank[:, :, :], rank[:, :, :], 2.0, None, ALU.is_lt))
                    dve.wait_ge(t["exp_ready"], 1)
                    link(nc.vector.tensor_tensor(expl[:, :, :], expl[:, :, :], rank[:, :, :], ALU.mult))
                    link(nc.vector.tensor_reduce(den[:, :], expl[:, :, :], axis=AX.X, op=ALU.add))
                    link(nc.vector.reciprocal(den[:, :], den[:, :]))
                    link(nc.vector.tensor_scalar(den[:, :], den[:, :], 0.5, None, ALU.mult))
                    nc.vector.tensor_tensor(gates[:, :, :], expl[:, :, :],
                                            den[:, :].rearrange("p (q a) -> p q a", a=1).broadcast_to([P, TT, E]),
                                            ALU.mult).then_inc(t["gate_ready"], 1)
                    for i in range(2):
                        dve.wait_ge(t["b2_done"], i + 1)
                        nc.vector.tensor_tensor(acc[:, 2 * i:2 * i + 2, :], op_banks[i].rearrange("p (a d) -> p a d", a=2),
                                                x0[:, 2 * i:2 * i + 2, :], ALU.add).then_inc(t["acc_ready"], 1)

                    def combine(e):
                        for q in range(TT):
                            dve.wait_ge(t["out_done"], 2 * e + q // 2 + 1)
                            if q == 0:
                                dve.wait_ge(t["acc_ready"], 2)
                                if e:
                                    dve.wait_ge(t["comb_done"], e)
                            last = nc.vector.scalar_tensor_tensor(acc[:, q, :], op[:, q // 2, (q % 2) * D:(q % 2 + 1) * D],
                                                                  gates[:, q, e:e + 1], acc[:, q, :], ALU.mult, ALU.add)
                        last.then_inc(t["comb_done"], 1)

                    for n in range(E * HC):
                        e, hc = n // HC, n % HC
                        if hc == 0 and e >= 2:
                            dve.wait_ge(t["out_done"], 2 * (e - 1))
                        dve.wait_ge(t["sil_ready"], n + 1)
                        nc.vector.scalar_tensor_tensor(hid[:, e % 2, hc, :], hp[:, 2 * (n % 2), :], b0[:, e, hc:hc + 1], sil[:, n % 2, :],
                                                       ALU.add, ALU.mult).then_inc(t["hid_ready"], 1)
                        if hc == 2 and e:
                            combine(e - 1)
                    combine(E - 1)

                @block.tensor
                def _(pe):
                    pe.wait_ge(t["norm_ready"], 1)
                    pe_transpose_tokens(nc, tp_banks, xn, ident, t["tr_done"])
                    pe.wait_ge(t["xt_ready"], DC)
                    for q in range(TT):
                        for c in range(DC):
                            last = nc.tensor.matmul(tp[:, 0, q * E:(q + 1) * E], x_t[:, c, q * P:(q + 1) * P], gate_w[:, c, :],
                                                    start=(c == 0), stop=(c == DC - 1))
                    last.then_inc(t["logit_done"], 1)

                    def hidden(n):
                        e, hc = n // HC, n % HC
                        if n >= 2:
                            pe.wait_ge(t["hid_ready"], n - 1)
                        for j, wgt in enumerate((w0, w1)):
                            for c in range(DC):
                                last = nc.tensor.matmul(hp[:, 2 * (n % 2) + j, :], wgt[:, c, e, hc * P:(hc + 1) * P], x_t[:, c, :],
                                                        start=(c == 0), stop=(c == DC - 1))
                        last.then_inc(t["h_done"], 1)

                    def down(e):
                        pe.wait_ge(t["hid_ready"], HC * (e + 1))
                        if e:
                            pe.wait_ge(t["comb_done"], e)
                        for q in range(TT):
                            for hc in range(HC):
                                last = nc.tensor.matmul(op[:, q // 2, (q % 2) * D:(q % 2 + 1) * D], hid[:, e % 2, hc, q * P:(q + 1) * P],
                                                        w2[:, hc, e, :], start=(hc == 0), stop=(hc == HC - 1))
                            if q % 2:
                                last.then_inc(t["out_done"], 1)

                    hidden(0)
                    hidden(1)
                    pe.wait_ge(t["gate_ready"], 1)
                    for q in range(TT):
                        last = nc.tensor.transpose(tp[0:E, 1, q * P:(q + 1) * P], gates[:, q, :], ident[:, :])
                    last.then_inc(t["gt_done"], 1)
                    pe.wait_ge(t["gt_ready"], 1)
                    for q in range(TT):
                        last = nc.tensor.matmul(op[:, q // 2, (q % 2) * D:(q % 2 + 1) * D], gates_t[:, q * P:(q + 1) * P], b2[:, :],
                                                start=True, stop=True)
                        if q % 2:
                            last.then_inc(t["b2_done"], 1)
                    pe.wait_ge(t["acc_ready"], 2)
                    for n in range(2, E * HC):
                        hidden(n)
                        if n % HC == 0:
                            down(n // HC - 1)
                    down(E - 1)

            end_turn(nc, t)


def lay_out(**a):
    f = lambda n: np.asarray(a[n])
    idx = np.outer(np.arange(D), np.arange(D)) % D
    ang = 2 * np.pi * idx / D
    pos = np.arange(S, dtype=np.float32)[:, None]
    div = np.exp(np.arange(0, D, 2, dtype=np.float32) * np.float32(-np.log(10000.0) / D))
    pe = np.zeros((S, D), np.float32)
    pe[:, 0::2] = np.sin(pos * div)
    pe[:, 1::2] = np.cos(pos * div)
    c, d, j = np.meshgrid(np.arange(DC), np.arange(DH), np.arange(8), indexing="ij")
    perm = ((2 * j + c) * DH + d).reshape(-1)
    pick = np.zeros((96, 2 * NS, P), np.float32)
    for part in range(3):
        pick[32 * part + np.arange(2 * NS), np.arange(2 * NS)] = 1.0
    pick = pick.astype(mybir.dt.np(BF16))
    out = {
        "ident": np.eye(P, dtype=np.float32),
        "pos": pe,
        "cos": np.cos(ang).astype(np.float32), "sin": np.sin(ang).astype(np.float32), "ncos": (-np.cos(ang)).astype(np.float32),
        "w_real": f("L0_ffn_w_freq_real"), "w_imag": f("L0_ffn_w_freq_imag"), "ffn_bias": f("L0_ffn_bias"),
        "Wq": f("L0_attn_Wq")[:, perm], "Wk": f("L0_attn_Wk")[:, perm], "Wv": f("L0_attn_Wv"), "Wo": f("L0_attn_Wo"),
        "bq": f("L0_attn_bq")[perm].reshape(DC, P).T, "bk": f("L0_attn_bk")[perm].reshape(DC, P).T, "bv": f("L0_attn_bv"), "bo": f("L0_attn_bo"),
        "gamma": f("L0_attn_gamma"), "beta": f("L0_attn_beta"),
        "pick": pick,
        "w_in": f("L1_attn_w_in"), "w_dt": f("L1_attn_w_dt"), "w_out": f("L1_attn_w_out"),
        "w_xproj3": np.concatenate([f("L1_attn_w_xproj")] * 3, axis=1),
        "ln_g": f("L1_attn_ln_g"), "ln_b": f("L1_attn_ln_b"),
        "conv_w": f("L1_attn_conv_w").reshape(IC, P, KC).transpose(1, 0, 2),
        "A_log": f("L1_attn_A_log").reshape(IC, P, NS).transpose(1, 0, 2),
        "conv_b": f("L1_attn_conv_b").reshape(IC, P).T, "b_dt": f("L1_attn_b_dt").reshape(IC, P).T,
        "skip": f("L1_attn_D").reshape(IC, P).T,
        "w0": f("L1_ffn_w0").reshape(E, HID, DC, P).transpose(3, 2, 0, 1), "w1": f("L1_ffn_w1").reshape(E, HID, DC, P).transpose(3, 2, 0, 1),
        "w2": f("L1_ffn_w2").reshape(E, D, HC, P).transpose(3, 2, 0, 1),
        "b0": f("L1_ffn_b0").reshape(E, HC, P).transpose(2, 0, 1), "b1": f("L1_ffn_b1").reshape(E, HC, P).transpose(2, 0, 1),
        "b2": f("L1_ffn_b2"), "gate_w": f("L1_ffn_gate_w").reshape(E, DC, P).transpose(2, 1, 0), "gate_b": f("L1_ffn_gate_b"),
        "lower": np.tril(np.ones((E, E), np.float32), -1),
    }
    return {k: np.ascontiguousarray(v) for k, v in out.items()}


def build(nc, w, out_d):
    rows = lambda name: nc.dram_tensor(name, (NB * S, D), F32).ap()
    mix, x3, x4, x5 = nc.dram_tensor("mix_matrix", (D, D), F32).ap(), rows("x3_rows"), rows("x4_rows"), rows("x5_rows")
    mixer_matrix(nc, w["cos"], w["sin"], w["ncos"], w["w_real"], w["w_imag"], mix)
    attention_stage(nc, w["x"], x3, {**w, "mix": mix})
    dense_moe_stage(nc, x3, x4, w, "moe1")
    mamba_stage(nc, x4, x5, w)
    dense_moe_stage(nc, x5, out_d, w, "moe2")


def kernel(**inputs):
    import concourse.bacc as bacc
    from concourse.bass_utils import run_bass_kernel_spmd

    arrays = {"in_" + k: v for k, v in lay_out(**inputs).items()}
    arrays["in_x"] = np.ascontiguousarray(np.asarray(inputs["L0_attn_x"]).reshape(NB * S, D))
    nc = bacc.Bacc("TRN2", target_bir_lowering=False, num_devices=1)
    w = {k[3:]: nc.dram_tensor(k, a.shape, mybir.dt.from_np(a.dtype), kind="ExternalInput").ap() for k, a in arrays.items()}
    out_d = nc.dram_tensor("out_rows", (NB * S, D), F32, kind="ExternalOutput").ap()
    build(nc, w, out_d)
    r = run_bass_kernel_spmd(nc, [arrays], core_ids=[0])
    return r.results[0]["out_rows"].reshape(NB, S, D)
```

```python
from contextlib import ExitStack

import numpy as np

import concourse.bass as bass
from concourse import mybir

F32 = mybir.dt.float32
BF16 = mybir.dt.bfloat16
I32 = mybir.dt.int32
ALU = mybir.AluOpType
ACT = mybir.ActivationFunctionType
AX = mybir.AxisListType

P = 128
NB, S, D = 8, 512, 256
TT = S // P
DC = D // P
H, DH = 16, 16
HG = 4
NG = H // HG
DI, NS, KC = 512, 16, 4
IC = DI // P
E, HID = 8, 512
HC = HID // P
EPS = 1e-5
NT = NB * TT
NTILE = 72
TILES = 12
FIRST_SEMAPHORE = 100
SOFTWARE = 5
NPIECE = 6


def semaphores(nc, ctx, names, after=None):
    first = max(s.num for s in after.values()) + 1 if after else FIRST_SEMAPHORE + 2 * SOFTWARE
    return {n: ctx.enter_context(nc.semaphore(n, num=first + i)) for i, n in enumerate(names)}


def software_semaphores(nc, ctx, use):
    names = ["sent", *(f"row_loaded{i}" for i in range(SOFTWARE - 1))]
    return {n: ctx.enter_context(nc.semaphore(n, num=FIRST_SEMAPHORE + use * SOFTWARE + i)) for i, n in enumerate(names)}


def end_turn(nc, sems):
    numbers = sorted(s.num for s in sems.values())
    assert numbers == list(range(numbers[0], numbers[-1] + 1))
    nc.all_engine_barrier(sems_to_clear=range(numbers[0], numbers[-1] + 1))


def linker(engine, sem):
    count = [0]

    def link(instruction):
        count[0] += 1
        instruction.then_inc(sem, 1)
        engine.wait_ge(sem, count[0])

    return link


def token_major(dram_rows):
    return dram_rows.rearrange("(q p) d -> p q d", p=P)


def dve_layernorm(nc, dve, link, src, dst, ln, var_ready, rstd_ready, turn, tiles=TT):
    for q in range(tiles):
        last = nc.vector.bn_stats(ln["stats"][:, q, :], src[:, q, :])
    link(last)
    for q in range(tiles):
        last = nc.vector.bn_aggr(ln["mv"][:, q, :], ln["stats"][:, q, :])
    link(last)
    nc.vector.tensor_scalar(ln["vareps"][:, :], ln["mv"][:, :, 1], EPS, None, ALU.add).then_inc(var_ready, 1)
    dve.wait_ge(rstd_ready, turn)
    for q in range(tiles):
        last = nc.vector.tensor_scalar(dst[:, q, :], src[:, q, :], ln["mv"][:, q, 0:1],
                                       ln["rstd"][:, q:q + 1], ALU.subtract, ALU.mult)
    return last


def pool_rstd(nc, pool, ln, var_ready, rstd_ready, turn):
    pool.wait_ge(var_ready, turn)
    nc.gpsimd.tensor_tensor(ln["rstd"][:, :], ln["vareps"][:, :], ln["neghalf"][:, :], ALU.pow).then_inc(rstd_ready, 1)


def ln_buffers(sb, tiles=TT):
    return {"stats": sb("ln_stats", [P, tiles, 6], F32), "mv": sb("ln_mv", [P, tiles, 2], F32),
            "vareps": sb("ln_vareps", [P, tiles], F32), "rstd": sb("ln_rstd", [P, tiles], F32),
            "neghalf": sb("ln_neghalf", [P, tiles], F32)}


def pe_transpose_tokens(nc, banks, src, ident, done):
    for c in range(DC):
        for q in range(TT):
            last = nc.tensor.transpose(banks[c][:, q * P:(q + 1) * P], src[:, q, c * P:(c + 1) * P], ident[:, :])
        last.then_inc(done, 1)


def pe_project_tokens(nc, banks, lhs_t, weights, chunks, done):
    for q in range(TT):
        for c in range(chunks):
            last = nc.tensor.matmul(banks[q // 2][:, (q % 2) * D:(q % 2 + 1) * D], lhs_t[:, c, q * P:(q + 1) * P],
                                    weights[:, c, :], start=(c == 0), stop=(c == chunks - 1))
        if q % 2:
            last.then_inc(done, 1)


def mixer_matrix(nc, cos_d, sin_d, ncos_d, wr_d, wi_d, mix_d):
    with ExitStack() as ctx:
        sb = lambda n, s, t: ctx.enter_context(nc.sbuf_tensor(n, s, t))
        pb = lambda n: ctx.enter_context(nc.psum_tensor(n, [P, DC, D], F32))
        cos, sin, ncos, wr, wi = [sb(n, [P, DC, D], F32) for n in ("cos", "sin", "ncos", "wr", "wi")]
        pt, nqt, mix = [sb(n, [P, DC, D], F32) for n in ("pt", "nqt", "mix_build")]
        pt_ps, nqt_ps, mix_ps = pb("pt_ps"), pb("nqt_ps"), pb("mix_ps")
        t = semaphores(nc, ctx, ["mix_loaded", "parts_done", "parts_copied", "mix_done", "mix_copied", "mix_stored"])
        with nc.Block() as block:

            @block.sync
            def _(sp):
                for dst, src in ((cos, cos_d), (sin, sin_d), (ncos, ncos_d), (wr, wr_d), (wi, wi_d)):
                    sp.dma_start(dst[:, :, :], src.rearrange("(c p) n -> p c n", p=P)).then_inc(t["mix_loaded"], 16)
                sp.wait_ge(t["mix_copied"], 1)
                sp.dma_start(mix_d.rearrange("(c p) n -> p c n", p=P), mix[:, :, :]).then_inc(t["mix_stored"], 16)
                sp.wait_ge(t["mix_stored"], 16)

            @block.tensor
            def _(pe):
                pe.wait_ge(t["mix_loaded"], 5 * 16)
                for out, a, b in ((pt_ps, cos, sin), (nqt_ps, sin, ncos)):
                    for m in range(DC):
                        for c in range(DC):
                            nc.tensor.matmul(out[:, m, :], wr[:, c, m * P:(m + 1) * P], a[:, c, :], start=(c == 0), stop=False)
                            last = nc.tensor.matmul(out[:, m, :], wi[:, c, m * P:(m + 1) * P], b[:, c, :], start=False,
                                                    stop=(c == DC - 1))
                    last.then_inc(t["parts_done"], 1)
                pe.wait_ge(t["parts_copied"], 2)
                for m in range(DC):
                    for c in range(DC):
                        nc.tensor.matmul(mix_ps[:, m, :], pt[:, c, m * P:(m + 1) * P], cos[:, c, :], start=(c == 0), stop=False)
                        last = nc.tensor.matmul(mix_ps[:, m, :], nqt[:, c, m * P:(m + 1) * P], sin[:, c, :], start=False,
                                                stop=(c == DC - 1))
                last.then_inc(t["mix_done"], 1)

            @block.vector
            def _(dve):
                for i, (dst, src) in enumerate(((pt, pt_ps), (nqt, nqt_ps))):
                    dve.wait_ge(t["parts_done"], i + 1)
                    nc.vector.tensor_copy(dst[:, :, :], src[:, :, :]).then_inc(t["parts_copied"], 1)
                dve.wait_ge(t["mix_done"], 1)
                nc.vector.tensor_scalar(mix[:, :, :], mix_ps[:, :, :], 0.5 / D, None, ALU.mult).then_inc(t["mix_copied"], 1)

        end_turn(nc, t)


def attention_stage(nc, x_d, x_out_d, w, tag="att"):
    with ExitStack() as ctx:
        sb = lambda n, s, t: ctx.enter_context(nc.sbuf_tensor(f"{tag}_{n}", s, t))
        pb = lambda n, s: ctx.enter_context(nc.psum_tensor(f"{tag}_{n}", s, F32))
        ident = sb("ident", [P, P], F32)
        pos = sb("pos", [P, TT, D], F32)
        mix, wq, wk, wv, wo = [sb(n, [P, DC, D], F32) for n in ("mix", "wq", "wk", "wv", "wo")]
        rows = {n: sb(n, [P, D], F32) for n in ("half_bias", "bv", "bo", "gamma", "beta")}
        bqc, bkc = sb("bqc", [P, DC], F32), sb("bkc", [P, DC], F32)
        ln = ln_buffers(sb)

        x0, xn, x0b, x1, h, hb, x1b, x2, x2b, o_tok = [
            sb(n, [P, TT, D], F32) for n in ("x0", "xn", "x0b", "x1", "h", "hb", "x1b", "x2", "x2b", "o_tok")]
        x_t = sb("x_t", [P, DC, S], F32)
        qk_f = sb("qk_f", [P, 2 * DC, S], F32)
        res = sb("res", [P, 2 * DC, S], F32)
        parts = [sb(f"part{i}", [P, 2 * DC, S], BF16) for i in range(3)]
        q_st, k_st = sb("q_st", [P, H, S], BF16), sb("k_st", [P, H, S], BF16)
        v_aug = sb("v_aug", [P, TT, H, 32], F32)
        probs = sb("probs", [P, 4, 2 * S], F32)
        negmax = sb("negmax", [P, NG, HG, TT], F32)
        nm_hi, nm_lo = sb("nm_hi", [P, NG, P], BF16), sb("nm_lo", [P, NG, P], BF16)
        o_t = sb("o_t", [P, 2, S], F32)
        rden = sb("rden", [P, TT, HG], F32)

        sc = pb("sc", [P, 2, S])
        st = pb("st", [P, 4, S])
        ob = pb("ob", [P, S])
        tb = pb("tb", [P, S])
        sc_banks = [sc[:, i, :] for i in range(2)]
        st_banks = [st[:, i, :] for i in range(4)]

        setup = semaphores(nc, ctx, ["a_loaded", "pool_filled", "dve_filled"])
        loads = [(ident[:, :], w["ident"]), (pos[:, :, :], token_major(w["pos"]))]
        loads += [(dst[:, :, :], w[n].rearrange("(c p) n -> p c n", p=P))
                  for dst, n in ((mix, "mix"), (wq, "Wq"), (wk, "Wk"), (wv, "Wv"), (wo, "Wo"))]
        loads += [(rows[n][:, :], w[src].partition_broadcast(P))
                  for n, src in (("half_bias", "ffn_bias"), ("bv", "bv"), ("bo", "bo"), ("gamma", "gamma"), ("beta", "beta"))]
        loads += [(bqc[:, :], w["bq"]), (bkc[:, :], w["bk"])]
        with nc.Block() as block:

            @block.sync
            def _(sp):
                for dst, src in loads:
                    sp.dma_start(dst, src).then_inc(setup["a_loaded"], 16)
                sp.wait_ge(setup["a_loaded"], 16 * len(loads))

            @block.gpsimd
            def _(pool):
                nc.gpsimd.memset(ln["neghalf"][:, :], -0.5).then_inc(setup["pool_filled"], 1)
                nc.gpsimd.memset(v_aug[:, :, :, 16:32], 0.0).then_inc(setup["pool_filled"], 1)
                pool.wait_ge(setup["pool_filled"], 2)
                nc.gpsimd.memset(v_aug[:, :, :, 16:17], 1.0).then_inc(setup["pool_filled"], 1)
                pool.wait_ge(setup["pool_filled"], 3)

            @block.vector
            def _(dve):
                nc.vector.memset(k_st[96:98, :, :], 1.0).then_inc(setup["dve_filled"], 1)
                dve.wait_ge(setup["a_loaded"], 16 * len(loads))
                nc.vector.tensor_scalar(rows["half_bias"][:, :], rows["half_bias"][:, :], 0.5, None,
                                        ALU.mult).then_inc(setup["dve_filled"], 1)

        end_turn(nc, setup)

        t = semaphores(nc, ctx, ["x_loaded", "x_stored", "dve_step", "act_step", "pool_step", "var_ready", "rstd_ready",
                           "biased", "norm_ready", "tr_done", "xt_ready", "tok_done", "tok_used",
                           "qk_done", "q_in", "k_in", "hi_ready", "mid_ready", "lo_ready", "stacked",
                           "v_done", "v_ready", "sc_done", "sc_used", "negmax_ready", "nmt_done", "nm_ready", *(f"nm_placed{g}" for g in range(NG)),
                           "st_done", "probs_ready", "pv_done", "ot_ready", "otr_done", "o_ready"], after=setup)
        nm_placed = [t["nm_placed0"], t["nm_placed1"], t["nm_placed2"], t["nm_placed3"]]

        def bc(row):
            return row[:, :].rearrange("p (a d) -> p a d", a=1).broadcast_to([P, TT, D])
        q_piece, k_piece = (0, 0, 1, 1, 0, 2), (0, 1, 0, 1, 2, 0)

        with nc.Fori(0, NB) as b:
            with nc.Block() as block:

                @block.sync
                def _(sp):
                    sp.dma_start(x0[:, :, :], token_major(x_d[bass.ds(b * S, S), :])).then_inc(t["x_loaded"], 16)
                    ready = (t["hi_ready"], t["mid_ready"], t["lo_ready"])
                    for part in range(3):
                        sp.wait_ge(ready[part], 2)
                        for i in range(NPIECE):
                            for which, (piece, stack) in enumerate(((q_piece, q_st), (k_piece, k_st))):
                                if piece[i] == part:
                                    sp.dma_start(stack[DH * i:DH * i + DH, :, :],
                                                 parts[part][:, DC * which:DC * which + DC, :]).then_inc(t["stacked"], 16)
                    for g in range(NG):
                        sp.wait_ge(t["nm_ready"], 2 * (g + 1))
                        for row, src in ((96, nm_hi), (97, nm_lo)):
                            sp.dma_start(q_st[row:row + 1, HG * g:HG * g + HG, :], src[0:HG * TT, g, :]).then_inc(nm_placed[g], 16)
                    sp.wait_ge(t["norm_ready"], 4)
                    sp.dma_start(token_major(x_out_d[bass.ds(b * S, S), :]), x2b[:, :, :]).then_inc(t["x_stored"], 16)
                    sp.wait_ge(t["x_stored"], 16)

                @block.gpsimd
                def _(pool):
                    pool.wait_ge(t["x_loaded"], 16)
                    nc.gpsimd.tensor_tensor(x0b[:, :, :], x0[:, :, :], bc(rows["half_bias"]), ALU.add).then_inc(t["biased"], 1)
                    pool_rstd(nc, pool, ln, t["var_ready"], t["rstd_ready"], 1)
                    pool_rstd(nc, pool, ln, t["var_ready"], t["rstd_ready"], 2)
                    pool.wait_ge(t["norm_ready"], 2)
                    nc.gpsimd.tensor_tensor(hb[:, :, :], h[:, :, :], bc(rows["bo"]), ALU.add).then_inc(t["biased"], 1)
                    nc.gpsimd.tensor_tensor(x1b[:, :, :], x1[:, :, :], bc(rows["beta"]), ALU.add).then_inc(t["biased"], 1)
                    pool_rstd(nc, pool, ln, t["var_ready"], t["rstd_ready"], 3)
                    pool_rstd(nc, pool, ln, t["var_ready"], t["rstd_ready"], 4)
                    nc.gpsimd.tensor_tensor(x2b[:, :, :], x2[:, :, :], bc(rows["half_bias"]), ALU.add).then_inc(t["biased"], 1)

                @block.scalar
                def _(act):
                    def copy_transposed(turn):
                        for c in range(DC):
                            act.wait_ge(t["tr_done"], DC * (turn - 1) + c + 1)
                            nc.scalar.copy(x_t[:, c, :], st_banks[c]).then_inc(t["xt_ready"], 1)

                    copy_transposed(1)
                    copy_transposed(2)
                    for i in range(2 * DC):
                        act.wait_ge(t["qk_done"], i + 1)
                        bias = (bqc if i < DC else bkc)[:, i % DC:i % DC + 1]
                        last = nc.scalar.activation(qk_f[:, i, :], st_banks[(DC + i) % 4], ACT.Identity, bias=bias)
                        last.then_inc(t["q_in"], 1)
                    act.wait_ge(t["q_in"], 4)
                    for i in range(2):
                        nc.scalar.copy(parts[0][:, DC * i:DC * i + DC, :], qk_f[:, DC * i:DC * i + DC, :]).then_inc(t["hi_ready"], 1)
                    for n in range(2 * H):
                        g, hh = n // (2 * HG), n // 2
                        act.wait_ge(t["st_done"], n + 1)
                        if n >= 4:
                            act.wait_ge(t["pv_done"], n - 3)
                        pair = st[:, 2 * (n % 2):2 * (n % 2) + 2, :].rearrange("p a s -> p (a s)")
                        nc.scalar.activation(probs[:, n % 4, :], pair, ACT.Exp, scale=DH ** -0.5).then_inc(t["probs_ready"], 1)
                        if n % (2 * HG) == 0 and g >= 1:
                            act.wait_ge(t["pv_done"], n)
                            if g >= 3:
                                act.wait_ge(t["otr_done"], g - 2)
                            nc.scalar.copy(o_t[:, (g - 1) % 2, :], ob[:, :]).then_inc(t["ot_ready"], 1)
                    act.wait_ge(t["pv_done"], 2 * H)
                    act.wait_ge(t["otr_done"], NG - 2)
                    nc.scalar.copy(o_t[:, (NG - 1) % 2, :], ob[:, :]).then_inc(t["ot_ready"], 1)
                    copy_transposed(3)
                    copy_transposed(4)

                @block.vector
                def _(dve):
                    link = linker(dve, t["dve_step"])
                    dve.wait_ge(t["x_loaded"], 16)
                    dve_layernorm(nc, dve, link, x0, xn, ln, t["var_ready"], t["rstd_ready"], 1).then_inc(t["norm_ready"], 1)
                    dve.wait_ge(t["biased"], 1)
                    for i in range(2):
                        dve.wait_ge(t["tok_done"], i + 1)
                        last = nc.vector.tensor_tensor(x1[:, 2 * i:2 * i + 2, :], sc_banks[i].rearrange("p (a d) -> p a d", a=2),
                                                       x0b[:, 2 * i:2 * i + 2, :], ALU.add)
                    link(last)
                    link(dve_layernorm(nc, dve, link, x1, h, ln, t["var_ready"], t["rstd_ready"], 2))
                    nc.vector.tensor_tensor(h[:, :, :], h[:, :, :], pos[:, :, :], ALU.add).then_inc(t["norm_ready"], 1)
                    for i in range(2):
                        sl = slice(DC * i, DC * i + DC)
                        dve.wait_ge(t["hi_ready"], i + 1)
                        link(nc.vector.tensor_tensor(res[:, sl, :], qk_f[:, sl, :], parts[0][:, sl, :], ALU.subtract))
                        nc.vector.tensor_copy(parts[1][:, sl, :], res[:, sl, :]).then_inc(t["mid_ready"], 1)
                        dve.wait_ge(t["mid_ready"], i + 1)
                        nc.vector.tensor_tensor(parts[2][:, sl, :], res[:, sl, :], parts[1][:, sl, :], ALU.subtract).then_inc(t["lo_ready"], 1)
                    bv3 = rows["bv"][:, :].rearrange("p (h e) -> p h e", h=H)
                    for q in range(TT):
                        dve.wait_ge(t["v_done"], q // 2 + 1)
                        last = nc.vector.tensor_tensor(v_aug[:, q, :, 0:DH],
                                                       sc[:, q // 2, (q % 2) * D:(q % 2 + 1) * D].rearrange("p (h e) -> p h e", h=H),
                                                       bv3, ALU.add)
                    last.then_inc(t["v_ready"], 1)

                    def group_max(g):
                        for i in range(HG * TT):
                            n = HG * TT * g + i
                            dve.wait_ge(t["sc_done"], n + 1)
                            last = nc.vector.tensor_reduce(negmax[:, g, i // TT, i % TT:i % TT + 1], sc_banks[n % 2], axis=AX.X,
                                                           op=ALU.max, negate=True)
                            last.then_inc(t["sc_used"], 1)

                    def place_max(g):
                        dve.wait_ge(t["nmt_done"], g + 1)
                        nc.vector.tensor_copy(nm_hi[0:HG * TT, g, :], tb[0:HG * TT, 0:P]).then_inc(t["nm_ready"], 1)
                        dve.wait_ge(t["nm_ready"], 2 * g + 1)
                        nc.vector.tensor_tensor(nm_lo[0:HG * TT, g, :], tb[0:HG * TT, 0:P], nm_hi[0:HG * TT, g, :],
                                                ALU.subtract).then_inc(t["nm_ready"], 1)

                    def normalise(g):
                        dve.wait_ge(t["otr_done"], g + 1)
                        view = tb[:, :].rearrange("p (q h e) -> p q h e", q=TT, h=HG)
                        link(nc.vector.reciprocal(rden[:, :, :], view[:, :, :, DH]))
                        for q in range(TT):
                            last = nc.vector.tensor_tensor(
                                o_tok[:, q, g * HG * DH:(g + 1) * HG * DH].rearrange("p (h e) -> p h e", h=HG),
                                view[:, q, :, 0:DH],
                                rden[:, q, :].rearrange("p (h e) -> p h e", e=1).broadcast_to([P, HG, DH]), ALU.mult)
                        last.then_inc(t["o_ready"], 1)

                    group_max(0)
                    place_max(0)
                    group_max(1)
                    place_max(1)
                    for g in range(NG):
                        if g + 2 < NG:
                            group_max(g + 2)
                            place_max(g + 2)
                        normalise(g)
                    dve.wait_ge(t["biased"], 3)
                    for i in range(2):
                        dve.wait_ge(t["tok_done"], 2 + i + 1)
                        last = nc.vector.tensor_tensor(h[:, 2 * i:2 * i + 2, :], sc_banks[i].rearrange("p (a d) -> p a d", a=2),
                                                       hb[:, 2 * i:2 * i + 2, :], ALU.add)
                    link(last)
                    link(dve_layernorm(nc, dve, link, h, xn, ln, t["var_ready"], t["rstd_ready"], 3))
                    link(nc.vector.tensor_tensor(xn[:, :, :], xn[:, :, :], bc(rows["gamma"]), ALU.mult))
                    link(nc.vector.tensor_tensor(x2[:, :, :], xn[:, :, :], x1b[:, :, :], ALU.add))
                    dve_layernorm(nc, dve, link, x2, xn, ln, t["var_ready"], t["rstd_ready"], 4).then_inc(t["norm_ready"], 1)
                    dve.wait_ge(t["biased"], 4)
                    for i in range(2):
                        dve.wait_ge(t["tok_done"], 4 + i + 1)
                        last = nc.vector.tensor_tensor(x2b[:, 2 * i:2 * i + 2, :], sc_banks[i].rearrange("p (a d) -> p a d", a=2),
                                                       x2b[:, 2 * i:2 * i + 2, :], ALU.add)
                    last.then_inc(t["norm_ready"], 1)

                @block.tensor
                def _(pe):
                    pe.wait_ge(t["norm_ready"], 1)
                    pe_transpose_tokens(nc, st_banks, xn, ident, t["tr_done"])
                    pe.wait_ge(t["xt_ready"], DC)
                    pe_project_tokens(nc, sc_banks, x_t, mix, DC, t["tok_done"])
                    pe.wait_ge(t["norm_ready"], 2)
                    pe_transpose_tokens(nc, st_banks, h, ident, t["tr_done"])
                    pe.wait_ge(t["xt_ready"], 2 * DC)
                    for i in range(2 * DC):
                        wgt = wq if i < DC else wk
                        for c in range(DC):
                            last = nc.tensor.matmul(st_banks[(DC + i) % 4], wgt[:, c, (i % DC) * P:(i % DC + 1) * P], x_t[:, c, :],
                                                    start=(c == 0), stop=(c == DC - 1))
                        last.then_inc(t["qk_done"], 1)
                    pe_project_tokens(nc, sc_banks, x_t, wv, DC, t["v_done"])

                    def score(n):
                        hh, q = n // TT, n % TT
                        if n >= 2:
                            pe.wait_ge(t["sc_used"], n - 1)
                        nc.tensor.matmul(sc_banks[n % 2], q_st[0:96, hh, q * P:(q + 1) * P], k_st[0:96, hh, :],
                                         start=True, stop=True).then_inc(t["sc_done"], 1)

                    def transpose_max(g):
                        pe.wait_ge(t["sc_used"], HG * TT * (g + 1))
                        if g >= 1:
                            pe.wait_ge(t["nm_ready"], 2 * g)
                        if g >= 3:
                            pe.wait_ge(t["o_ready"], g - 2)
                        nc.tensor.transpose(tb[0:HG * TT, 0:P], negmax[:, g, :, :].rearrange("p h q -> p (h q)"),
                                            ident[:, :]).then_inc(t["nmt_done"], 1)

                    def scores_t(n):
                        if n == 0:
                            pe.wait_ge(t["q_in"], 2 * DC)
                        if n % (2 * HG) == 0:
                            pe.wait_ge(nm_placed[n // (2 * HG)], 32)
                        if n >= 2:
                            pe.wait_ge(t["probs_ready"], n - 1)
                        for j in range(2):
                            kb = 2 * (n % 2) + j
                            last = nc.tensor.matmul(st_banks[2 * (n % 2) + j], k_st[0:98, n // 2, kb * P:(kb + 1) * P],
                                                    q_st[0:98, n // 2, :], start=True, stop=True)
                        last.then_inc(t["st_done"], 1)

                    def weighted_values(n):
                        hh = n // 2
                        hg = hh % HG
                        pe.wait_ge(t["probs_ready"], n + 1)
                        for j in range(2):
                            kb = 2 * (n % 2) + j
                            last = nc.tensor.matmul(ob[32 * hg:32 * hg + 32, :], v_aug[:, kb, hh, :], probs[:, n % 4, j * S:(j + 1) * S],
                                                    start=(kb == 0), stop=(kb == TT - 1))
                        last.then_inc(t["pv_done"], 1)

                    def transpose_out(g):
                        pe.wait_ge(t["ot_ready"], g + 1)
                        pe.wait_ge(t["nm_ready"], 2 * min(g + 3, NG))
                        if g:
                            pe.wait_ge(t["o_ready"], g)
                        for q in range(TT):
                            last = nc.tensor.transpose(tb[:, q * P:(q + 1) * P], o_t[:, g % 2, q * P:(q + 1) * P], ident[:, :])
                        last.then_inc(t["otr_done"], 1)

                    pe.wait_ge(t["v_ready"], 1)
                    pe.wait_ge(t["stacked"], 16 * 2 * NPIECE)
                    for g in range(2):
                        for i in range(HG * TT):
                            score(HG * TT * g + i)
                        transpose_max(g)
                    scores_t(0)
                    for n in range(2 * H):
                        g = n // (2 * HG)
                        if g + 2 < NG:
                            score(HG * TT * (g + 2) + 2 * (n % (2 * HG)))
                        if n + 1 < 2 * H:
                            scores_t(n + 1)
                        if n % (2 * HG) == 0 and g:
                            transpose_out(g - 1)
                        if g + 2 < NG:
                            score(HG * TT * (g + 2) + 2 * (n % (2 * HG)) + 1)
                        weighted_values(n)
                        if n % (2 * HG) == 2 * HG - 1 and g + 2 < NG:
                            transpose_max(g + 2)
                    transpose_out(NG - 1)
                    pe.wait_ge(t["o_ready"], NG)
                    pe_transpose_tokens(nc, st_banks, o_tok, ident, t["tr_done"])
                    pe.wait_ge(t["xt_ready"], 3 * DC)
                    pe_project_tokens(nc, sc_banks, x_t, wo, DC, t["tok_done"])
                    pe.wait_ge(t["norm_ready"], 3)
                    pe_transpose_tokens(nc, st_banks, xn, ident, t["tr_done"])
                    pe.wait_ge(t["xt_ready"], 4 * DC)
                    pe_project_tokens(nc, sc_banks, x_t, mix, DC, t["tok_done"])

            end_turn(nc, t)


def mamba_stage(nc, x_d, x_out_d, w, tag="mamba"):
    with ExitStack() as ctx:
        sb = lambda n, s, t: ctx.enter_context(nc.sbuf_tensor(f"{tag}_{n}", s, t))
        pb = lambda n, s: ctx.enter_context(nc.psum_tensor(f"{tag}_{n}", s, F32))
        ident = sb("ident", [P, P], F32)
        w_in, w_dt = sb("w_in", [P, DC, 2 * DI], F32), sb("w_dt", [P, IC, DI], F32)
        w_out, w_x = sb("w_out", [P, IC, D], F32), sb("w_x", [P, IC, 96], F32)
        ln_g, ln_b = sb("ln_g", [P, D], F32), sb("ln_b", [P, D], F32)
        conv_w, a_neg = sb("conv_w", [P, IC, KC], F32), sb("a_neg", [P, IC, NS], F32)
        cols = {n: sb(n, [P, IC], F32) for n in ("conv_b", "b_dt", "skip")}
        pick = sb("pick", [96, 2 * NS, P], BF16)
        ln = ln_buffers(sb)
        x0, xm, xs, out = [sb(n, [P, TT, D], F32) for n in ("m_x0", "m_xm", "m_xs", "m_out")]
        x_t = sb("m_xt", [P, DC, S], F32)
        xpad = sb("xpad", [P, IC, KC - 1 + S], F32)
        cv, xb, zs, u, ex, dt, dtx, yv = [sb("m_" + n, [P, IC, S], F32) for n in ("cv", "xb", "zs", "u", "ex", "dt", "dtx", "yv")]
        bc_st = sb("bc_st", [96, S], BF16)
        bc_res, bc_mid = sb("bc_res", [96, S], F32), sb("bc_mid", [96, S], BF16)
        b_bc = sb("b_bc", [P, 2, S], F32)
        decay, drive, state, read = [sb(n, [P, 2, IC, S], F32) for n in ("decay", "drive", "state", "read")]

        ya, bb, cb = pb("ya", [P, IC, S]), pb("bb", [P, 2, S]), pb("cb", [P, 2, S])
        banks = {"ya": [ya[:, i, :] for i in range(IC)], "b": [bb[:, i, :] for i in range(2)], "c": [cb[:, i, :] for i in range(2)]}

        setup = semaphores(nc, ctx, ["m_loaded", "pool_filled", "dve_filled", "act_filled"])
        loads = [(ident[:, :], w["ident"]), (pick[:, :, :], w["pick"]),
                 (w_in[:, :, :], w["w_in"].rearrange("(c p) n -> p c n", p=P)),
                 (w_dt[:, :, :], w["w_dt"].rearrange("(c p) n -> p c n", p=P)),
                 (w_out[:, :, :], w["w_out"].rearrange("(c p) n -> p c n", p=P)),
                 (w_x[:, :, :], w["w_xproj3"].rearrange("(c p) n -> p c n", p=P)),
                 (ln_g[:, :], w["ln_g"].partition_broadcast(P)), (ln_b[:, :], w["ln_b"].partition_broadcast(P)),
                 (conv_w[:, :, :], w["conv_w"]), (a_neg[:, :, :], w["A_log"])]
        loads += [(cols[n][:, :], w[n]) for n in cols]
        with nc.Block() as block:

            @block.sync
            def _(sp):
                for dst, src in loads:
                    sp.dma_start(dst, src).then_inc(setup["m_loaded"], 16)
                sp.wait_ge(setup["m_loaded"], 16 * len(loads))

            @block.gpsimd
            def _(pool):
                nc.gpsimd.memset(ln["neghalf"][:, :], -0.5).then_inc(setup["pool_filled"], 1)
                nc.gpsimd.memset(xpad[:, :, 0:KC - 1], 0.0).then_inc(setup["pool_filled"], 1)
                nc.gpsimd.memset(decay[:, :, :, 0:1], 0.0).then_inc(setup["pool_filled"], 1)

            @block.scalar
            def _(act):
                act.wait_ge(setup["m_loaded"], 16 * len(loads))
                nc.scalar.activation(a_neg[:, :, :], a_neg[:, :, :], ACT.Exp).then_inc(setup["act_filled"], 1)

            @block.vector
            def _(dve):
                dve.wait_ge(setup["act_filled"], 1)
                nc.vector.tensor_scalar(a_neg[:, :, :], a_neg[:, :, :], -1.0, None, ALU.mult).then_inc(setup["dve_filled"], 1)

        end_turn(nc, setup)

        t = semaphores(nc, ctx, ["x_loaded", "x_stored", "dve_step", "act_step", "var_ready", "rstd_ready", "norm_ready", "sum_ready",
                           "tr_done", "xt_ready", "in_done", "in_used", "conv_ready", "xb_ready", "xd_done", "bc_ready",
                           "dt_done", "u_ready", "abs_ready", "ln_ready", "dtx_ready", "b_done", "c_done", "b_ready",
                           "decay_ready", "drive_ready", "scan_done", "read_ready", "sum_done", "y_ready", "tok_done", "out_ready"], after=setup)

        def row(r):
            return r[:, :].rearrange("p (a d) -> p a d", a=1).broadcast_to([P, TT, D])

        def over_blocks(one):
            return one.rearrange("p (a s) -> p a s", a=1).broadcast_to([P, IC, S])

        def flat(x):
            return x.rearrange("p c s -> p (c s)")

        with nc.Fori(0, NB) as b:
            with nc.Block() as block:

                @block.sync
                def _(sp):
                    sp.dma_start(x0[:, :, :], token_major(x_d[bass.ds(b * S, S), :])).then_inc(t["x_loaded"], 16)
                    sp.wait_ge(t["out_ready"], 1)
                    sp.dma_start(token_major(x_out_d[bass.ds(b * S, S), :]), out[:, :, :]).then_inc(t["x_stored"], 16)
                    sp.wait_ge(t["x_stored"], 16)

                @block.gpsimd
                def _(pool):
                    pool_rstd(nc, pool, ln, t["var_ready"], t["rstd_ready"], 1)
                    pool_rstd(nc, pool, ln, t["var_ready"], t["rstd_ready"], 2)
                    pool.wait_ge(t["norm_ready"], 1)
                    nc.gpsimd.tensor_tensor(xs[:, :, :], x0[:, :, :], xm[:, :, :], ALU.add).then_inc(t["sum_ready"], 1)
                    pool.wait_ge(t["dtx_ready"], 1)
                    for n in range(NS):
                        pool.wait_ge(t["b_ready"], n + 1)
                        if n >= 2:
                            pool.wait_ge(t["scan_done"], n - 1)
                        nc.gpsimd.tensor_tensor(drive[:, n % 2, :, :], dtx[:, :, :], over_blocks(b_bc[:, n % 2, :]),
                                                ALU.mult).then_inc(t["drive_ready"], 1)

                @block.scalar
                def _(act):
                    for c in range(DC):
                        act.wait_ge(t["tr_done"], c + 1)
                        nc.scalar.copy(x_t[:, c, :], banks["ya"][c]).then_inc(t["xt_ready"], 1)
                    for i in range(IC):
                        act.wait_ge(t["in_done"], i + 1)
                        nc.scalar.copy(xpad[:, i, KC - 1:], (banks["b"] + banks["c"])[i]).then_inc(t["in_used"], 1)
                    for i in range(IC):
                        act.wait_ge(t["in_done"], IC + i + 1)
                        nc.scalar.activation(zs[:, i, :], banks["ya"][(2 + i) % IC], ACT.Silu).then_inc(t["in_used"], 1)
                    for i in range(IC):
                        act.wait_ge(t["conv_ready"], i + 1)
                        nc.scalar.activation(xb[:, i, :], cv[:, i, :], ACT.Silu, bias=cols["conv_b"][:, i:i + 1]).then_inc(t["xb_ready"], 1)
                    for i in range(IC):
                        act.wait_ge(t["dt_done"], i + 1)
                        nc.scalar.activation(u[:, i, :], banks["ya"][i], ACT.Identity, bias=cols["b_dt"][:, i:i + 1]).then_inc(t["u_ready"], 1)
                    act.wait_ge(t["u_ready"], IC)
                    nc.scalar.activation(ex[:, :, :], u[:, :, :], ACT.Abs).then_inc(t["abs_ready"], 1)
                    act.wait_ge(t["abs_ready"], 1)
                    nc.scalar.activation(ex[:, :, :], ex[:, :, :], ACT.Exp, scale=-1.0).then_inc(t["act_step"], 1)
                    act.wait_ge(t["act_step"], 1)
                    nc.scalar.activation(ex[:, :, :], ex[:, :, :], ACT.Ln, bias=1.0).then_inc(t["ln_ready"], 1)
                    act.wait_ge(t["dtx_ready"], 1)
                    for n in range(NS):
                        act.wait_ge(t["b_done"], n + 1)
                        if n >= 2:
                            act.wait_ge(t["drive_ready"], n - 1)
                        nc.scalar.copy(b_bc[:, n % 2, :], banks["b"][n % 2]).then_inc(t["b_ready"], 1)
                        if n >= 2:
                            act.wait_ge(t["scan_done"], n - 1)
                        for i in range(IC):
                            last = nc.scalar.activation(decay[:, n % 2, i, 1:], dt[:, i, 1:], ACT.Exp, scale=a_neg[:, i, n:n + 1])
                        last.then_inc(t["decay_ready"], 1)

                @block.vector
                def _(dve):
                    link = linker(dve, t["dve_step"])
                    dve.wait_ge(t["x_loaded"], 16)
                    dve_layernorm(nc, dve, link, x0, xm, ln, t["var_ready"], t["rstd_ready"], 1).then_inc(t["norm_ready"], 1)
                    dve.wait_ge(t["norm_ready"], 1)
                    link(dve_layernorm(nc, dve, link, xm, out, ln, t["var_ready"], t["rstd_ready"], 2))
                    link(nc.vector.tensor_tensor(out[:, :, :], out[:, :, :], row(ln_g), ALU.mult))
                    nc.vector.tensor_tensor(out[:, :, :], out[:, :, :], row(ln_b), ALU.add).then_inc(t["norm_ready"], 1)
                    for i in range(IC):
                        dve.wait_ge(t["in_used"], i + 1)
                        link(nc.vector.tensor_scalar(cv[:, i, :], xpad[:, i, 0:S], conv_w[:, i, 0:1], None, ALU.mult))
                        for k in range(1, KC):
                            last = nc.vector.scalar_tensor_tensor(cv[:, i, :], xpad[:, i, k:k + S], conv_w[:, i, k:k + 1], cv[:, i, :],
                                                                  ALU.mult, ALU.add)
                            link(last) if k < KC - 1 else last.then_inc(t["conv_ready"], 1)
                    dve.wait_ge(t["xd_done"], 1)
                    link(nc.vector.tensor_copy(bc_st[:, :], cb[0:96, 0, :]))
                    link(nc.vector.tensor_tensor(bc_res[:, :], cb[0:96, 0, :], bc_st[:, :], ALU.subtract))
                    nc.vector.tensor_copy(bc_mid[:, :], bc_res[:, :])
                    link(nc.vector.tensor_copy(bc_st[32:64, :], bc_res[32:64, :]))
                    nc.vector.tensor_tensor(bc_st[64:96, :], bc_res[64:96, :], bc_mid[64:96, :], ALU.subtract).then_inc(t["bc_ready"], 1)
                    dve.wait_ge(t["u_ready"], IC)
                    link(nc.vector.tensor_scalar(flat(dt[:, :, :]), flat(u[:, :, :]), 0.0, None, ALU.max))
                    dve.wait_ge(t["ln_ready"], 1)
                    link(nc.vector.tensor_tensor(flat(dt[:, :, :]), flat(dt[:, :, :]), flat(ex[:, :, :]), ALU.add))
                    nc.vector.tensor_tensor(flat(dtx[:, :, :]), flat(dt[:, :, :]), flat(xb[:, :, :]), ALU.mult).then_inc(t["dtx_ready"], 1)

                    def scan(n):
                        dve.wait_ge(t["decay_ready"], n + 1)
                        dve.wait_ge(t["drive_ready"], n + 1)
                        nc.vector.tensor_tensor_scan(flat(state[:, n % 2, :, :]), flat(decay[:, n % 2, :, :]),
                                                     flat(drive[:, n % 2, :, :]), 0.0, ALU.mult, ALU.add).then_inc(t["scan_done"], 1)

                    def read_out(n):
                        dve.wait_ge(t["scan_done"], n + 1)
                        dve.wait_ge(t["c_done"], n + 1)
                        if n >= 2:
                            dve.wait_ge(t["sum_done"], n - 1)
                        nc.vector.tensor_tensor(read[:, n % 2, :, :], state[:, n % 2, :, :], over_blocks(banks["c"][n % 2]),
                                                ALU.mult).then_inc(t["read_ready"], 1)

                    scan(0)
                    for n in range(NS):
                        if n + 1 < NS:
                            if n >= 1:
                                dve.wait_ge(t["read_ready"], n)
                            scan(n + 1)
                        read_out(n)
                    dve.wait_ge(t["sum_done"], NS)
                    for i in range(IC):
                        last = nc.vector.scalar_tensor_tensor(yv[:, i, :], xb[:, i, :], cols["skip"][:, i:i + 1], banks["ya"][i],
                                                              ALU.mult, ALU.add)
                    link(last)
                    nc.vector.tensor_tensor(flat(yv[:, :, :]), flat(yv[:, :, :]), flat(zs[:, :, :]), ALU.mult).then_inc(t["y_ready"], 1)
                    dve.wait_ge(t["sum_ready"], 1)
                    for i in range(2):
                        dve.wait_ge(t["tok_done"], i + 1)
                        last = nc.vector.tensor_tensor(out[:, 2 * i:2 * i + 2, :], banks["b"][i].rearrange("p (a d) -> p a d", a=2),
                                                       xs[:, 2 * i:2 * i + 2, :], ALU.add)
                    last.then_inc(t["out_ready"], 1)

                @block.tensor
                def _(pe):
                    pe.wait_ge(t["norm_ready"], 2)
                    pe_transpose_tokens(nc, banks["ya"], out, ident, t["tr_done"])
                    pe.wait_ge(t["xt_ready"], DC)
                    targets = banks["b"] + banks["c"] + banks["ya"][2:] + banks["ya"][:2]
                    for i in range(2 * IC):
                        for c in range(DC):
                            last = nc.tensor.matmul(targets[i], w_in[:, c, i * P:(i + 1) * P], x_t[:, c, :], start=(c == 0), stop=(c == DC - 1))
                        last.then_inc(t["in_done"], 1)
                    pe.wait_ge(t["xb_ready"], IC)
                    for k in range(IC):
                        last = nc.tensor.matmul(cb[0:96, 0, :], w_x[:, k, :], xb[:, k, :], start=(k == 0), stop=(k == IC - 1))
                    last.then_inc(t["xd_done"], 1)
                    pe.wait_ge(t["in_used"], 2 * IC)
                    for i in range(IC):
                        for k in range(IC):
                            last = nc.tensor.matmul(banks["ya"][i], w_dt[:, k, i * P:(i + 1) * P], xb[:, k, :], start=(k == 0), stop=(k == IC - 1))
                        last.then_inc(t["dt_done"], 1)

                    def spread(n):
                        if n >= 2:
                            pe.wait_ge(t["b_ready"], n - 1)
                            pe.wait_ge(t["read_ready"], n - 1)
                        nc.tensor.matmul(banks["b"][n % 2], pick[:, n, :], bc_st[:, :], start=True, stop=True).then_inc(t["b_done"], 1)
                        nc.tensor.matmul(banks["c"][n % 2], pick[:, NS + n, :], bc_st[:, :], start=True, stop=True).then_inc(t["c_done"], 1)

                    pe.wait_ge(t["bc_ready"], 1)
                    spread(0)
                    spread(1)
                    pe.wait_ge(t["u_ready"], IC)
                    for n in range(NS):
                        pe.wait_ge(t["read_ready"], n + 1)
                        if n + 2 < NS:
                            spread(n + 2)
                        for i in range(IC):
                            last = nc.tensor.matmul(banks["ya"][i], ident[:, :], read[:, n % 2, i, :], start=(n == 0), stop=(n == NS - 1))
                        last.then_inc(t["sum_done"], 1)
                    pe.wait_ge(t["y_ready"], 1)
                    pe_project_tokens(nc, banks["b"], yv, w_out, IC, t["tok_done"])

            end_turn(nc, t)


def moe_stage(nc, x_d, x_out_d, w, slots_d, expert_out_d, use=0, tag="moe"):
    with ExitStack() as ctx:
        sb = lambda n, s, t: ctx.enter_context(nc.sbuf_tensor(f"{tag}_{n}", s, t))
        ident = sb("ident", [P, P], F32)
        w0, w1, w2 = sb("w0", [P, DC, E * HID], F32), sb("w1", [P, DC, E * HID], F32), sb("w2", [P, HC, E * D], F32)
        b0, b1, b2 = sb("b0", [P, E * HID], F32), sb("b1", [P, E * HID], F32), sb("b2", [P, E * D], F32)
        slot = sb("slot", [P, 2, NT], I32)
        weight = sb("weight", [P, 2, NT], F32)
        expert_of = sb("expert_of", [P, NTILE], I32)
        big = semaphores(nc, ctx, ["weights_loaded", "zeroed"])
        soft = software_semaphores(nc, ctx, use)

        with ExitStack() as part:
            moe_route(nc, part, x_d, w, slots_d, tag, ident, (w0, w1, w2, b0, b1, b2), slot, weight, expert_of, big, soft)
        with ExitStack() as part:
            moe_experts(nc, part, slots_d, expert_out_d, tag, ident, (w0, w1, w2, b0, b1, b2), expert_of, big)
        with ExitStack() as part:
            moe_combine(nc, part, x_d, x_out_d, expert_out_d, tag, slot, weight, big, soft)
        end_turn(nc, big)


def moe_route(nc, ctx, x_d, w, slots_d, tag, ident, weights, slot, weight, expert_of, big, soft):
    sb = lambda n, s, t: ctx.enter_context(nc.sbuf_tensor(f"{tag}_{n}", s, t))
    pb = lambda n, s: ctx.enter_context(nc.psum_tensor(f"{tag}_{n}", s, F32))
    HALF = NT // 2
    gate_w, gate_b = sb("gate_w", [P, DC, E], F32), sb("gate_b", [P, E], F32)
    lower = sb("lower", [P, E, E], F32)
    before = sb("before", [P, P], F32)
    ones = sb("ones", [P, P], F32)
    keep = sb("keep", [P, E, NT], F32)
    step = sb("step", [P, NT], F32)
    number = sb("number", [P, NTILE], F32)
    zeros = sb("zeros", [P, D], F32)
    ln = ln_buffers(sb, HALF)
    xn = sb("xn", [P, NT, D], F32)
    x_t = sb("x_t", [P, 2, DC, S], F32)
    logit, expl, gates, rank = [sb(n, [P, NT, E], F32) for n in ("logit", "expl", "gates", "rank")]
    ahead, tie = sb("ahead", [P, NT, E, E], BF16), sb("tie", [P, NT, E, E], BF16)
    is_first, is_second, chosen = [sb(n, [P, NT, E], F32) for n in ("is_first", "is_second", "chosen")]
    top, den = sb("top", [P, NT], F32), sb("den", [P, NT], F32)
    per_tile, running, base = [sb(n, [P, E, NT], F32) for n in ("per_tile", "running", "base")]
    n_tiles, tiles_to, first_tile = [sb(n, [P, E], F32) for n in ("n_tiles", "tiles_to", "first_tile")]
    place, picked = sb("place", [P, NT, E], F32), sb("picked", [P, NT, E], F32)
    slot_f = sb("slot_f", [P, 2, NT], F32)
    ended, expert_f = sb("ended", [P, NTILE, E], F32), sb("expert_f", [P, NTILE], F32)

    tp, lp = pb("tp", [P, 4, S]), pb("lp", [P, 2, S])
    cum, tot = pb("cum", [P, S]), pb("tot", [P, S])

    t = semaphores(nc, ctx, ["x_loaded0", "x_loaded1", "r_loaded", "pool_filled", "dve_step", "var_ready", "rstd_ready", "norm_ready",
                             "tr_done", "xt_ready", "logit_done", "logit_ready", "shift_ready", "exp_ready", "chosen_ready",
                             "count_done", "slots_ready"], after=big)
    x_loaded = [t["x_loaded0"], t["x_loaded1"]]
    small = [(gate_w[:, :, :], w["gate_w"]), (gate_b[:, :], w["gate_b"].partition_broadcast(P)),
             (lower[:, :, :], w["lower"].partition_broadcast(P)), (before[:, :], w["before"]), (ident[:, :], w["ident"]),
             (keep[:, :, :], w["keep"].partition_broadcast(P)), (step[:, :], w["step"].partition_broadcast(P)),
             (number[:, :], w["number"].partition_broadcast(P))]
    w0, w1, w2, b0, b1, b2 = weights
    large = [(w0[:, :, :], w["w0"]), (w1[:, :, :], w["w1"]), (w2[:, :, :], w["w2"]),
             (b0[:, :], w["b0"].partition_broadcast(P)), (b1[:, :], w["b1"].partition_broadcast(P)),
             (b2[:, :], w["b2"].partition_broadcast(P))]

    def tiles_first(x):
        return x.rearrange("p e q -> p q e")

    def per_token(x):
        return x.rearrange("p (q a) -> p q a", a=1).broadcast_to([P, NT, E])

    with nc.Block() as block:

        @block.sync
        def _(sp):
            for half in range(2):
                rows = x_d[half * HALF * P:(half + 1) * HALF * P, :]
                sp.dma_start(xn[:, half * HALF:(half + 1) * HALF, :], token_major(rows)).then_inc(x_loaded[half], 16)
                if half == 0:
                    for dst, src in small:
                        sp.dma_start(dst, src).then_inc(t["r_loaded"], 16)
            sp.wait_ge(t["pool_filled"], 3)
            for j in range(NTILE):
                sp.dma_start(slots_d[j * P:(j + 1) * P, :], zeros[:, :]).then_inc(big["zeroed"], 16)
            for dst, src in large:
                sp.dma_start(dst, src).then_inc(big["weights_loaded"], 16)
            sp.wait_ge(big["weights_loaded"], 16 * len(large))

        @block.gpsimd
        def _(pool):
            nc.gpsimd.memset(ln["neghalf"][:, :], -0.5).then_inc(t["pool_filled"], 1)
            nc.gpsimd.memset(ones[:, :], 1.0).then_inc(t["pool_filled"], 1)
            nc.gpsimd.memset(zeros[:, :], 0.0).then_inc(t["pool_filled"], 1)
            pool.wait_ge(t["pool_filled"], 3)
            for half in range(2):
                pool_rstd(nc, pool, ln, t["var_ready"], t["rstd_ready"], half + 1)
            pool.wait_ge(t["slots_ready"], 1)
            pool.wait_ge(big["zeroed"], 16 * NTILE)
            for q in range(NT):
                for k in range(2):
                    nc.gpsimd.indirect_dma_start(slots_d[:, :], bass.IndirectOffsetOnAxis(slot[:, k, q:q + 1], 0),
                                                 xn[:, q, :], None, bounds_check=NTILE * P - 1, oob_is_err=True).then_inc(soft["sent"], 16)
            pool.wait_ge(soft["sent"], 16 * 2 * NT)

        @block.scalar
        def _(act):
            for g in range(NT // TT):
                for c in range(DC):
                    act.wait_ge(t["tr_done"], DC * g + c + 1)
                    if g >= 2:
                        act.wait_ge(t["logit_done"], g - 1)
                    nc.scalar.copy(x_t[:, g % 2, c, :], tp[:, DC * (g % 2) + c, :]).then_inc(t["xt_ready"], 1)
            act.wait_ge(t["shift_ready"], 1)
            nc.scalar.activation(expl[:, :, :], logit[:, :, :], ACT.Exp).then_inc(t["exp_ready"], 1)

        @block.vector
        def _(dve):
            link = linker(dve, t["dve_step"])
            for half in range(2):
                part = xn[:, half * HALF:(half + 1) * HALF, :]
                dve.wait_ge(x_loaded[half], 16)
                dve_layernorm(nc, dve, link, part, part, ln, t["var_ready"], t["rstd_ready"], half + 1, HALF).then_inc(t["norm_ready"], 1)
                dve.wait_ge(t["norm_ready"], half + 1)
            dve.wait_ge(t["r_loaded"], 16 * len(small))
            for half in range(2):
                dve.wait_ge(t["logit_done"], (half + 1) * NT // TT // 2)
                last = nc.vector.tensor_tensor(logit[:, half * HALF:(half + 1) * HALF, :],
                                               lp[:, half, 0:HALF * E].rearrange("p (q e) -> p q e", e=E),
                                               gate_b[:, :].rearrange("p (a e) -> p a e", a=1).broadcast_to([P, HALF, E]), ALU.add)
            link(last)
            mine = logit[:, :, :].rearrange("p q (e a) -> p q e a", a=1).broadcast_to([P, NT, E, E])
            others = logit[:, :, :].rearrange("p q (a e) -> p q a e", a=1).broadcast_to([P, NT, E, E])
            lowers = lower[:, :, :].rearrange("p (a e) j -> p a e j", a=1).broadcast_to([P, NT, E, E])
            nc.vector.tensor_tensor(ahead[:, :, :, :], others, mine, ALU.is_gt)
            nc.vector.tensor_tensor(tie[:, :, :, :], others, mine, ALU.is_equal)
            link(nc.vector.tensor_reduce(top[:, :], logit[:, :, :], axis=AX.X, op=ALU.max))
            nc.vector.tensor_tensor(logit[:, :, :], logit[:, :, :], per_token(top[:, :]), ALU.subtract).then_inc(t["shift_ready"], 1)
            link(nc.vector.tensor_tensor(tie[:, :, :, :], tie[:, :, :, :], lowers, ALU.mult))
            link(nc.vector.tensor_tensor(ahead[:, :, :, :], ahead[:, :, :, :], tie[:, :, :, :], ALU.add))
            link(nc.vector.tensor_reduce(rank[:, :, :], ahead[:, :, :, :], axis=AX.X, op=ALU.add))
            nc.vector.tensor_scalar(is_first[:, :, :], rank[:, :, :], 0.0, None, ALU.is_equal)
            nc.vector.tensor_scalar(is_second[:, :, :], rank[:, :, :], 1.0, None, ALU.is_equal)
            nc.vector.tensor_scalar(chosen[:, :, :], rank[:, :, :], 2.0, None, ALU.is_lt).then_inc(t["chosen_ready"], 1)
            dve.wait_ge(t["exp_ready"], 1)
            dve.wait_ge(t["chosen_ready"], 1)
            link(nc.vector.tensor_tensor(expl[:, :, :], expl[:, :, :], chosen[:, :, :], ALU.mult))
            link(nc.vector.tensor_reduce(den[:, :], expl[:, :, :], axis=AX.X, op=ALU.add))
            link(nc.vector.reciprocal(den[:, :], den[:, :]))
            link(nc.vector.tensor_scalar(den[:, :], den[:, :], 0.5, None, ALU.mult))
            link(nc.vector.tensor_tensor(gates[:, :, :], expl[:, :, :], per_token(den[:, :]), ALU.mult))
            dve.wait_ge(t["count_done"], 2)
            link(nc.vector.tensor_copy(per_tile[:, :, :], tot[:, 0:NT * E].rearrange("p (q e) -> p e q", e=E)))
            link(nc.vector.tensor_tensor_scan(running[:, :, :].rearrange("p e q -> p (e q)"), keep[:, :, :].rearrange("p e q -> p (e q)"),
                                              per_tile[:, :, :].rearrange("p e q -> p (e q)"), 0.0, ALU.mult, ALU.add))
            count = running[:, :, NT - 1:NT].broadcast_to([P, E, NT])
            steps = step[:, :].rearrange("p (a q) -> p a q", a=1).broadcast_to([P, E, NT])
            link(nc.vector.tensor_tensor(base[:, :, :], count, steps, ALU.is_gt))
            link(nc.vector.tensor_reduce(n_tiles[:, :], base[:, :, :], axis=AX.X, op=ALU.add))
            link(nc.vector.tensor_tensor_scan(tiles_to[:, :], ones[:, 0:E], n_tiles[:, :], 0.0, ALU.mult, ALU.add))
            link(nc.vector.tensor_tensor(first_tile[:, :], tiles_to[:, :], n_tiles[:, :], ALU.subtract))
            link(nc.vector.tensor_tensor(per_tile[:, :, :], running[:, :, :], per_tile[:, :, :], ALU.subtract))
            firsts = first_tile[:, :].rearrange("p (e a) -> p e a", a=1).broadcast_to([P, E, NT])
            link(nc.vector.scalar_tensor_tensor(base[:, :, :], firsts, float(P), per_tile[:, :, :], ALU.mult, ALU.add))
            link(nc.vector.tensor_tensor(place[:, :, :], cum[:, 0:NT * E].rearrange("p (q e) -> p q e", e=E), tiles_first(base[:, :, :]), ALU.add))
            for k, mark in enumerate((is_first, is_second)):
                link(nc.vector.tensor_tensor(picked[:, :, :], mark[:, :, :], place[:, :, :], ALU.mult))
                link(nc.vector.tensor_reduce(slot_f[:, k, :], picked[:, :, :], axis=AX.X, op=ALU.add))
                link(nc.vector.tensor_tensor(picked[:, :, :], mark[:, :, :], gates[:, :, :], ALU.mult))
                link(nc.vector.tensor_reduce(weight[:, k, :], picked[:, :, :], axis=AX.X, op=ALU.add))
            nc.vector.tensor_copy(slot[:, :, :], slot_f[:, :, :]).then_inc(t["slots_ready"], 1)
            ends = tiles_to[:, :].rearrange("p (a e) -> p a e", a=1).broadcast_to([P, NTILE, E])
            numbers = number[:, :].rearrange("p (j a) -> p j a", a=1).broadcast_to([P, NTILE, E])
            link(nc.vector.tensor_tensor(ended[:, :, :], ends, numbers, ALU.is_le))
            link(nc.vector.tensor_reduce(expert_f[:, :], ended[:, :, :], axis=AX.X, op=ALU.add))
            link(nc.vector.tensor_scalar(expert_f[:, :], expert_f[:, :], float(E - 1), None, ALU.min))
            link(nc.vector.tensor_copy(expert_of[:, :], expert_f[:, :]))

        @block.tensor
        def _(pe):
            pe.wait_ge(t["r_loaded"], 16 * len(small))
            pe.wait_ge(t["pool_filled"], 3)

            def transpose_group(g):
                pe.wait_ge(t["norm_ready"], g // (HALF // TT) + 1)
                if g >= 2:
                    pe.wait_ge(t["xt_ready"], DC * (g - 1))
                pe_transpose_tokens(nc, [tp[:, DC * (g % 2) + c, :] for c in range(DC)], xn[:, g * TT:(g + 1) * TT, :], ident, t["tr_done"])

            transpose_group(0)
            for g in range(NT // TT):
                if g + 1 < NT // TT:
                    transpose_group(g + 1)
                pe.wait_ge(t["xt_ready"], DC * (g + 1))
                for q in range(TT):
                    col = (g * TT + q) % HALF * E
                    for c in range(DC):
                        last = nc.tensor.matmul(lp[:, g * TT // HALF, col:col + E], x_t[:, g % 2, c, q * P:(q + 1) * P], gate_w[:, c, :],
                                                start=(c == 0), stop=(c == DC - 1))
                last.then_inc(t["logit_done"], 1)
            pe.wait_ge(t["chosen_ready"], 1)
            marks = chosen[:, :, :].rearrange("p q e -> p (q e)")
            nc.tensor.matmul(cum[:, 0:NT * E], before[:, :], marks, start=True, stop=True).then_inc(t["count_done"], 1)
            nc.tensor.matmul(tot[:, 0:NT * E], ones[:, :], marks, start=True, stop=True).then_inc(t["count_done"], 1)

    end_turn(nc, t)


def moe_experts(nc, ctx, slots_d, expert_out_d, tag, ident, weights, expert_of, big):
    sb = lambda n, s, t: ctx.enter_context(nc.sbuf_tensor(f"{tag}_{n}", s, t))
    pb = lambda n, s: ctx.enter_context(nc.psum_tensor(f"{tag}_{n}", s, F32))
    w0, w1, w2, b0, b1, b2 = weights
    NX = 4
    xs, ys = sb("xs", [P, NX, D], F32), sb("ys", [P, 2, D], F32)
    xs_t = sb("xs_t", [P, 2, DC, P], F32)
    z, up, sil, hid = [sb(n, [P, 2, HID], F32) for n in ("z", "up", "sil", "hid")]
    hid_t = sb("hid_t", [P, 2, HC, P], F32)
    tp = pb("tpx", [P, S])
    h0, h1 = pb("h0", [P, 2, S]), pb("h1", [P, 2, S])
    hp = pb("hpx", [P, 2, S])
    op = pb("opx", [P, S])
    t = semaphores(nc, ctx, ["xs_loaded0", "xs_loaded1", "xs_loaded2", "xs_loaded3", "xs_tr_done", "xs_t_ready", "h1_done", "h0_done",
                             "z_ready", "up_ready", "sil_ready", "hid_ready", "hid_tr_done", "hid_t_ready", "out_done", "ys_ready",
                             "ys_stored0", "ys_stored1"], after=big)
    xs_loaded = [t[f"xs_loaded{i}"] for i in range(NX)]
    ys_stored = [t["ys_stored0"], t["ys_stored1"]]

    with nc.Fori(0, NTILE // TILES) as r:
        with nc.Block() as block:

            @block.sync
            def _(sp):
                def store(i):
                    sp.wait_ge(t["ys_ready"], i + 1)
                    sp.dma_start(expert_out_d[bass.ds((r * TILES + i) * P, P), :], ys[:, i % 2, :]).then_inc(ys_stored[i % 2], 16)

                for i in range(TILES):
                    if i >= NX:
                        sp.wait_ge(t["xs_tr_done"], i - NX + 1)
                    sp.dma_start(xs[:, i % NX, :], slots_d[bass.ds((r * TILES + i) * P, P), :]).then_inc(xs_loaded[i % NX], 16)
                    if i >= NX:
                        store(i - NX)
                for i in range(TILES - NX, TILES):
                    store(i)
                for k in range(2):
                    sp.wait_ge(ys_stored[k], 16 * (TILES // 2))

            @block.gpsimd
            def _(pool):
                for i in range(TILES):
                    pool.wait_ge(t["sil_ready"], i + 1)
                    pool.wait_ge(t["up_ready"], i + 1)
                    if i >= 2:
                        pool.wait_ge(t["hid_tr_done"], i - 1)
                    nc.gpsimd.tensor_tensor(hid[:, i % 2, :], up[:, i % 2, :], sil[:, i % 2, :], ALU.mult).then_inc(t["hid_ready"], 1)

            @block.scalar
            def _(act):
                def copy_rows(i):
                    act.wait_ge(t["xs_tr_done"], i + 1)
                    if i >= 2:
                        act.wait_ge(t["h0_done"], i - 1)
                    nc.scalar.copy(xs_t[:, i % 2, :, :].rearrange("p c s -> p (c s)"), tp[:, 0:DC * P]).then_inc(t["xs_t_ready"], 1)

                def copy_hidden(i):
                    act.wait_ge(t["hid_tr_done"], i + 1)
                    if i >= 2:
                        act.wait_ge(t["out_done"], i - 1)
                    nc.scalar.copy(hid_t[:, i % 2, :, :].rearrange("p c s -> p (c s)"), hp[:, i % 2, :]).then_inc(t["hid_t_ready"], 1)

                copy_rows(0)
                for i in range(TILES):
                    if i + 1 < TILES:
                        copy_rows(i + 1)
                    act.wait_ge(t["z_ready"], i + 1)
                    if i >= 2:
                        act.wait_ge(t["hid_ready"], i - 1)
                    nc.scalar.activation(sil[:, i % 2, :], z[:, i % 2, :], ACT.Silu).then_inc(t["sil_ready"], 1)
                    if i:
                        copy_hidden(i - 1)
                copy_hidden(TILES - 1)

            @block.vector
            def _(dve):
                def finish(i, e):
                    dve.wait_ge(t["out_done"], i + 1)
                    if i >= 2:
                        dve.wait_ge(ys_stored[i % 2], 16 * (i // 2))
                    nc.vector.tensor_tensor(ys[:, i % 2, :], op[:, 0:D], b2[:, bass.ds(e * D, D)], ALU.add).then_inc(t["ys_ready"], 1)

                was = None
                for i in range(TILES):
                    e = dve.value_load(expert_of[0:1, bass.ds(r * TILES + i, 1)], min_val=0, max_val=E - 1)
                    dve.wait_ge(t["h1_done"], i + 1)
                    if i >= 2:
                        dve.wait_ge(t["sil_ready"], i - 1)
                    nc.vector.tensor_tensor(z[:, i % 2, :], h1[:, i % 2, :], b1[:, bass.ds(e * HID, HID)], ALU.add).then_inc(t["z_ready"], 1)
                    dve.wait_ge(t["h0_done"], i + 1)
                    if i >= 2:
                        dve.wait_ge(t["hid_ready"], i - 1)
                    nc.vector.tensor_tensor(up[:, i % 2, :], h0[:, i % 2, :], b0[:, bass.ds(e * HID, HID)], ALU.add).then_inc(t["up_ready"], 1)
                    if i:
                        finish(i - 1, was)
                    was = e
                finish(TILES - 1, was)

            @block.tensor
            def _(pe):
                def transpose_rows(i):
                    pe.wait_ge(xs_loaded[i % NX], 16 * (i // NX + 1))
                    if i:
                        pe.wait_ge(t["xs_t_ready"], i)
                    for c in range(DC):
                        last = nc.tensor.transpose(tp[:, c * P:(c + 1) * P], xs[:, i % NX, c * P:(c + 1) * P], ident[:, :])
                    last.then_inc(t["xs_tr_done"], 1)

                def up_products(i, e):
                    pe.wait_ge(t["xs_t_ready"], i + 1)
                    if i >= 2:
                        pe.wait_ge(t["up_ready"], i - 1)
                    for out, wgt, done in ((h1, w1, t["h1_done"]), (h0, w0, t["h0_done"])):
                        for c in range(DC):
                            last = nc.tensor.matmul(out[:, i % 2, :], xs_t[:, i % 2, c, :], wgt[:, c, bass.ds(e * HID, HID)],
                                                    start=(c == 0), stop=(c == DC - 1))
                        last.then_inc(done, 1)

                def transpose_hidden(i):
                    pe.wait_ge(t["hid_ready"], i + 1)
                    if i >= 2:
                        pe.wait_ge(t["hid_t_ready"], i - 1)
                    for c in range(HC):
                        last = nc.tensor.transpose(hp[:, i % 2, c * P:(c + 1) * P], hid[:, i % 2, c * P:(c + 1) * P], ident[:, :])
                    last.then_inc(t["hid_tr_done"], 1)

                def down_products(i, e):
                    pe.wait_ge(t["hid_t_ready"], i + 1)
                    if i:
                        pe.wait_ge(t["ys_ready"], i)
                    for c in range(HC):
                        last = nc.tensor.matmul(op[:, 0:D], hid_t[:, i % 2, c, :], w2[:, c, bass.ds(e * D, D)], start=(c == 0), stop=(c == HC - 1))
                    last.then_inc(t["out_done"], 1)

                transpose_rows(0)
                was = None
                for i in range(TILES):
                    e = pe.value_load(expert_of[0:1, bass.ds(r * TILES + i, 1)], min_val=0, max_val=E - 1)
                    if i + 1 < TILES:
                        transpose_rows(i + 1)
                    up_products(i, e)
                    if i:
                        transpose_hidden(i - 1)
                        down_products(i - 1, was)
                    was = e
                transpose_hidden(TILES - 1)
                down_products(TILES - 1, was)

        end_turn(nc, t)


def moe_combine(nc, ctx, x_d, x_out_d, expert_out_d, tag, slot, weight, big, soft):
    sb = lambda n, s, t: ctx.enter_context(nc.sbuf_tensor(f"{tag}_{n}", s, t))
    NR = SOFTWARE - 1
    rows = sb("rows", [P, NR, 2, D], F32)
    x = sb("xc", [P, NT, D], F32)
    t = semaphores(nc, ctx, ["xc_loaded", "first_added", "added", "x_stored"], after=big)
    row_loaded = [soft[f"row_loaded{i}"] for i in range(NR)]
    with nc.Block() as block:

        @block.sync
        def _(sp):
            sp.dma_start(x[:, :, :], token_major(x_d)).then_inc(t["xc_loaded"], 16)
            for g in range(NT // TT):
                sp.wait_ge(t["added"], TT * (g + 1))
                sp.dma_start(token_major(x_out_d[g * S:(g + 1) * S, :]), x[:, g * TT:(g + 1) * TT, :]).then_inc(t["x_stored"], 16)
            sp.wait_ge(t["x_stored"], 16 * (NT // TT))

        @block.gpsimd
        def _(pool):
            for q in range(NT):
                if q >= NR:
                    pool.wait_ge(t["added"], q - NR + 1)
                for k in range(2):
                    nc.gpsimd.indirect_dma_start(rows[:, q % NR, k, :], None, expert_out_d[:, :],
                                                 bass.IndirectOffsetOnAxis(slot[:, k, q:q + 1], 0),
                                                 bounds_check=NTILE * P - 1, oob_is_err=True).then_inc(row_loaded[q % NR], 16)

        @block.vector
        def _(dve):
            dve.wait_ge(t["xc_loaded"], 16)
            for q in range(NT):
                dve.wait_ge(row_loaded[q % NR], 32 * (q // NR + 1))
                nc.vector.scalar_tensor_tensor(x[:, q, :], rows[:, q % NR, 0, :], weight[:, 0, q:q + 1], x[:, q, :],
                                               ALU.mult, ALU.add).then_inc(t["first_added"], 1)
                dve.wait_ge(t["first_added"], q + 1)
                nc.vector.scalar_tensor_tensor(x[:, q, :], rows[:, q % NR, 1, :], weight[:, 1, q:q + 1], x[:, q, :],
                                               ALU.mult, ALU.add).then_inc(t["added"], 1)

    end_turn(nc, t)


def lay_out(**a):
    f = lambda n: np.asarray(a[n])
    idx = np.outer(np.arange(D), np.arange(D)) % D
    ang = 2 * np.pi * idx / D
    pos = np.arange(S, dtype=np.float32)[:, None]
    div = np.exp(np.arange(0, D, 2, dtype=np.float32) * np.float32(-np.log(10000.0) / D))
    pe = np.zeros((S, D), np.float32)
    pe[:, 0::2] = np.sin(pos * div)
    pe[:, 1::2] = np.cos(pos * div)
    c, d, j = np.meshgrid(np.arange(DC), np.arange(DH), np.arange(8), indexing="ij")
    perm = ((2 * j + c) * DH + d).reshape(-1)
    pick = np.zeros((96, 2 * NS, P), np.float32)
    for part in range(3):
        pick[32 * part + np.arange(2 * NS), np.arange(2 * NS)] = 1.0
    pick = pick.astype(mybir.dt.np(BF16))
    out = {
        "ident": np.eye(P, dtype=np.float32),
        "pos": pe,
        "cos": np.cos(ang).astype(np.float32), "sin": np.sin(ang).astype(np.float32), "ncos": (-np.cos(ang)).astype(np.float32),
        "w_real": f("L0_ffn_w_freq_real"), "w_imag": f("L0_ffn_w_freq_imag"), "ffn_bias": f("L0_ffn_bias"),
        "Wq": f("L0_attn_Wq")[:, perm], "Wk": f("L0_attn_Wk")[:, perm], "Wv": f("L0_attn_Wv"), "Wo": f("L0_attn_Wo"),
        "bq": f("L0_attn_bq")[perm].reshape(DC, P).T, "bk": f("L0_attn_bk")[perm].reshape(DC, P).T, "bv": f("L0_attn_bv"), "bo": f("L0_attn_bo"),
        "gamma": f("L0_attn_gamma"), "beta": f("L0_attn_beta"),
        "pick": pick,
        "w_in": f("L1_attn_w_in"), "w_dt": f("L1_attn_w_dt"), "w_out": f("L1_attn_w_out"),
        "w_xproj3": np.concatenate([f("L1_attn_w_xproj")] * 3, axis=1),
        "ln_g": f("L1_attn_ln_g"), "ln_b": f("L1_attn_ln_b"),
        "conv_w": f("L1_attn_conv_w").reshape(IC, P, KC).transpose(1, 0, 2),
        "A_log": f("L1_attn_A_log").reshape(IC, P, NS).transpose(1, 0, 2),
        "conv_b": f("L1_attn_conv_b").reshape(IC, P).T, "b_dt": f("L1_attn_b_dt").reshape(IC, P).T,
        "skip": f("L1_attn_D").reshape(IC, P).T,
        "w0": f("L1_ffn_w0").reshape(E, HID, DC, P).transpose(3, 2, 0, 1).reshape(P, DC, E * HID),
        "w1": f("L1_ffn_w1").reshape(E, HID, DC, P).transpose(3, 2, 0, 1).reshape(P, DC, E * HID),
        "w2": f("L1_ffn_w2").reshape(E, D, HC, P).transpose(3, 2, 0, 1).reshape(P, HC, E * D),
        "b0": f("L1_ffn_b0").reshape(E * HID), "b1": f("L1_ffn_b1").reshape(E * HID), "b2": f("L1_ffn_b2").reshape(E * D),
        "gate_w": f("L1_ffn_gate_w").reshape(E, DC, P).transpose(2, 1, 0), "gate_b": f("L1_ffn_gate_b"),
        "lower": np.tril(np.ones((E, E), np.float32), -1),
        "before": np.triu(np.ones((P, P), np.float32), 1),
        "keep": np.tile(np.arange(NT) > 0, (E, 1)).astype(np.float32),
        "step": (P * np.arange(NT)).astype(np.float32), "number": np.arange(NTILE, dtype=np.float32),
    }
    return {k: np.ascontiguousarray(v) for k, v in out.items()}


def build(nc, w, out_d):
    rows = lambda name: nc.dram_tensor(name, (NB * S, D), F32).ap()
    mix, x3, x4, x5 = nc.dram_tensor("mix_matrix", (D, D), F32).ap(), rows("x3_rows"), rows("x4_rows"), rows("x5_rows")
    slots = nc.dram_tensor("slot_rows", (NTILE * P, D), F32).ap()
    expert_out = nc.dram_tensor("expert_rows", (NTILE * P, D), F32).ap()
    mixer_matrix(nc, w["cos"], w["sin"], w["ncos"], w["w_real"], w["w_imag"], mix)
    attention_stage(nc, w["x"], x3, {**w, "mix": mix})
    moe_stage(nc, x3, x4, w, slots, expert_out, 0, "moe1")
    mamba_stage(nc, x4, x5, w)
    moe_stage(nc, x5, out_d, w, slots, expert_out, 1, "moe2")


def kernel(**inputs):
    import concourse.bacc as bacc
    from concourse.bass_utils import run_bass_kernel_spmd

    arrays = {"in_" + k: v for k, v in lay_out(**inputs).items()}
    arrays["in_x"] = np.ascontiguousarray(np.asarray(inputs["L0_attn_x"]).reshape(NB * S, D))
    nc = bacc.Bacc("TRN2", target_bir_lowering=False, num_devices=1)
    w = {k[3:]: nc.dram_tensor(k, a.shape, mybir.dt.from_np(a.dtype), kind="ExternalInput").ap() for k, a in arrays.items()}
    out_d = nc.dram_tensor("out_rows", (NB * S, D), F32, kind="ExternalOutput").ap()
    build(nc, w, out_d)
    r = run_bass_kernel_spmd(nc, [arrays], core_ids=[0])
    return r.results[0]["out_rows"].reshape(NB, S, D)
```

```python
from contextlib import ExitStack

import numpy as np

import concourse.bass as bass
from concourse import mybir

F32 = mybir.dt.float32
BF16 = mybir.dt.bfloat16
I32 = mybir.dt.int32
ALU = mybir.AluOpType
ACT = mybir.ActivationFunctionType
AX = mybir.AxisListType

P = 128
NB, S, D = 8, 512, 256
TT = S // P
DC = D // P
H, DH = 16, 16
HG = 4
NG = H // HG
DI, NS, KC = 512, 16, 4
IC = DI // P
E, HID = 8, 512
HC = HID // P
EPS = 1e-5
NT = NB * TT
NTILE = 72
TILES = 24
FIRST_SEMAPHORE = 100
SOFTWARE = 7
NPIECE = 6


def semaphores(nc, ctx, names, after=None):
    first = max(s.num for s in after.values()) + 1 if after else FIRST_SEMAPHORE + 2 * SOFTWARE + 1
    return {n: ctx.enter_context(nc.semaphore(n, num=first + i)) for i, n in enumerate(names)}


def software_semaphores(nc, ctx, use):
    names = [*(f"xs_loaded{i}" for i in range(4)), *(f"ys_stored{i}" for i in range(3))]
    return {n: ctx.enter_context(nc.semaphore(n, num=FIRST_SEMAPHORE + use * SOFTWARE + i)) for i, n in enumerate(names)}


def end_turn(nc, sems):
    numbers = sorted(s.num for s in sems.values())
    assert numbers == list(range(numbers[0], numbers[-1] + 1))
    nc.all_engine_barrier(sems_to_clear=range(numbers[0], numbers[-1] + 1))


def linker(engine, sem):
    count = [0]

    def link(instruction):
        count[0] += 1
        instruction.then_inc(sem, 1)
        engine.wait_ge(sem, count[0])

    return link


def token_major(dram_rows):
    return dram_rows.rearrange("(q p) d -> p q d", p=P)


def dve_layernorm(nc, dve, link, src, dst, ln, var_ready, rstd_ready, turn, tiles=TT):
    for q in range(tiles):
        last = nc.vector.bn_stats(ln["stats"][:, q, :], src[:, q, :])
    link(last)
    for q in range(tiles):
        last = nc.vector.bn_aggr(ln["mv"][:, q, :], ln["stats"][:, q, :])
    link(last)
    nc.vector.tensor_scalar(ln["vareps"][:, :], ln["mv"][:, :, 1], EPS, None, ALU.add).then_inc(var_ready, 1)
    dve.wait_ge(rstd_ready, turn)
    for q in range(tiles):
        last = nc.vector.tensor_scalar(dst[:, q, :], src[:, q, :], ln["mv"][:, q, 0:1],
                                       ln["rstd"][:, q:q + 1], ALU.subtract, ALU.mult)
    return last


def pool_rstd(nc, pool, ln, var_ready, rstd_ready, turn):
    pool.wait_ge(var_ready, turn)
    nc.gpsimd.tensor_tensor(ln["rstd"][:, :], ln["vareps"][:, :], ln["neghalf"][:, :], ALU.pow).then_inc(rstd_ready, 1)


def ln_buffers(sb, tiles=TT):
    return {"stats": sb("ln_stats", [P, tiles, 6], F32), "mv": sb("ln_mv", [P, tiles, 2], F32),
            "vareps": sb("ln_vareps", [P, tiles], F32), "rstd": sb("ln_rstd", [P, tiles], F32),
            "neghalf": sb("ln_neghalf", [P, tiles], F32)}


def pe_transpose_tokens(nc, banks, src, ident, done):
    for c in range(DC):
        for q in range(TT):
            last = nc.tensor.transpose(banks[c][:, q * P:(q + 1) * P], src[:, q, c * P:(c + 1) * P], ident[:, :])
        last.then_inc(done, 1)


def pe_project_tokens(nc, banks, lhs_t, weights, chunks, done):
    for q in range(TT):
        for c in range(chunks):
            last = nc.tensor.matmul(banks[q // 2][:, (q % 2) * D:(q % 2 + 1) * D], lhs_t[:, c, q * P:(q + 1) * P],
                                    weights[:, c, :], start=(c == 0), stop=(c == chunks - 1))
        if q % 2:
            last.then_inc(done, 1)


def attention_stage(nc, x_d, x_out_d, w, tag="att"):
    UNITS = H * TT
    GU = HG * TT
    LEAD = 3 * GU // 2
    with ExitStack() as ctx:
        sb = lambda n, s, t: ctx.enter_context(nc.sbuf_tensor(f"{tag}_{n}", s, t))
        pb = lambda n, s: ctx.enter_context(nc.psum_tensor(f"{tag}_{n}", s, F32))
        ident = sb("ident", [P, P], F32)
        pos = sb("pos", [P, TT, D], F32)
        mix, wq, wk, wv, wo = [sb(n, [P, DC, D], F32) for n in ("mix", "wq", "wk", "wv", "wo")]
        consts = {n: sb(n, [P, D], F32) for n in ("half_bias", "bv", "bo", "gamma", "beta")}
        bqc, bkc = sb("bqc", [P, DC], F32), sb("bkc", [P, DC], F32)
        ln = ln_buffers(sb)

        x0, x0b, xn, x1, h = [sb(n, [P, TT, D], F32) for n in ("x0", "x0b", "xn", "x1", "h")]
        y, yn, out, o_tok = [sb(n, [P, TT, D], F32) for n in ("y", "yn", "out", "o_tok")]
        x_t = sb("x_t", [P, DC, S], F32)
        qk_f = sb("qk_f", [P, 2 * DC, S], F32)
        res = sb("res", [P, 2 * DC, S], F32)
        parts = [sb(f"part{i}", [P, 2 * DC, S], BF16) for i in range(3)]
        rows = [{"q": sb(f"q{k}", [P, H, S], BF16), "k": sb(f"k{k}", [P, H, S], BF16),
                 "v": sb(f"v{k}", [P, TT, H, 32], F32),
                 "hb": sb(f"hb{k}", [P, TT, D], F32), "x1b": sb(f"x1b{k}", [P, TT, D], F32)} for k in range(2)]
        NPR = 4
        probs = sb("probs", [P, NPR, S], F32)
        negmax = sb("negmax", [P, NG, HG, TT], F32)
        nm_hi, nm_lo = sb("nm_hi", [P, NG, P], BF16), sb("nm_lo", [P, NG, P], BF16)
        o_t = sb("o_t", [P, 2, S], F32)
        rden = sb("rden", [P, TT, HG], F32)

        NRING = 3
        ring = pb("ring", [P, NRING, S])
        st = pb("st", [P, 2, S])
        ob = pb("ob", [P, S])
        pp = pb("pp", [P, 2, S])
        pp_banks = [pp[:, i, :] for i in range(2)]

        setup = semaphores(nc, ctx, ["a_loaded", "mix_loaded", "pool_filled", "dve_filled", "mix_parts_done", "mix_parts_copied", "mix_done"])
        loads = [(ident[:, :], w["ident"]), (pos[:, :, :], token_major(w["pos"]))]
        loads += [(dst[:, :, :], w[n].rearrange("(c p) n -> p c n", p=P))
                  for dst, n in ((wq, "Wq"), (wk, "Wk"), (wv, "Wv"), (wo, "Wo"))]
        loads += [(consts[n][:, :], w[src].partition_broadcast(P))
                  for n, src in (("half_bias", "ffn_bias"), ("bv", "bv"), ("bo", "bo"), ("gamma", "gamma"), ("beta", "beta"))]
        loads += [(bqc[:, :], w["bq"]), (bkc[:, :], w["bk"])]
        loads += [(rows[k]["k"][96:98, :, :], w["ones"]) for k in range(2)]
        cos, sin, ncos, wr, wi = [b[:, 0:DC, :] for b in (x0, x0b, xn, x1, h)]
        pt, nqt = y[:, 0:DC, :], yn[:, 0:DC, :]
        pt_ps, nqt_ps, mix_ps = [bank.rearrange("p (c n) -> p c n", c=DC) for bank in (ring[:, 0, :], ring[:, 1, :], st[:, 0, :])]
        mix_loads = [(dst, w[n].rearrange("(c p) n -> p c n", p=P))
                     for dst, n in ((cos, "cos"), (sin, "sin"), (ncos, "ncos"), (wr, "w_real"), (wi, "w_imag"))]
        with nc.Block() as block:

            @block.sync
            def _(sp):
                for dst, src in mix_loads:
                    sp.dma_start(dst, src).then_inc(setup["mix_loaded"], 16)
                for dst, src in loads:
                    sp.dma_start(dst, src).then_inc(setup["a_loaded"], 16)
                sp.wait_ge(setup["a_loaded"], 16 * len(loads))

            @block.gpsimd
            def _(pool):
                nc.gpsimd.memset(ln["neghalf"][:, :], -0.5).then_inc(setup["pool_filled"], 1)
                for k in range(2):
                    nc.gpsimd.memset(rows[k]["v"][:, :, :, 16:32], 0.0).then_inc(setup["pool_filled"], 1)
                    pool.wait_ge(setup["pool_filled"], 2 + 2 * k)
                    nc.gpsimd.memset(rows[k]["v"][:, :, :, 16:17], 1.0).then_inc(setup["pool_filled"], 1)
                pool.wait_ge(setup["pool_filled"], 5)

            @block.tensor
            def _(pe):
                pe.wait_ge(setup["mix_loaded"], 16 * len(mix_loads))
                for out_ps, a, b in ((pt_ps, cos, sin), (nqt_ps, sin, ncos)):
                    for m in range(DC):
                        for c in range(DC):
                            nc.tensor.matmul(out_ps[:, m, :], wr[:, c, m * P:(m + 1) * P], a[:, c, :], start=(c == 0), stop=False)
                            last = nc.tensor.matmul(out_ps[:, m, :], wi[:, c, m * P:(m + 1) * P], b[:, c, :], start=False,
                                                    stop=(c == DC - 1))
                    last.then_inc(setup["mix_parts_done"], 1)
                pe.wait_ge(setup["mix_parts_copied"], 2)
                for m in range(DC):
                    for c in range(DC):
                        nc.tensor.matmul(mix_ps[:, m, :], pt[:, c, m * P:(m + 1) * P], cos[:, c, :], start=(c == 0), stop=False)
                        last = nc.tensor.matmul(mix_ps[:, m, :], nqt[:, c, m * P:(m + 1) * P], sin[:, c, :], start=False,
                                                stop=(c == DC - 1))
                last.then_inc(setup["mix_done"], 1)

            @block.vector
            def _(dve):
                for i, (dst, src) in enumerate(((pt, pt_ps), (nqt, nqt_ps))):
                    dve.wait_ge(setup["mix_parts_done"], i + 1)
                    nc.vector.tensor_copy(dst, src).then_inc(setup["mix_parts_copied"], 1)
                dve.wait_ge(setup["mix_done"], 1)
                nc.vector.tensor_scalar(mix[:, :, :], mix_ps, 0.5 / D, None, ALU.mult).then_inc(setup["dve_filled"], 1)
                dve.wait_ge(setup["a_loaded"], 16 * len(loads))
                nc.vector.tensor_scalar(consts["half_bias"][:, :], consts["half_bias"][:, :], 0.5, None,
                                        ALU.mult).then_inc(setup["dve_filled"], 1)

        end_turn(nc, setup)

        t = semaphores(nc, ctx, ["x_loaded", "x_stored", "dve_step", "var_ready", "rstd_ready", "x0b_ready", "out_base_ready",
                                 "taken", "renewed", "norm_ready", "out_ready", "h_ready",
                                 "tr_done", "xt_ready", "tok_done", "tok_used", "qk_done", "qk_in", "hi_ready", "mid_ready", "lo_ready",
                                 "stacked", "ring_done", "ring_used", "nm_ready", *(f"nm_placed{g}" for g in range(NG)),
                                 "st_done", "probs_ready", "pv_done", "ot_ready"], after=setup)
        nm_placed = [t["nm_placed0"], t["nm_placed1"], t["nm_placed2"], t["nm_placed3"]]
        q_piece, k_piece = (0, 0, 1, 1, 0, 2), (0, 1, 0, 1, 2, 0)

        def bc(row):
            return row[:, :].rearrange("p (a d) -> p a d", a=1).broadcast_to([P, TT, D])

        def pairs(bank):
            return bank.rearrange("p (a d) -> p a d", a=2)

        def phase(cur, other, core=True, prologue=True, ahead_row=None, last_row=None):
            ahead, epilogue = ahead_row is not None, last_row is not None
            present = {"o": epilogue, "h": prologue, "x2": epilogue, "x0": ahead,
                       "wo": epilogue, "v": prologue, "mix_last": epilogue, "mix_ahead": ahead,
                       "norm_y": epilogue, "norm_x2": epilogue, "norm_x0": ahead, "norm_x1": ahead}
            order = {"transposed": ("o", "h", "x2", "x0"), "projected": ("wo", "v", "mix_last", "mix_ahead"),
                     "normed": ("norm_y", "norm_x2", "norm_x0", "norm_x1")}

            def before(kind, name):
                steps = order[kind]
                return sum(present[s] for s in steps[:steps.index(name)])

            def turn(kind, name):
                return before(kind, name) + 1

            projected_before = {"o": 0, "h": before("projected", "v"), "x2": before("projected", "mix_last"),
                                "x0": before("projected", "mix_ahead")}

            def has_score(u):
                return prologue if u + LEAD >= UNITS else core

            complete = {GU * g + GU - LEAD: g for g in range(1, NG)} if core else {}
            if prologue:
                complete[UNITS + GU - LEAD] = 0
            placed_to = {u: i + 1 for i, u in enumerate(sorted(complete))}
            turned = {GU * (g + 1) + 3: g for g in range(NG - 1)} if core else {}
            entries = [("outputs", -1)] if epilogue else []
            for u in range(UNITS):
                entries += [("scores", u)] * has_score(u) + [("maxima", u)] * (u in complete) + [("outputs", u)] * (u in turned)
            entry = {e: i + 1 for i, e in enumerate(entries)}

            def bank(e):
                return ring[:, (entry[e] - 1) % NRING, :]

            with nc.Block() as block:

                @block.sync
                def _(sp):
                    def place(u):
                        g = complete[u]
                        target = other if g == 0 else cur
                        sp.wait_ge(t["nm_ready"], 2 * placed_to[u])
                        for row, src in ((96, nm_hi), (97, nm_lo)):
                            sp.dma_start(target["q"][row:row + 1, HG * g:HG * g + HG, :], src[0:HG * TT, g, :]).then_inc(nm_placed[g], 16)

                    if ahead:
                        sp.dma_start(x0[:, :, :], token_major(x_d[bass.ds(ahead_row, S), :])).then_inc(t["x_loaded"], 16)
                    places = sorted(complete)
                    if core:
                        place(places[0])
                    if prologue:
                        ready = (t["hi_ready"], t["mid_ready"], t["lo_ready"])
                        for part in range(3):
                            sp.wait_ge(ready[part], 2)
                            for i in range(NPIECE):
                                for which, (piece, stack) in enumerate(((q_piece, other["q"]), (k_piece, other["k"]))):
                                    if piece[i] == part:
                                        sp.dma_start(stack[DH * i:DH * i + DH, :, :],
                                                     parts[part][:, DC * which:DC * which + DC, :]).then_inc(t["stacked"], 16)
                    if core:
                        place(places[1])
                    if epilogue:
                        sp.wait_ge(t["out_ready"], 1)
                        sp.dma_start(token_major(x_out_d[bass.ds(last_row, S), :]), out[:, :, :]).then_inc(t["x_stored"], 16)
                    if core:
                        place(places[2])
                    if prologue:
                        place(places[-1])
                        sp.wait_ge(nm_placed[0], 32)
                    if epilogue:
                        sp.wait_ge(t["x_stored"], 16)

                @block.gpsimd
                def _(pool):
                    if epilogue:
                        pool_rstd(nc, pool, ln, t["var_ready"], t["rstd_ready"], turn("normed", "norm_y"))
                    if prologue:
                        if epilogue:
                            pool.wait_ge(t["taken"], 1)
                        nc.gpsimd.tensor_tensor(other["hb"][:, :, :], h[:, :, :], bc(consts["bo"]), ALU.add).then_inc(t["renewed"], 1)
                        if epilogue:
                            pool.wait_ge(t["taken"], 2)
                        nc.gpsimd.tensor_tensor(other["x1b"][:, :, :], x1[:, :, :], bc(consts["beta"]), ALU.add).then_inc(t["renewed"], 1)
                    if epilogue:
                        pool_rstd(nc, pool, ln, t["var_ready"], t["rstd_ready"], turn("normed", "norm_x2"))
                        nc.gpsimd.tensor_tensor(out[:, :, :], y[:, :, :], bc(consts["half_bias"]), ALU.add).then_inc(t["out_base_ready"], 1)
                    if ahead:
                        pool.wait_ge(t["x_loaded"], 16)
                        nc.gpsimd.tensor_tensor(x0b[:, :, :], x0[:, :, :], bc(consts["half_bias"]), ALU.add).then_inc(t["x0b_ready"], 1)
                        pool_rstd(nc, pool, ln, t["var_ready"], t["rstd_ready"], turn("normed", "norm_x0"))
                        pool_rstd(nc, pool, ln, t["var_ready"], t["rstd_ready"], turn("normed", "norm_x1"))

                @block.scalar
                def _(act):
                    def copy_transposed(name):
                        before_it = before("transposed", name)
                        if projected_before[name]:
                            act.wait_ge(t["tok_done"], 2 * projected_before[name])
                        for c in range(DC):
                            act.wait_ge(t["tr_done"], DC * before_it + c + 1)
                            nc.scalar.copy(x_t[:, c, :], pp_banks[c]).then_inc(t["xt_ready"], 1)

                    def copy_outputs(g):
                        act.wait_ge(t["pv_done"], GU * (g + 1))
                        if g >= 2 or (g == 1 and epilogue):
                            act.wait_ge(t["ring_done"], entry[("outputs", GU * (g - 1) + 3 if g >= 2 else -1)])
                        nc.scalar.copy(o_t[:, g % 2, :], ob[:, :]).then_inc(t["ot_ready"], 1)

                    for u in range(UNITS):
                        if core:
                            act.wait_ge(t["st_done"], u + 1)
                            if u >= NPR:
                                act.wait_ge(t["pv_done"], u - NPR + 1)
                            nc.scalar.activation(probs[:, u % NPR, :], st[:, u % 2, :], ACT.Exp, scale=DH ** -0.5).then_inc(t["probs_ready"], 1)
                            if u and u % GU == 0:
                                copy_outputs(u // GU - 1)
                        if epilogue and u == 6:
                            copy_transposed("o")
                        if prologue and u == 10:
                            copy_transposed("h")
                        if prologue and u in (12, 13, 14, 15):
                            i = u - 12
                            act.wait_ge(t["qk_done"], i + 1)
                            bias = (bqc if i < DC else bkc)[:, i % DC:i % DC + 1]
                            nc.scalar.activation(qk_f[:, i, :], pp_banks[i % 2], ACT.Identity, bias=bias).then_inc(t["qk_in"], 1)
                        if prologue and u in (16, 18):
                            i = (u - 16) // 2
                            act.wait_ge(t["qk_in"], 2 * DC)
                            nc.scalar.copy(parts[0][:, DC * i:DC * i + DC, :], qk_f[:, DC * i:DC * i + DC, :]).then_inc(t["hi_ready"], 1)
                        if epilogue and u == 26:
                            copy_transposed("x2")
                        if ahead and u == 35:
                            copy_transposed("x0")
                    if core:
                        copy_outputs(NG - 1)

                @block.vector
                def _(dve):
                    link = linker(dve, t["dve_step"])

                    def norm_stats(src):
                        for q in range(TT):
                            last = nc.vector.bn_stats(ln["stats"][:, q, :], src[:, q, :])
                        link(last)
                        for q in range(TT):
                            last = nc.vector.bn_aggr(ln["mv"][:, q, :], ln["stats"][:, q, :])
                        link(last)
                        nc.vector.tensor_scalar(ln["vareps"][:, :], ln["mv"][:, :, 1], EPS, None, ALU.add).then_inc(t["var_ready"], 1)

                    def norm_apply(dst, src, name):
                        dve.wait_ge(t["rstd_ready"], turn("normed", name))
                        for q in range(TT):
                            last = nc.vector.tensor_scalar(dst[:, q, :], src[:, q, :], ln["mv"][:, q, 0:1],
                                                           ln["rstd"][:, q:q + 1], ALU.subtract, ALU.mult)
                        link(last)

                    def add_projected(dst, name, base):
                        for i in range(2):
                            dve.wait_ge(t["tok_done"], 2 * before("projected", name) + i + 1)
                            last = nc.vector.tensor_tensor(dst[:, 2 * i:2 * i + 2, :], pairs(pp_banks[i]), base[:, 2 * i:2 * i + 2, :], ALU.add)
                            last.then_inc(t["tok_used"], 1)
                        dve.wait_ge(t["tok_used"], 2 * turn("projected", name))

                    def row_max(u):
                        n = (u + LEAD) % UNITS
                        g, i = n // GU, n % GU
                        dve.wait_ge(t["ring_done"], entry[("scores", u)])
                        nc.vector.tensor_reduce(negmax[:, g, i // TT, i % TT:i % TT + 1], bank(("scores", u)), axis=AX.X,
                                                op=ALU.max, negate=True).then_inc(t["ring_used"], 1)

                    def split_max(u):
                        g, done = complete[u], placed_to[u]
                        tb = bank(("maxima", u))
                        dve.wait_ge(t["ring_done"], entry[("maxima", u)])
                        nc.vector.tensor_copy(nm_hi[0:HG * TT, g, :], tb[0:HG * TT, 0:P]).then_inc(t["nm_ready"], 1)
                        dve.wait_ge(t["nm_ready"], 2 * done - 1)
                        nc.vector.tensor_tensor(nm_lo[0:HG * TT, g, :], tb[0:HG * TT, 0:P], nm_hi[0:HG * TT, g, :],
                                                ALU.subtract).then_inc(t["nm_ready"], 1)
                        dve.wait_ge(t["nm_ready"], 2 * done)
                        dve.sem_inc(t["ring_used"], 1)

                    def normalise(g, u):
                        dve.wait_ge(t["ring_done"], entry[("outputs", u)])
                        view = bank(("outputs", u)).rearrange("p (q h e) -> p q h e", q=TT, h=HG)
                        link(nc.vector.reciprocal(rden[:, :, :], view[:, :, :, DH]))
                        for q in range(TT):
                            last = nc.vector.tensor_tensor(
                                o_tok[:, q, g * HG * DH:(g + 1) * HG * DH].rearrange("p (h e) -> p h e", h=HG),
                                view[:, q, :, 0:DH],
                                rden[:, q, :].rearrange("p (h e) -> p h e", e=1).broadcast_to([P, HG, DH]), ALU.mult)
                        last.then_inc(t["ring_used"], 1)

                    def epilogue_step(u):
                        if u == 7:
                            add_projected(y, "wo", other["hb"])
                            dve.sem_inc(t["taken"], 1)
                        if u == 8:
                            norm_stats(y)
                        if u == 11:
                            norm_apply(yn, y, "norm_y")
                            link(nc.vector.tensor_tensor(yn[:, :, :], yn[:, :, :], bc(consts["gamma"]), ALU.mult))
                        if u == 13:
                            nc.vector.tensor_tensor(y[:, :, :], yn[:, :, :], other["x1b"][:, :, :], ALU.add).then_inc(t["taken"], 1)
                            dve.wait_ge(t["taken"], 2)
                        if u == 14:
                            norm_stats(y)
                        if u == 21:
                            norm_apply(yn, y, "norm_x2")
                            dve.sem_inc(t["norm_ready"], 1)
                        if u == 28:
                            dve.wait_ge(t["out_base_ready"], 1)
                            add_projected(out, "mix_last", out)
                            dve.sem_inc(t["out_ready"], 1)

                    def prologue_step(u):
                        for i, (first, second, third) in enumerate(((17, 18, 19), (22, 23, 24))):
                            sl = slice(DC * i, DC * i + DC)
                            if u == first:
                                dve.wait_ge(t["hi_ready"], i + 1)
                                link(nc.vector.tensor_tensor(res[:, sl, :], qk_f[:, sl, :], parts[0][:, sl, :], ALU.subtract))
                            if u == second:
                                nc.vector.tensor_copy(parts[1][:, sl, :], res[:, sl, :]).then_inc(t["mid_ready"], 1)
                            if u == third:
                                dve.wait_ge(t["mid_ready"], i + 1)
                                nc.vector.tensor_tensor(parts[2][:, sl, :], res[:, sl, :], parts[1][:, sl, :],
                                                        ALU.subtract).then_inc(t["lo_ready"], 1)
                        if u == 16:
                            bv3 = consts["bv"][:, :].rearrange("p (h e) -> p h e", h=H)
                            for q in range(TT):
                                dve.wait_ge(t["tok_done"], 2 * before("projected", "v") + q // 2 + 1)
                                last = nc.vector.tensor_tensor(other["v"][:, q, :, 0:DH],
                                                               pp[:, q // 2, (q % 2) * D:(q % 2 + 1) * D].rearrange("p (h e) -> p h e", h=H),
                                                               bv3, ALU.add)
                                if q % 2:
                                    last.then_inc(t["tok_used"], 1)

                    def ahead_step(u):
                        if u == 26:
                            dve.wait_ge(t["x_loaded"], 16)
                            norm_stats(x0)
                        if u == 30:
                            norm_apply(xn, x0, "norm_x0")
                            dve.sem_inc(t["norm_ready"], 1)
                        if u == 37:
                            dve.wait_ge(t["x0b_ready"], 1)
                            if prologue:
                                dve.wait_ge(t["renewed"], 2)
                            add_projected(x1, "mix_ahead", x0b)
                        if u == 39:
                            norm_stats(x1)
                        if u == 42:
                            if prologue:
                                dve.wait_ge(t["tr_done"], DC * turn("transposed", "h"))
                            norm_apply(h, x1, "norm_x1")
                            nc.vector.tensor_tensor(h[:, :, :], h[:, :, :], pos[:, :, :], ALU.add).then_inc(t["h_ready"], 1)

                    if epilogue:
                        normalise(NG - 1, -1)
                    for u in range(UNITS):
                        if has_score(u):
                            row_max(u)
                        if u in complete:
                            split_max(u)
                        if u in turned:
                            if epilogue:
                                dve.wait_ge(t["tr_done"], DC)
                            normalise(turned[u], u)
                        if epilogue:
                            epilogue_step(u)
                        if prologue:
                            prologue_step(u)
                        if ahead:
                            ahead_step(u)

                @block.tensor
                def _(pe):
                    def ring_free(e):
                        if entry[e] > NRING:
                            pe.wait_ge(t["ring_used"], entry[e] - NRING)

                    def score(u):
                        source = cur if u + LEAD < UNITS else other
                        n = (u + LEAD) % UNITS
                        hh, q = n // TT, n % TT
                        if n == 0:
                            pe.wait_ge(t["stacked"], 16 * 2 * NPIECE)
                        ring_free(("scores", u))
                        nc.tensor.matmul(bank(("scores", u)), source["q"][0:96, hh, q * P:(q + 1) * P], source["k"][0:96, hh, :],
                                         start=True, stop=True).then_inc(t["ring_done"], 1)

                    def transpose_max(u):
                        g = complete[u]
                        pe.wait_ge(t["ring_used"], entry[("scores", u - 1)])
                        ring_free(("maxima", u))
                        nc.tensor.transpose(bank(("maxima", u))[0:HG * TT, 0:P], negmax[:, g, :, :].rearrange("p h q -> p (h q)"),
                                            ident[:, :]).then_inc(t["ring_done"], 1)

                    def transpose_out(g, u):
                        if u >= 0:
                            pe.wait_ge(t["ot_ready"], g + 1)
                        ring_free(("outputs", u))
                        for q in range(TT):
                            last = nc.tensor.transpose(bank(("outputs", u))[:, q * P:(q + 1) * P], o_t[:, g % 2, q * P:(q + 1) * P], ident[:, :])
                        last.then_inc(t["ring_done"], 1)

                    def scores_t(u):
                        if u % GU == 0 and u:
                            pe.wait_ge(nm_placed[u // GU], 32)
                        if u >= 2:
                            pe.wait_ge(t["probs_ready"], u - 1)
                        hh, kb = u // TT, u % TT
                        nc.tensor.matmul(st[:, u % 2, :], cur["k"][0:98, hh, kb * P:(kb + 1) * P], cur["q"][0:98, hh, :],
                                         start=True, stop=True).then_inc(t["st_done"], 1)

                    def weighted_values(u):
                        hh, kb = u // TT, u % TT
                        hg = hh % HG
                        pe.wait_ge(t["probs_ready"], u + 1)
                        if u and u % GU == 0:
                            pe.wait_ge(t["ot_ready"], u // GU)
                        nc.tensor.matmul(ob[32 * hg:32 * hg + 32, :], cur["v"][:, kb, hh, :], probs[:, u % NPR, :],
                                         start=(kb == 0), stop=(kb == TT - 1)).then_inc(t["pv_done"], 1)

                    def transpose_tokens(src, name):
                        if projected_before[name]:
                            pe.wait_ge(t["tok_used"], 2 * projected_before[name])
                        pe_transpose_tokens(nc, pp_banks, src, ident, t["tr_done"])

                    def project(weights, name):
                        pe.wait_ge(t["xt_ready"], DC * turn("transposed", name))
                        pe_project_tokens(nc, pp_banks, x_t, weights, DC, t["tok_done"])

                    def epilogue_step(u):
                        if u == 4:
                            pe.wait_ge(t["ring_used"], entry[("outputs", -1)])
                            transpose_tokens(o_tok, "o")
                        if u == 6:
                            project(wo, "o")
                        if u == 24:
                            pe.wait_ge(t["norm_ready"], 1)
                            transpose_tokens(yn, "x2")
                        if u == 26:
                            project(mix, "x2")

                    def prologue_step(u):
                        if u == 8:
                            transpose_tokens(h, "h")
                        if u in (10, 11, 12, 13):
                            i = u - 10
                            pe.wait_ge(t["xt_ready"], DC * turn("transposed", "h"))
                            if i >= 2:
                                pe.wait_ge(t["qk_in"], i - 1)
                            wgt = wq if i < DC else wk
                            for c in range(DC):
                                last = nc.tensor.matmul(pp_banks[i % 2], wgt[:, c, (i % DC) * P:(i % DC + 1) * P], x_t[:, c, :],
                                                        start=(c == 0), stop=(c == DC - 1))
                            last.then_inc(t["qk_done"], 1)
                        if u == 15:
                            pe.wait_ge(t["qk_in"], 2 * DC)
                            project(wv, "h")

                    def ahead_step(u):
                        if u == 33:
                            pe.wait_ge(t["norm_ready"], 1 + epilogue)
                            transpose_tokens(xn, "x0")
                        if u == 35:
                            project(mix, "x0")

                    if core:
                        scores_t(0)
                        scores_t(1)
                    if epilogue:
                        transpose_out(NG - 1, -1)
                    for u in range(UNITS):
                        if core and u + 2 < UNITS:
                            scores_t(u + 2)
                        if has_score(u):
                            score(u)
                        if u in complete:
                            transpose_max(u)
                        if u in turned:
                            transpose_out(turned[u], u)
                        if epilogue:
                            epilogue_step(u)
                        if prologue:
                            prologue_step(u)
                        if ahead:
                            ahead_step(u)
                        if core:
                            weighted_values(u)

            end_turn(nc, t)

        even, odd = rows
        phase(None, None, core=False, prologue=False, ahead_row=0)
        phase(odd, even, core=False, ahead_row=S)
        phase(even, odd, ahead_row=2 * S)
        with nc.Fori(0, (NB - 4) // 2) as r:
            phase(odd, even, ahead_row=r * (2 * S) + 3 * S, last_row=r * (2 * S))
            phase(even, odd, ahead_row=r * (2 * S) + 4 * S, last_row=r * (2 * S) + S)
        phase(odd, even, ahead_row=(NB - 1) * S, last_row=(NB - 4) * S)
        phase(even, odd, last_row=(NB - 3) * S)
        phase(odd, even, prologue=False, last_row=(NB - 2) * S)
        phase(even, odd, core=False, prologue=False, last_row=(NB - 1) * S)


def mamba_stage(nc, x_d, x_out_d, w, pairs_d, weight, tag="mamba"):
    with ExitStack() as ctx:
        sb = lambda n, s, t: ctx.enter_context(nc.sbuf_tensor(f"{tag}_{n}", s, t))
        pb = lambda n, s: ctx.enter_context(nc.psum_tensor(f"{tag}_{n}", s, F32))
        ident = sb("ident", [P, P], F32)
        w_in, w_dt = sb("w_in", [P, DC, 2 * DI], F32), sb("w_dt", [P, IC, DI], F32)
        w_out, w_x = sb("w_out", [P, IC, D], F32), sb("w_x", [P, IC, 96], F32)
        ln_g, ln_b = sb("ln_g", [P, D], F32), sb("ln_b", [P, D], F32)
        conv_w, a_neg = sb("conv_w", [P, IC, KC], F32), sb("a_neg", [P, IC, NS], F32)
        cols = {n: sb(n, [P, IC], F32) for n in ("conv_b", "b_dt", "skip")}
        pick = sb("pick", [96, 2 * NS, P], BF16)
        ln = ln_buffers(sb)
        now_weight = sb("now_weight", [P, 2, TT], F32)
        x_in, xm, xn, out = [sb(n, [P, TT, D], F32) for n in ("x_in", "xm", "xn", "out")]
        expert_rows = [xm, xn]
        x_t = sb("x_t", [P, DC, S], F32)
        xpad = sb("xpad", [P, IC, KC - 1 + S], F32)
        cv = sb("cv", [P, IC, S], F32)
        bc_res = out[0:96, 0:2, :].rearrange("p q d -> p (q d)")
        bc_mid = sb("bc_mid", [96, S], BF16)
        rows = [{"residual": sb(f"residual{k}", [P, TT, D], F32),
                 "xb": sb(f"xb{k}", [P, IC, S], F32),
                 "zs": sb(f"zs{k}", [P, IC, S], F32),
                 "dt": sb(f"dt{k}", [P, IC, S], F32),
                 "dtx": sb(f"dtx{k}", [P, IC, S], F32),
                 "bc": sb(f"bc{k}", [96, S], BF16)} for k in range(2)]
        b_bc = sb("b_bc", [P, 3, S], F32)
        decay, drive = sb("decay", [P, 2, IC, S], F32), sb("drive", [P, 2, IC, S], F32)
        state = sb("state", [P, 3, IC, S], F32)

        ya, bb, cb, pp = pb("ya", [P, IC, S]), pb("bb", [P, S]), pb("cb", [P, S]), pb("pp", [P, 2, S])
        ya_banks, pp_banks = [ya[:, i, :] for i in range(IC)], [pp[:, i, :] for i in range(2)]

        setup = semaphores(nc, ctx, ["m_loaded", "pool_filled", "dve_filled", "act_filled"])
        weights_loaded = ctx.enter_context(nc.semaphore("weights_loaded", num=FIRST_SEMAPHORE + 2 * SOFTWARE))
        weight_loads = [(ident[:, :], w["ident"]), (pick[:, :, :], w["pick"]),
                 (w_in[:, :, :], w["w_in"].rearrange("(c p) n -> p c n", p=P)),
                 (w_dt[:, :, :], w["w_dt"].rearrange("(c p) n -> p c n", p=P)),
                 (w_out[:, :, :], w["w_out"].rearrange("(c p) n -> p c n", p=P)),
                 (w_x[:, :, :], w["w_xproj3"].rearrange("(c p) n -> p c n", p=P))]
        loads = [(ln_g[:, :], w["ln_g"].partition_broadcast(P)), (ln_b[:, :], w["ln_b"].partition_broadcast(P)),
                 (conv_w[:, :, :], w["conv_w"]), (a_neg[:, :, :], w["A_log"])]
        loads += [(cols[n][:, :], w[n]) for n in cols]
        with nc.Block() as block:

            @block.sync
            def _(sp):
                for dst, src in loads:
                    sp.dma_start(dst, src).then_inc(setup["m_loaded"], 16)
                sp.wait_ge(setup["m_loaded"], 16 * len(loads))

            @block.gpsimd
            def _(pool):
                nc.gpsimd.memset(ln["neghalf"][:, :], -0.5).then_inc(setup["pool_filled"], 1)
                nc.gpsimd.memset(xpad[:, :, 0:KC - 1], 0.0).then_inc(setup["pool_filled"], 1)
                nc.gpsimd.memset(decay[:, :, :, 0:1], 0.0).then_inc(setup["pool_filled"], 1)

            @block.scalar
            def _(act):
                act.wait_ge(setup["m_loaded"], 16 * len(loads))
                nc.scalar.activation(a_neg[:, :, :], a_neg[:, :, :], ACT.Exp).then_inc(setup["act_filled"], 1)

            @block.vector
            def _(dve):
                dve.wait_ge(setup["act_filled"], 1)
                nc.vector.tensor_scalar(a_neg[:, :, :], a_neg[:, :, :], -1.0, None, ALU.mult).then_inc(setup["dve_filled"], 1)

        end_turn(nc, setup)

        t = semaphores(nc, ctx, ["x_loaded", "x_stored", "weights_ready", "dve_step", "act_step", "var_ready", "rstd_ready", "norm_ready", "sum_ready",
                           "tr_done", "xt_ready", "in_done", "in_used", "conv_ready", "xb_ready", "xd_done", "bc_ready",
                           "dt_done", "u_ready", "dt_ready", "ln_ready", "dtx_ready", "b_done", "c_done", "b_ready",
                           "decay_ready", "drive_ready", "scan_done", "read_ready", "sum_done", "ya_free", "y_ready", "tok_done",
                           "out_ready"], after=setup)

        def row(r):
            return r[:, :].rearrange("p (a d) -> p a d", a=1).broadcast_to([P, TT, D])

        def over_blocks(one):
            return one.rearrange("p (a s) -> p a s", a=1).broadcast_to([P, IC, S])

        def flat(x):
            return x.rearrange("p c s -> p (c s)")

        def phase(cur, other, core=True, prologue=True, ahead_row=None, last_row=None, first=False):
            ahead, epilogue = ahead_row is not None, last_row is not None
            end = NS + 1 if prologue else NS

            def made(n):
                return n if core else 1

            with nc.Block() as block:

                @block.sync
                def _(sp):
                    if ahead:
                        if prologue:
                            sp.wait_ge(t["sum_ready"], 1)
                        sp.dma_start(x_in[:, :, :], token_major(x_d[bass.ds(ahead_row * S, S), :])).then_inc(t["x_loaded"], 16)
                        if prologue:
                            sp.wait_ge(t["tr_done"], DC)
                        for k in range(2):
                            rows_k = pairs_d[bass.ds(ahead_row * (2 * S), 2 * S), :].rearrange("(q p k) d -> k p q d", p=P, k=2)[k]
                            sp.dma_start(expert_rows[k][:, :, :], rows_k).then_inc(t["x_loaded"], 16)
                    if not core and not prologue and ahead:
                        for dst, src in weight_loads:
                            sp.dma_start(dst, src).then_inc(weights_loaded, 16)
                    if epilogue:
                        sp.wait_ge(t["out_ready"], 1)
                        sp.dma_start(token_major(x_out_d[bass.ds(last_row * S, S), :]), out[:, :, :]).then_inc(t["x_stored"], 16)
                        sp.wait_ge(t["x_stored"], 16)
                    if ahead:
                        sp.wait_ge(t["x_loaded"], 48)

                @block.gpsimd
                def _(pool):
                    def make_drive(n):
                        source = cur if n < NS else other
                        if n == NS:
                            pool.wait_ge(t["dtx_ready"], 1)
                        pool.wait_ge(t["b_ready"], made(n))
                        if core and n >= 2:
                            pool.wait_ge(t["scan_done"], n - 1)
                        nc.gpsimd.tensor_tensor(drive[:, n % 2, :, :], source["dtx"][:, :, :], over_blocks(b_bc[:, n % 3, :]),
                                                ALU.mult).then_inc(t["drive_ready"], 1)

                    if ahead:
                        nc.gpsimd.tensor_copy(now_weight[:, :, :], weight[:, :, bass.ds(ahead_row * TT, TT)]).then_inc(t["weights_ready"], 1)
                    for n in range(NS):
                        if core and n >= 1:
                            make_drive(n)
                        if prologue and n == 2:
                            if epilogue:
                                pool.wait_ge(t["out_ready"], 1)
                            nc.gpsimd.tensor_tensor(other["residual"][:, :, :], x_in[:, :, :], xm[:, :, :], ALU.add).then_inc(t["sum_ready"], 1)
                        if ahead and n in (9, 11):
                            pool_rstd(nc, pool, ln, t["var_ready"], t["rstd_ready"], 1 if n == 9 else 2)
                    if prologue:
                        pool.wait_ge(t["dt_ready"], 1)
                        nc.gpsimd.tensor_tensor(flat(other["dtx"][:, :, :]), flat(other["dt"][:, :, :]), flat(other["xb"][:, :, :]),
                                                ALU.mult).then_inc(t["dtx_ready"], 1)
                        make_drive(NS)

                @block.scalar
                def _(act):
                    def prologue_step(n):
                        if n == 0:
                            for c in range(DC):
                                act.wait_ge(t["tr_done"], c + 1)
                                nc.scalar.copy(x_t[:, c, :], pp_banks[c]).then_inc(t["xt_ready"], 1)
                        if n in (4, 5):
                            for i in (2 * (n - 4), 2 * (n - 4) + 1):
                                act.wait_ge(t["in_done"], i + 1)
                                nc.scalar.copy(xpad[:, i, KC - 1:], pp_banks[i % 2]).then_inc(t["in_used"], 1)
                        if n in (6, 7):
                            if epilogue:
                                act.wait_ge(t["y_ready"], 1)
                            for i in (2 * (n - 6), 2 * (n - 6) + 1):
                                act.wait_ge(t["in_done"], IC + i + 1)
                                nc.scalar.activation(other["zs"][:, i, :], pp_banks[i % 2], ACT.Silu).then_inc(t["in_used"], 1)
                        if n == 7:
                            if epilogue:
                                act.wait_ge(t["tok_done"], 2)
                            for i in range(IC):
                                act.wait_ge(t["conv_ready"], i + 1)
                                nc.scalar.activation(other["xb"][:, i, :], cv[:, i, :], ACT.Silu,
                                                     bias=cols["conv_b"][:, i:i + 1]).then_inc(t["xb_ready"], 1)
                        for i in {9: (0,), 10: (1,), 11: (2,), 12: (3,)}.get(n, ()):
                            act.wait_ge(t["dt_done"], i + 1)
                            act.wait_ge(t["xb_ready"], IC)
                            nc.scalar.activation(other["dt"][:, i, :], pp_banks[(1 + i) % 2], ACT.Relu, bias=cols["b_dt"][:, i:i + 1])
                            nc.scalar.activation(other["dtx"][:, i, :], pp_banks[(1 + i) % 2], ACT.Abs,
                                                 bias=cols["b_dt"][:, i:i + 1]).then_inc(t["u_ready"], 1)
                        if n == 12:
                            act.wait_ge(t["u_ready"], IC)
                            nc.scalar.activation(other["dtx"][:, :, :], other["dtx"][:, :, :], ACT.Exp, scale=-1.0).then_inc(t["act_step"], 1)
                        if n == 13:
                            act.wait_ge(t["act_step"], 1)
                            nc.scalar.activation(other["dtx"][:, :, :], other["dtx"][:, :, :], ACT.Ln, bias=1.0).then_inc(t["ln_ready"], 1)

                    def make_decay(n):
                        source = cur if n < NS else other
                        act.wait_ge(t["b_done"], made(n))
                        if core and n >= 4:
                            act.wait_ge(t["drive_ready"], n - 3)
                        nc.scalar.copy(b_bc[:, n % 3, :], bb[:, :]).then_inc(t["b_ready"], 1)
                        if n == NS:
                            act.wait_ge(t["dt_ready"], 1)
                        if core and n >= 2:
                            act.wait_ge(t["scan_done"], n - 1)
                        for i in range(IC):
                            last = nc.scalar.activation(decay[:, n % 2, i, 1:], source["dt"][:, i, 1:], ACT.Exp,
                                                        scale=a_neg[:, i, n % NS:n % NS + 1])
                        last.then_inc(t["decay_ready"], 1)

                    for n in range(NS):
                        if core and n >= 1:
                            make_decay(n)
                        if prologue:
                            prologue_step(n)
                    if prologue:
                        make_decay(NS)

                @block.vector
                def _(dve):
                    link = linker(dve, t["dve_step"])

                    def scan(n):
                        if n >= 1:
                            dve.wait_ge(t["decay_ready"], n)
                            dve.wait_ge(t["drive_ready"], n)
                        if n >= 3:
                            dve.wait_ge(t["sum_done"], n - 2)
                        nc.vector.tensor_tensor_scan(flat(state[:, n % 3, :, :]), flat(decay[:, n % 2, :, :]),
                                                     flat(drive[:, n % 2, :, :]), 0.0, ALU.mult, ALU.add).then_inc(t["scan_done"], 1)

                    def read_out(n):
                        dve.wait_ge(t["scan_done"], n + 1)
                        dve.wait_ge(t["c_done"], n + 1)
                        nc.vector.tensor_tensor(state[:, n % 3, :, :], state[:, n % 3, :, :], over_blocks(cb[:, :]),
                                                ALU.mult).then_inc(t["read_ready"], 1)

                    def norm_stats(src, turn):
                        for q in range(TT):
                            last = nc.vector.bn_stats(ln["stats"][:, q, :], src[:, q, :])
                        link(last)
                        for q in range(TT):
                            last = nc.vector.bn_aggr(ln["mv"][:, q, :], ln["stats"][:, q, :])
                        link(last)
                        if turn == 2:
                            dve.wait_ge(t["rstd_ready"], 1)
                        nc.vector.tensor_scalar(ln["vareps"][:, :], ln["mv"][:, :, 1], EPS, None, ALU.add).then_inc(t["var_ready"], 1)

                    def norm_apply(dst, src, turn):
                        dve.wait_ge(t["rstd_ready"], turn)
                        for q in range(TT):
                            last = nc.vector.tensor_scalar(dst[:, q, :], src[:, q, :], ln["mv"][:, q, 0:1],
                                                           ln["rstd"][:, q:q + 1], ALU.subtract, ALU.mult)
                        return last

                    def convolve(i):
                        dve.wait_ge(t["in_used"], i + 1)
                        link(nc.vector.tensor_scalar(cv[:, i, :], xpad[:, i, 0:S], conv_w[:, i, 0:1], None, ALU.mult))
                        for k in range(1, KC):
                            last = nc.vector.scalar_tensor_tensor(cv[:, i, :], xpad[:, i, k:k + S], conv_w[:, i, k:k + 1],
                                                                  cv[:, i, :], ALU.mult, ALU.add)
                            link(last) if k < KC - 1 else last.then_inc(t["conv_ready"], 1)

                    def ahead_step(n):
                        if n == 7:
                            dve.wait_ge(t["x_loaded"], 48)
                            dve.wait_ge(t["weights_ready"], 1)
                            for k in range(2):
                                for q in range(TT):
                                    last = nc.vector.scalar_tensor_tensor(x_in[:, q, :], expert_rows[k][:, q, :], now_weight[:, k, q:q + 1],
                                                                          x_in[:, q, :], ALU.mult, ALU.add)
                                link(last)
                            norm_stats(x_in, 1)
                        if n == 9:
                            norm_apply(xm, x_in, 1).then_inc(t["norm_ready"], 1)
                            dve.wait_ge(t["norm_ready"], 1)
                            norm_stats(xm, 2)
                        if n == 11:
                            if prologue:
                                dve.wait_ge(t["tr_done"], DC)
                            link(norm_apply(xn, xm, 2))
                            link(nc.vector.tensor_tensor(xn[:, :, :], xn[:, :, :], row(ln_g), ALU.mult))
                            nc.vector.tensor_tensor(xn[:, :, :], xn[:, :, :], row(ln_b), ALU.add)

                    def prologue_step(n):
                        if n in (3, 4):
                            convolve(2 * (n - 3))
                            convolve(2 * (n - 3) + 1)
                        if n == 7:
                            if epilogue:
                                dve.wait_ge(t["x_stored"], 16)
                            dve.wait_ge(t["xd_done"], 1)
                            high = other["bc"]
                            link(nc.vector.tensor_copy(high[:, :], pp[0:96, 0, :]))
                            link(nc.vector.tensor_tensor(bc_res, pp[0:96, 0, :], high[:, :], ALU.subtract))
                            nc.vector.tensor_copy(bc_mid[:, :], bc_res)
                            link(nc.vector.tensor_copy(high[32:64, :], bc_res[32:64, :]))
                            nc.vector.tensor_tensor(high[64:96, :], bc_res[64:96, :], bc_mid[64:96, :],
                                                    ALU.subtract).then_inc(t["bc_ready"], 1)
                        if n == 13:
                            dt, dtx = other["dt"], other["dtx"]
                            dve.wait_ge(t["ln_ready"], 1)
                            nc.vector.tensor_tensor(flat(dt[:, :, :]), flat(dt[:, :, :]), flat(dtx[:, :, :]), ALU.add).then_inc(t["dt_ready"], 1)

                    if epilogue:
                        yv = other["xb"]
                        for i in range(IC):
                            last = nc.vector.scalar_tensor_tensor(yv[:, i, :], other["xb"][:, i, :], cols["skip"][:, i:i + 1],
                                                                  ya_banks[i], ALU.mult, ALU.add)
                        last.then_inc(t["ya_free"], 1)
                        dve.wait_ge(t["ya_free"], 1)
                        nc.vector.tensor_tensor(flat(yv[:, :, :]), flat(yv[:, :, :]), flat(other["zs"][:, :, :]),
                                                ALU.mult).then_inc(t["y_ready"], 1)
                    if core:
                        scan(0)
                    for n in range(NS):
                        if core:
                            if n + 1 < NS:
                                scan(n + 1)
                            read_out(n)
                        if epilogue and n == 0:
                            for i in range(2):
                                dve.wait_ge(t["tok_done"], i + 1)
                                last = nc.vector.tensor_tensor(out[:, 2 * i:2 * i + 2, :], pp_banks[i].rearrange("p (a d) -> p a d", a=2),
                                                               other["residual"][:, 2 * i:2 * i + 2, :], ALU.add)
                            last.then_inc(t["out_ready"], 1)
                        if prologue:
                            prologue_step(n)
                        if ahead:
                            ahead_step(n)

                @block.tensor
                def _(pe):
                    if first:
                        pe.wait_ge(weights_loaded, 16 * len(weight_loads))

                    def spread_b(n):
                        if n == NS:
                            pe.wait_ge(t["bc_ready"], 1)
                        if core and n >= 2:
                            pe.wait_ge(t["b_ready"], n - 1)
                        source = cur if n < NS else other
                        nc.tensor.matmul(bb[:, :], pick[:, n % NS, :], source["bc"][:, :], start=True, stop=True).then_inc(t["b_done"], 1)

                    def spread_c(n):
                        if n >= 1:
                            pe.wait_ge(t["read_ready"], n)
                        nc.tensor.matmul(cb[:, :], pick[:, NS + n, :], cur["bc"][:, :], start=True, stop=True).then_inc(t["c_done"], 1)

                    def prologue_step(n):
                        if n in (1, 2, 3, 4):
                            pe.wait_ge(t["xt_ready"], DC)
                            if epilogue:
                                pe.wait_ge(t["out_ready"], 1)
                            for i in (2 * (n - 1), 2 * (n - 1) + 1):
                                if i >= 2:
                                    pe.wait_ge(t["in_used"], i - 1)
                                for c in range(DC):
                                    last = nc.tensor.matmul(pp_banks[i % 2], w_in[:, c, i * P:(i + 1) * P], x_t[:, c, :],
                                                            start=(c == 0), stop=(c == DC - 1))
                                last.then_inc(t["in_done"], 1)
                        if n == 6:
                            pe.wait_ge(t["xb_ready"], IC)
                            pe.wait_ge(t["in_used"], 2 * IC)
                            for k in range(IC):
                                last = nc.tensor.matmul(pp[0:96, 0, :], w_x[:, k, :], other["xb"][:, k, :], start=(k == 0), stop=(k == IC - 1))
                            last.then_inc(t["xd_done"], 1)
                        for i in {7: (0,), 8: (1,), 9: (2,), 10: (3,)}.get(n, ()):
                            if i == 1:
                                pe.wait_ge(t["bc_ready"], 1)
                            if i >= 2:
                                pe.wait_ge(t["u_ready"], i - 1)
                            for k in range(IC):
                                last = nc.tensor.matmul(pp_banks[(1 + i) % 2], w_dt[:, k, i * P:(i + 1) * P], other["xb"][:, k, :],
                                                        start=(k == 0), stop=(k == IC - 1))
                            last.then_inc(t["dt_done"], 1)

                    if prologue:
                        pe_transpose_tokens(nc, pp_banks, xn, ident, t["tr_done"])
                    if core:
                        spread_b(1)
                        spread_c(0)
                        spread_b(2)
                    if epilogue:
                        pe.wait_ge(t["y_ready"], 1)
                        if prologue:
                            pe.wait_ge(t["xt_ready"], DC)
                        pe_project_tokens(nc, pp_banks, other["xb"], w_out, IC, t["tok_done"])
                    for n in range(NS):
                        if core:
                            if n + 3 < end:
                                spread_b(n + 3)
                            pe.wait_ge(t["read_ready"], n + 1)
                            if n + 1 < NS:
                                spread_c(n + 1)
                        if prologue:
                            prologue_step(n)
                        if core:
                            for i in range(IC):
                                last = nc.tensor.matmul(ya_banks[i], ident[:, :], state[:, n % 3, i, :], start=(n == 0), stop=(n == NS - 1))
                            last.then_inc(t["sum_done"], 1)
                    if prologue and not core:
                        spread_b(NS)

            end_turn(nc, t)

        even, odd = rows
        phase(None, None, core=False, prologue=False, ahead_row=0)
        phase(odd, even, core=False, ahead_row=1, first=True)
        phase(even, odd, ahead_row=2)
        with nc.Fori(0, (NB - 4) // 2) as r:
            phase(odd, even, ahead_row=r * 2 + 3, last_row=r * 2)
            phase(even, odd, ahead_row=r * 2 + 4, last_row=r * 2 + 1)
        phase(odd, even, ahead_row=NB - 1, last_row=NB - 4)
        phase(even, odd, last_row=NB - 3)
        phase(odd, even, prologue=False, last_row=NB - 2)
        phase(even, odd, core=False, prologue=False, last_row=NB - 1)


def moe_stage(nc, x_d, x_out_d, w, normed_d, pairs_d, weight, use=0, tag="moe"):
    with ExitStack() as ctx:
        big = semaphores(nc, ctx, ["weights_loaded", "rows_stored"])
        soft = software_semaphores(nc, ctx, use)
        with ExitStack() as held:
            sb = lambda n, s, t: held.enter_context(nc.sbuf_tensor(f"{tag}_{n}", s, t))
            ident = sb("ident", [P, P], F32)
            w0, w1, w2 = sb("w0", [P, DC, E * HID], F32), sb("w1", [P, DC, E * HID], F32), sb("w2", [P, HC, E * D], F32)
            b0, b1, b2 = sb("b0", [P, E * HID], F32), sb("b1", [P, E * HID], F32), sb("b2", [P, E * D], F32)
            weights = (w0, w1, w2, b0, b1, b2)
            expert_of, token_of, pair_of = [sb(n, [P, NTILE], I32) for n in ("expert_of", "token_of", "pair_of")]
            with ExitStack() as part:
                moe_route(nc, part, x_d, w, normed_d, tag, ident, weights, weight, expert_of, token_of, pair_of, big)
            with ExitStack() as part:
                moe_experts(nc, part, normed_d, pairs_d, tag, ident, weights, expert_of, token_of, pair_of, big, soft)
        if x_out_d is not None:
            moe_combine(nc, ctx, x_d, x_out_d, pairs_d, tag, weight, big)
        end_turn(nc, big)


def moe_route(nc, ctx, x_d, w, normed_d, tag, ident, weights, weight, expert_of, token_of, pair_of, big):
    sb = lambda n, s, t: ctx.enter_context(nc.sbuf_tensor(f"{tag}_{n}", s, t))
    pb = lambda n, s: ctx.enter_context(nc.psum_tensor(f"{tag}_{n}", s, F32))
    GT = 8
    HALF = NT // 2
    CH = 8
    gate_w, gate_b = sb("gate_w", [P, DC, E], F32), sb("gate_b", [P, E], F32)
    lower = sb("lower", [P, E, E], F32)
    before = sb("before", [P, P], F32)
    ones = sb("ones", [P, P], F32)
    keep = sb("keep", [P, E, NT], F32)
    step = sb("step", [P, NT], F32)
    number = sb("number", [P, NTILE], F32)
    lane = sb("lane", [P, P], F32)
    code = sb("code", [P, 2, NT], F32)
    behind = sb("behind", [P, NTILE], F32)
    coded, spare = sb("coded", [P, NTILE], F32), sb("spare", [P, NTILE], F32)
    slot = sb("slot", [P, 2, NT], I32)
    in_tile = sb("in_tile", [P, 2, CH, NTILE], F32)
    slot_row, slot_tile = sb("slot_row", [P, 2, NT], F32), sb("slot_tile", [P, 2, NT], F32)
    ln = ln_buffers(sb, GT)
    xn = sb("xn", [P, NT, D], F32)
    x_t = sb("x_t", [P, 2, DC, S], F32)
    in_row = [x_t[:, i, :, :].rearrange("p c (j n) -> p (c j) n", n=P) for i in range(2)]
    logit, gates, rank = [sb(n, [P, NT, E], F32) for n in ("logit", "gates", "rank")]
    ahead, tie = sb("ahead", [P, NT, E, E], BF16), sb("tie", [P, NT, E, E], BF16)
    is_first, is_second, chosen = [sb(n, [P, NT, E], F32) for n in ("is_first", "is_second", "chosen")]
    top, den = sb("top", [P, NT], F32), sb("den", [P, NT], F32)
    per_tile, running, base = [sb(n, [P, E, NT], F32) for n in ("per_tile", "running", "base")]
    n_tiles, tiles_to, first_tile = [sb(n, [P, E], F32) for n in ("n_tiles", "tiles_to", "first_tile")]
    place, picked = sb("place", [P, NT, E], F32), sb("picked", [P, NT, E], F32)
    slot_f = sb("slot_f", [P, 2, NT], F32)
    slot_tile_i = sb("slot_tile_i", [P, 2, NT], I32)
    ended = ahead[:, :, :, :].rearrange("p q e j -> p (q e j)")[:, 0:NTILE * E].rearrange("p (j e) -> p j e", e=E)
    expert_f = sb("expert_f", [P, NTILE], F32)

    tp, lp = pb("tp", [P, 4, S]), pb("lp", [P, 2, S])
    cum, tot = pb("cum", [P, S]), pb("tot", [P, S])

    t = semaphores(nc, ctx, [*(f"x_loaded{g}" for g in range(NT // GT)), "r_loaded", "pool_filled", "dve_step", "var_ready", "rstd_ready", "norm_ready",
                             "tr_done", "xt_ready", "logit_done", "logit_ready", "shift_ready", "exp_ready", "chosen_ready",
                             "count_done", "tile_ready", "chunk_done", "table_ready"],
                   after=big)
    x_loaded = [t[f"x_loaded{g}"] for g in range(NT // GT)]
    small = [(gate_w[:, :, :], w["gate_w"]), (gate_b[:, :], w["gate_b"].partition_broadcast(P)),
             (lower[:, :, :], w["lower"].partition_broadcast(P)), (before[:, :], w["before"]), (ident[:, :], w["ident"]),
             (keep[:, :, :], w["keep"].partition_broadcast(P)), (step[:, :], w["step"].partition_broadcast(P)),
             (number[:, :], w["number"].partition_broadcast(P)), (lane[:, :], w["lane"].partition_broadcast(P)),
             (code[:, :, :], w["code"]), (behind[:, :], w["behind"])]
    w0, w1, w2, b0, b1, b2 = weights
    large = [(w0[:, :, :], w["w0"]), (w1[:, :, :], w["w1"]), (w2[:, :, :], w["w2"]),
             (b0[:, :], w["b0"].partition_broadcast(P)), (b1[:, :], w["b1"].partition_broadcast(P)),
             (b2[:, :], w["b2"].partition_broadcast(P))]

    def tiles_first(x):
        return x.rearrange("p e q -> p q e")

    def per_token(x):
        return x.rearrange("p (q a) -> p q a", a=1).broadcast_to([P, NT, E])

    CHUNKS = 2 * NT // CH

    def chunk_of(x, c):
        return x[:, :, :].rearrange("p k q -> p (k q)")[:, c * CH:(c + 1) * CH].rearrange("p (j a) -> p j a", a=1)

    with nc.Block() as block:

        @block.sync
        def _(sp):
            for g in range(NT // GT):
                sp.dma_start(xn[:, g * GT:(g + 1) * GT, :], token_major(x_d[g * GT * P:(g + 1) * GT * P, :])).then_inc(x_loaded[g], 16)
                if g == 0:
                    for dst, src in small:
                        sp.dma_start(dst, src).then_inc(t["r_loaded"], 16)
            for g in range(NT // GT):
                sp.wait_ge(t["norm_ready"], g + 1)
                sp.dma_start(token_major(normed_d[g * GT * P:(g + 1) * GT * P, :]), xn[:, g * GT:(g + 1) * GT, :]).then_inc(big["rows_stored"], 16)
            for dst, src in large:
                sp.dma_start(dst, src).then_inc(big["weights_loaded"], 16)
            sp.wait_ge(big["weights_loaded"], 16 * len(large))
            sp.wait_ge(big["rows_stored"], 16 * (NT // GT))

        @block.gpsimd
        def _(pool):
            nc.gpsimd.memset(ln["neghalf"][:, :], -0.5).then_inc(t["pool_filled"], 1)
            nc.gpsimd.memset(ones[:, :], 1.0).then_inc(t["pool_filled"], 1)
            pool.wait_ge(t["pool_filled"], 2)
            for g in range(NT // GT):
                pool_rstd(nc, pool, ln, t["var_ready"], t["rstd_ready"], g + 1)

        @block.scalar
        def _(act):
            for g in range(NT // TT):
                for c in range(DC):
                    act.wait_ge(t["tr_done"], DC * g + c + 1)
                    if g >= 2:
                        act.wait_ge(t["logit_done"], g - 1)
                    nc.scalar.copy(x_t[:, g % 2, c, :], tp[:, DC * (g % 2) + c, :]).then_inc(t["xt_ready"], 1)
            act.wait_ge(t["shift_ready"], 1)
            nc.scalar.activation(gates[:, :, :], logit[:, :, :], ACT.Exp).then_inc(t["exp_ready"], 1)

        @block.vector
        def _(dve):
            link = linker(dve, t["dve_step"])
            for g in range(NT // GT):
                part = xn[:, g * GT:(g + 1) * GT, :]
                dve.wait_ge(x_loaded[g], 16)
                dve_layernorm(nc, dve, link, part, part, ln, t["var_ready"], t["rstd_ready"], g + 1, GT).then_inc(t["norm_ready"], 1)
                dve.wait_ge(t["norm_ready"], g + 1)
            dve.wait_ge(t["r_loaded"], 16 * len(small))
            for half in range(2):
                dve.wait_ge(t["logit_done"], (half + 1) * NT // TT // 2)
                last = nc.vector.tensor_tensor(logit[:, half * HALF:(half + 1) * HALF, :],
                                               lp[:, half, 0:HALF * E].rearrange("p (q e) -> p q e", e=E),
                                               gate_b[:, :].rearrange("p (a e) -> p a e", a=1).broadcast_to([P, HALF, E]), ALU.add)
            link(last)
            mine = logit[:, :, :].rearrange("p q (e a) -> p q e a", a=1).broadcast_to([P, NT, E, E])
            others = logit[:, :, :].rearrange("p q (a e) -> p q a e", a=1).broadcast_to([P, NT, E, E])
            lowers = lower[:, :, :].rearrange("p (a e) j -> p a e j", a=1).broadcast_to([P, NT, E, E])
            nc.vector.tensor_tensor(ahead[:, :, :, :], others, mine, ALU.is_gt)
            nc.vector.tensor_tensor(tie[:, :, :, :], others, mine, ALU.is_equal)
            link(nc.vector.tensor_reduce(top[:, :], logit[:, :, :], axis=AX.X, op=ALU.max))
            nc.vector.tensor_tensor(logit[:, :, :], logit[:, :, :], per_token(top[:, :]), ALU.subtract).then_inc(t["shift_ready"], 1)
            link(nc.vector.tensor_tensor(tie[:, :, :, :], tie[:, :, :, :], lowers, ALU.mult))
            link(nc.vector.tensor_tensor(ahead[:, :, :, :], ahead[:, :, :, :], tie[:, :, :, :], ALU.add))
            link(nc.vector.tensor_reduce(rank[:, :, :], ahead[:, :, :, :], axis=AX.X, op=ALU.add))
            nc.vector.tensor_scalar(is_first[:, :, :], rank[:, :, :], 0.0, None, ALU.is_equal)
            nc.vector.tensor_scalar(is_second[:, :, :], rank[:, :, :], 1.0, None, ALU.is_equal)
            nc.vector.tensor_scalar(chosen[:, :, :], rank[:, :, :], 2.0, None, ALU.is_lt).then_inc(t["chosen_ready"], 1)
            dve.wait_ge(t["exp_ready"], 1)
            dve.wait_ge(t["chosen_ready"], 1)
            link(nc.vector.tensor_tensor(gates[:, :, :], gates[:, :, :], chosen[:, :, :], ALU.mult))
            link(nc.vector.tensor_reduce(den[:, :], gates[:, :, :], axis=AX.X, op=ALU.add))
            link(nc.vector.reciprocal(den[:, :], den[:, :]))
            link(nc.vector.tensor_scalar(den[:, :], den[:, :], 0.5, None, ALU.mult))
            link(nc.vector.tensor_tensor(gates[:, :, :], gates[:, :, :], per_token(den[:, :]), ALU.mult))
            dve.wait_ge(t["count_done"], 2)
            link(nc.vector.tensor_copy(per_tile[:, :, :], tot[:, 0:NT * E].rearrange("p (q e) -> p e q", e=E)))
            link(nc.vector.tensor_tensor_scan(running[:, :, :].rearrange("p e q -> p (e q)"), keep[:, :, :].rearrange("p e q -> p (e q)"),
                                              per_tile[:, :, :].rearrange("p e q -> p (e q)"), 0.0, ALU.mult, ALU.add))
            count = running[:, :, NT - 1:NT].broadcast_to([P, E, NT])
            steps = step[:, :].rearrange("p (a q) -> p a q", a=1).broadcast_to([P, E, NT])
            link(nc.vector.tensor_tensor(base[:, :, :], count, steps, ALU.is_gt))
            link(nc.vector.tensor_reduce(n_tiles[:, :], base[:, :, :], axis=AX.X, op=ALU.add))
            link(nc.vector.tensor_tensor_scan(tiles_to[:, :], ones[:, 0:E], n_tiles[:, :], 0.0, ALU.mult, ALU.add))
            link(nc.vector.tensor_tensor(first_tile[:, :], tiles_to[:, :], n_tiles[:, :], ALU.subtract))
            link(nc.vector.tensor_tensor(per_tile[:, :, :], running[:, :, :], per_tile[:, :, :], ALU.subtract))
            firsts = first_tile[:, :].rearrange("p (e a) -> p e a", a=1).broadcast_to([P, E, NT])
            link(nc.vector.scalar_tensor_tensor(base[:, :, :], firsts, float(P), per_tile[:, :, :], ALU.mult, ALU.add))
            link(nc.vector.tensor_tensor(place[:, :, :], cum[:, 0:NT * E].rearrange("p (q e) -> p q e", e=E), tiles_first(base[:, :, :]), ALU.add))
            for k, mark in enumerate((is_first, is_second)):
                link(nc.vector.tensor_tensor(picked[:, :, :], mark[:, :, :], place[:, :, :], ALU.mult))
                link(nc.vector.tensor_reduce(slot_f[:, k, :], picked[:, :, :], axis=AX.X, op=ALU.add))
            link(nc.vector.tensor_copy(slot[:, :, :], slot_f[:, :, :]))
            link(nc.vector.tensor_scalar(slot_tile_i[:, :, :], slot[:, :, :], P.bit_length() - 1, None, ALU.arith_shift_right))
            link(nc.vector.tensor_copy(slot_tile[:, :, :], slot_tile_i[:, :, :]))
            link(nc.vector.scalar_tensor_tensor(slot_row[:, :, :], slot_tile[:, :, :], -float(P), slot_f[:, :, :], ALU.mult, ALU.add))
            tiles = number[:, :].rearrange("p (a j) -> p a j", a=1).broadcast_to([P, CH, NTILE])
            for c in range(CHUNKS):
                if c >= 2:
                    dve.wait_ge(t["chunk_done"], c - 1)
                lanes = lane[:, :].rearrange("p (a n) -> p a n", a=1).broadcast_to([P, CH, P])
                nc.vector.tensor_tensor(in_row[c % 2], lanes, chunk_of(slot_row, c).broadcast_to([P, CH, P]), ALU.is_equal)
                link(nc.vector.tensor_tensor(in_tile[:, c % 2, :, :], tiles, chunk_of(slot_tile, c).broadcast_to([P, CH, NTILE]), ALU.is_equal))
                codes = chunk_of(code, c).broadcast_to([P, CH, NTILE])
                nc.vector.tensor_tensor(in_tile[:, c % 2, :, :], in_tile[:, c % 2, :, :], codes, ALU.mult).then_inc(t["tile_ready"], 1)
            for k, mark in enumerate((is_first, is_second)):
                link(nc.vector.tensor_tensor(picked[:, :, :], mark[:, :, :], gates[:, :, :], ALU.mult))
                link(nc.vector.tensor_reduce(weight[:, k, :], picked[:, :, :], axis=AX.X, op=ALU.add))
            ends = tiles_to[:, :].rearrange("p (a e) -> p a e", a=1).broadcast_to([P, NTILE, E])
            numbers = number[:, :].rearrange("p (j a) -> p j a", a=1).broadcast_to([P, NTILE, E])
            link(nc.vector.tensor_tensor(ended, ends, numbers, ALU.is_le))
            link(nc.vector.tensor_reduce(expert_f[:, :], ended, axis=AX.X, op=ALU.add))
            link(nc.vector.tensor_scalar(expert_f[:, :], expert_f[:, :], float(E - 1), None, ALU.min))
            link(nc.vector.tensor_copy(expert_of[:, :], expert_f[:, :]))
            dve.wait_ge(t["chunk_done"], CHUNKS)
            nc.vector.tensor_scalar(spare[:, :], tp[:, 0, 0:NTILE], 0.0, None, ALU.is_equal)
            link(nc.vector.tensor_scalar(coded[:, :], tp[:, 0, 0:NTILE], -1.0, None, ALU.add))
            link(nc.vector.tensor_tensor(spare[:, :], spare[:, :], behind[:, :], ALU.mult))
            link(nc.vector.tensor_tensor(spare[:, :], spare[:, :], coded[:, :], ALU.add))
            nc.vector.tensor_copy(pair_of[:, :], spare[:, :]).then_inc(t["table_ready"], 1)
            link(nc.vector.tensor_scalar(coded[:, :], coded[:, :], 0.0, None, ALU.max))
            link(nc.vector.tensor_copy(token_of[:, :], coded[:, :]))
            nc.vector.tensor_scalar(token_of[:, :], token_of[:, :], 1, None, ALU.arith_shift_right).then_inc(t["table_ready"], 1)

        @block.tensor
        def _(pe):
            pe.wait_ge(t["r_loaded"], 16 * len(small))
            pe.wait_ge(t["pool_filled"], 2)

            def transpose_group(g):
                pe.wait_ge(t["norm_ready"], g * TT // GT + 1)
                if g >= 2:
                    pe.wait_ge(t["xt_ready"], DC * (g - 1))
                pe_transpose_tokens(nc, [tp[:, DC * (g % 2) + c, :] for c in range(DC)], xn[:, g * TT:(g + 1) * TT, :], ident, t["tr_done"])

            transpose_group(0)
            for g in range(NT // TT):
                if g + 1 < NT // TT:
                    transpose_group(g + 1)
                pe.wait_ge(t["xt_ready"], DC * (g + 1))
                for q in range(TT):
                    col = (g * TT + q) % HALF * E
                    for c in range(DC):
                        last = nc.tensor.matmul(lp[:, g * TT // HALF, col:col + E], x_t[:, g % 2, c, q * P:(q + 1) * P], gate_w[:, c, :],
                                                start=(c == 0), stop=(c == DC - 1))
                last.then_inc(t["logit_done"], 1)
            pe.wait_ge(t["chosen_ready"], 1)
            marks = chosen[:, :, :].rearrange("p q e -> p (q e)")
            nc.tensor.matmul(cum[:, 0:NT * E], before[:, :], marks, start=True, stop=True).then_inc(t["count_done"], 1)
            nc.tensor.matmul(tot[:, 0:NT * E], ones[:, :], marks, start=True, stop=True).then_inc(t["count_done"], 1)
            for c in range(CHUNKS):
                pe.wait_ge(t["tile_ready"], c + 1)
                for j in range(CH):
                    last = nc.tensor.matmul(tp[:, 0, 0:NTILE], in_row[c % 2][:, j, :], in_tile[:, c % 2, j, :],
                                            start=(c == 0 and j == 0), stop=(c == CHUNKS - 1 and j == CH - 1))
                last.then_inc(t["chunk_done"], 1)

    end_turn(nc, t)


def moe_experts(nc, ctx, normed_d, pairs_d, tag, ident, weights, expert_of, token_of, pair_of, big, soft):
    sb = lambda n, s, t: ctx.enter_context(nc.sbuf_tensor(f"{tag}_{n}", s, t))
    pb = lambda n, s: ctx.enter_context(nc.psum_tensor(f"{tag}_{n}", s, F32))
    w0, w1, w2, b0, b1, b2 = weights
    NX = 4
    NY = 3
    xs, ys = sb("xs", [P, NX, D], F32), sb("ys", [P, NY, D], F32)
    xs_t = sb("xs_t", [P, 2, DC, P], F32)
    z, up, sil, hid = [sb(n, [P, 2, HID], F32) for n in ("z", "up", "sil", "hid")]
    hid_t = sb("hid_t", [P, 2, HC, P], F32)
    tp = pb("tpx", [P, S])
    h0, h1 = pb("h0", [P, 2, S]), pb("h1", [P, 2, S])
    hp = pb("hpx", [P, 2, S])
    op = pb("opx", [P, S])
    fetch, send = sb("fetch", [P, TILES], I32), sb("send", [P, TILES], I32)
    t = semaphores(nc, ctx, ["fetch_ready", "xs_tr_done", "xs_t_ready", "h1_done", "h0_done",
                             "z_ready", "up_ready", "sil_ready", "hid_ready", "hid_tr_done", "hid_t_ready", "out_done", "ys_ready",
                             ], after=big)
    xs_loaded = [soft[f"xs_loaded{i}"] for i in range(NX)]
    ys_stored = [soft[f"ys_stored{i}"] for i in range(NY)]

    with nc.Fori(0, NTILE // TILES) as r:
        with nc.Block() as block:

            @block.gpsimd
            def _(pool):
                def load_rows(i):
                    if i >= NX:
                        pool.wait_ge(t["xs_tr_done"], i - NX + 1)
                    nc.gpsimd.indirect_dma_start(xs[:, i % NX, :], None, normed_d[:, :], bass.IndirectOffsetOnAxis(fetch[:, i:i + 1], 0),
                                                 bounds_check=NB * S - 1, oob_is_err=True).then_inc(xs_loaded[i % NX], 16)

                def store_rows(i):
                    pool.wait_ge(t["ys_ready"], i + 1)
                    nc.gpsimd.indirect_dma_start(pairs_d[:, :], bass.IndirectOffsetOnAxis(send[:, i:i + 1], 0), ys[:, i % NY, :], None,
                                                 bounds_check=(2 * NT + NTILE) * P - 1, oob_is_err=True).then_inc(ys_stored[i % NY], 16)

                nc.gpsimd.tensor_copy(fetch[:, :], token_of[:, bass.ds(r * TILES, TILES)]).then_inc(t["fetch_ready"], 1)
                nc.gpsimd.tensor_copy(send[:, :], pair_of[:, bass.ds(r * TILES, TILES)]).then_inc(t["fetch_ready"], 1)
                pool.wait_ge(t["fetch_ready"], 2)
                for i in range(NX - 1):
                    load_rows(i)
                for i in range(TILES):
                    if i + NX - 1 < TILES:
                        load_rows(i + NX - 1)
                    pool.wait_ge(t["sil_ready"], i + 1)
                    pool.wait_ge(t["up_ready"], i + 1)
                    if i >= 2:
                        pool.wait_ge(t["hid_tr_done"], i - 1)
                    nc.gpsimd.tensor_tensor(hid[:, i % 2, :], up[:, i % 2, :], sil[:, i % 2, :], ALU.mult).then_inc(t["hid_ready"], 1)
                    if i >= 2:
                        store_rows(i - 2)
                store_rows(TILES - 2)
                store_rows(TILES - 1)
                for k in range(NY):
                    pool.wait_ge(ys_stored[k], (r + 1) * (16 * (TILES // NY)))

            @block.scalar
            def _(act):
                def copy_rows(i):
                    act.wait_ge(t["xs_tr_done"], i + 1)
                    if i >= 2:
                        act.wait_ge(t["h0_done"], i - 1)
                    nc.scalar.copy(xs_t[:, i % 2, :, :].rearrange("p c s -> p (c s)"), tp[:, 0:DC * P]).then_inc(t["xs_t_ready"], 1)

                def copy_hidden(i):
                    act.wait_ge(t["hid_tr_done"], i + 1)
                    if i >= 2:
                        act.wait_ge(t["out_done"], i - 1)
                    nc.scalar.copy(hid_t[:, i % 2, :, :].rearrange("p c s -> p (c s)"), hp[:, i % 2, :]).then_inc(t["hid_t_ready"], 1)

                copy_rows(0)
                for i in range(TILES):
                    if i + 1 < TILES:
                        copy_rows(i + 1)
                    act.wait_ge(t["z_ready"], i + 1)
                    if i >= 2:
                        act.wait_ge(t["hid_ready"], i - 1)
                    nc.scalar.activation(sil[:, i % 2, :], z[:, i % 2, :], ACT.Silu).then_inc(t["sil_ready"], 1)
                    if i:
                        copy_hidden(i - 1)
                copy_hidden(TILES - 1)

            @block.vector
            def _(dve):
                def finish(i, e):
                    dve.wait_ge(t["out_done"], i + 1)
                    if i >= NY:
                        dve.wait_ge(ys_stored[i % NY], r * (16 * (TILES // NY)) + 16 * (i // NY))
                    nc.vector.tensor_tensor(ys[:, i % NY, :], op[:, 0:D], b2[:, bass.ds(e * D, D)], ALU.add).then_inc(t["ys_ready"], 1)

                was = None
                for i in range(TILES):
                    e = dve.value_load(expert_of[0:1, bass.ds(r * TILES + i, 1)], min_val=0, max_val=E - 1)
                    dve.wait_ge(t["h1_done"], i + 1)
                    if i >= 2:
                        dve.wait_ge(t["sil_ready"], i - 1)
                    nc.vector.tensor_tensor(z[:, i % 2, :], h1[:, i % 2, :], b1[:, bass.ds(e * HID, HID)], ALU.add).then_inc(t["z_ready"], 1)
                    dve.wait_ge(t["h0_done"], i + 1)
                    if i >= 2:
                        dve.wait_ge(t["hid_ready"], i - 1)
                    nc.vector.tensor_tensor(up[:, i % 2, :], h0[:, i % 2, :], b0[:, bass.ds(e * HID, HID)], ALU.add).then_inc(t["up_ready"], 1)
                    if i:
                        finish(i - 1, was)
                    was = e
                finish(TILES - 1, was)

            @block.tensor
            def _(pe):
                def transpose_rows(i):
                    pe.wait_ge(xs_loaded[i % NX], r * (16 * (TILES // NX)) + 16 * (i // NX + 1))
                    if i:
                        pe.wait_ge(t["xs_t_ready"], i)
                    for c in range(DC):
                        last = nc.tensor.transpose(tp[:, c * P:(c + 1) * P], xs[:, i % NX, c * P:(c + 1) * P], ident[:, :])
                    last.then_inc(t["xs_tr_done"], 1)

                def up_product(i, e, out, wgt, done):
                    for c in range(DC):
                        last = nc.tensor.matmul(out[:, i % 2, :], xs_t[:, i % 2, c, :], wgt[:, c, bass.ds(e * HID, HID)],
                                                start=(c == 0), stop=(c == DC - 1))
                    last.then_inc(done, 1)

                def transpose_hidden(i):
                    pe.wait_ge(t["hid_ready"], i + 1)
                    if i >= 2:
                        pe.wait_ge(t["hid_t_ready"], i - 1)
                    for c in range(HC):
                        last = nc.tensor.transpose(hp[:, i % 2, c * P:(c + 1) * P], hid[:, i % 2, c * P:(c + 1) * P], ident[:, :])
                    last.then_inc(t["hid_tr_done"], 1)

                def down_products(i, e):
                    pe.wait_ge(t["hid_t_ready"], i + 1)
                    if i:
                        pe.wait_ge(t["ys_ready"], i)
                    for c in range(HC):
                        last = nc.tensor.matmul(op[:, 0:D], hid_t[:, i % 2, c, :], w2[:, c, bass.ds(e * D, D)], start=(c == 0), stop=(c == HC - 1))
                    last.then_inc(t["out_done"], 1)

                transpose_rows(0)
                was = None
                for i in range(TILES):
                    e = pe.value_load(expert_of[0:1, bass.ds(r * TILES + i, 1)], min_val=0, max_val=E - 1)
                    if i + 1 < TILES:
                        transpose_rows(i + 1)
                    pe.wait_ge(t["xs_t_ready"], i + 1)
                    if i >= 2:
                        pe.wait_ge(t["up_ready"], i - 1)
                    up_product(i, e, h1, w1, t["h1_done"])
                    if i:
                        transpose_hidden(i - 1)
                    up_product(i, e, h0, w0, t["h0_done"])
                    if i:
                        down_products(i - 1, was)
                    was = e
                transpose_hidden(TILES - 1)
                down_products(TILES - 1, was)

        end_turn(nc, t)


def moe_combine(nc, ctx, x_d, x_out_d, pairs_d, tag, weight, big):
    sb = lambda n, s, t: ctx.enter_context(nc.sbuf_tensor(f"{tag}_{n}", s, t))
    GROUPS = NT // TT
    pair = sb("pair", [P, NT, 2, D], F32)
    x = sb("xc", [P, NT, D], F32)
    t = semaphores(nc, ctx, [*(f"loaded{g}" for g in range(GROUPS)), "first_added", "added", "x_stored"], after=big)
    loaded = [t[f"loaded{g}"] for g in range(GROUPS)]
    with nc.Block() as block:

        @block.sync
        def _(sp):
            for g in range(GROUPS):
                tiles = slice(g * TT, (g + 1) * TT)
                sp.dma_start(x[:, tiles, :], token_major(x_d[g * S:(g + 1) * S, :])).then_inc(loaded[g], 16)
                sp.dma_start(pair[:, tiles, :, :], pairs_d[2 * g * S:2 * (g + 1) * S, :].rearrange("(q p k) d -> p q k d", p=P, k=2)
                             ).then_inc(loaded[g], 16)

        @block.scalar
        def _(act):
            for g in range(GROUPS):
                act.wait_ge(t["added"], g + 1)
                act.dma_start(token_major(x_out_d[g * S:(g + 1) * S, :]), x[:, g * TT:(g + 1) * TT, :]).then_inc(t["x_stored"], 16)
            act.wait_ge(t["x_stored"], 16 * GROUPS)

        @block.vector
        def _(dve):
            for g in range(GROUPS):
                dve.wait_ge(loaded[g], 32)
                for k in range(2):
                    for q in range(g * TT, (g + 1) * TT):
                        last = nc.vector.scalar_tensor_tensor(x[:, q, :], pair[:, q, k, :], weight[:, k, q:q + 1], x[:, q, :],
                                                              ALU.mult, ALU.add)
                    last.then_inc(t["added"] if k else t["first_added"], 1)
                    if k == 0:
                        dve.wait_ge(t["first_added"], g + 1)

    end_turn(nc, t)


def lay_out(**a):
    f = lambda n: np.asarray(a[n])
    idx = np.outer(np.arange(D), np.arange(D)) % D
    ang = 2 * np.pi * idx / D
    pos = np.arange(S, dtype=np.float32)[:, None]
    div = np.exp(np.arange(0, D, 2, dtype=np.float32) * np.float32(-np.log(10000.0) / D))
    pe = np.zeros((S, D), np.float32)
    pe[:, 0::2] = np.sin(pos * div)
    pe[:, 1::2] = np.cos(pos * div)
    c, d, j = np.meshgrid(np.arange(DC), np.arange(DH), np.arange(8), indexing="ij")
    perm = ((2 * j + c) * DH + d).reshape(-1)
    pick = np.zeros((96, 2 * NS, P), np.float32)
    for part in range(3):
        pick[32 * part + np.arange(2 * NS), np.arange(2 * NS)] = 1.0
    pick = pick.astype(mybir.dt.np(BF16))
    out = {
        "ident": np.eye(P, dtype=np.float32),
        "pos": pe,
        "cos": np.cos(ang).astype(np.float32), "sin": np.sin(ang).astype(np.float32), "ncos": (-np.cos(ang)).astype(np.float32),
        "w_real": f("L0_ffn_w_freq_real"), "w_imag": f("L0_ffn_w_freq_imag"), "ffn_bias": f("L0_ffn_bias"),
        "Wq": f("L0_attn_Wq")[:, perm], "Wk": f("L0_attn_Wk")[:, perm], "Wv": f("L0_attn_Wv"), "Wo": f("L0_attn_Wo"),
        "bq": f("L0_attn_bq")[perm].reshape(DC, P).T, "bk": f("L0_attn_bk")[perm].reshape(DC, P).T, "bv": f("L0_attn_bv"), "bo": f("L0_attn_bo"),
        "gamma": f("L0_attn_gamma"), "beta": f("L0_attn_beta"),
        "pick": pick, "ones": np.ones((2, H, S), mybir.dt.np(BF16)),
        "w_in": f("L1_attn_w_in"), "w_dt": f("L1_attn_w_dt"), "w_out": f("L1_attn_w_out"),
        "w_xproj3": np.concatenate([f("L1_attn_w_xproj")] * 3, axis=1),
        "ln_g": f("L1_attn_ln_g"), "ln_b": f("L1_attn_ln_b"),
        "conv_w": f("L1_attn_conv_w").reshape(IC, P, KC).transpose(1, 0, 2),
        "A_log": f("L1_attn_A_log").reshape(IC, P, NS).transpose(1, 0, 2),
        "conv_b": f("L1_attn_conv_b").reshape(IC, P).T, "b_dt": f("L1_attn_b_dt").reshape(IC, P).T,
        "skip": f("L1_attn_D").reshape(IC, P).T,
        "w0": f("L1_ffn_w0").reshape(E, HID, DC, P).transpose(3, 2, 0, 1).reshape(P, DC, E * HID),
        "w1": f("L1_ffn_w1").reshape(E, HID, DC, P).transpose(3, 2, 0, 1).reshape(P, DC, E * HID),
        "w2": f("L1_ffn_w2").reshape(E, D, HC, P).transpose(3, 2, 0, 1).reshape(P, HC, E * D),
        "b0": f("L1_ffn_b0").reshape(E * HID), "b1": f("L1_ffn_b1").reshape(E * HID), "b2": f("L1_ffn_b2").reshape(E * D),
        "gate_w": f("L1_ffn_gate_w").reshape(E, DC, P).transpose(2, 1, 0), "gate_b": f("L1_ffn_gate_b"),
        "lower": np.tril(np.ones((E, E), np.float32), -1),
        "before": np.triu(np.ones((P, P), np.float32), 1),
        "keep": np.tile(np.arange(NT) > 0, (E, 1)).astype(np.float32),
        "step": (P * np.arange(NT)).astype(np.float32), "number": np.arange(NTILE, dtype=np.float32),
        "lane": np.arange(P, dtype=np.float32), 
        "code": (2 * (np.arange(NT) * P + np.arange(P)[:, None])[:, None, :] + np.arange(2)[:, None] + 1).astype(np.float32),
        "behind": (2 * NB * S + 1 + np.arange(NTILE) * P + np.arange(P)[:, None]).astype(np.float32),
    }
    return {k: np.ascontiguousarray(v) for k, v in out.items()}


def build(nc, w, out_d):
    rows = lambda name: nc.dram_tensor(name, (NB * S, D), F32).ap()
    x3, x5, normed = rows("x3_rows"), rows("x5_rows"), rows("normed_rows")
    pairs = nc.dram_tensor("pair_rows", ((2 * NT + NTILE) * P, D), F32).ap()
    attention_stage(nc, w["x"], x3, w)
    with ExitStack() as ctx:
        weight = ctx.enter_context(nc.sbuf_tensor("moe1_weight", [P, 2, NT], F32))
        moe_stage(nc, x3, None, w, normed, pairs, weight, 0, "moe1")
        mamba_stage(nc, x3, x5, w, pairs, weight)
    with ExitStack() as ctx:
        weight = ctx.enter_context(nc.sbuf_tensor("moe2_weight", [P, 2, NT], F32))
        moe_stage(nc, x5, out_d, w, normed, pairs, weight, 1, "moe2")


def kernel(**inputs):
    import concourse.bacc as bacc
    from concourse.bass_utils import run_bass_kernel_spmd

    arrays = {"in_" + k: v for k, v in lay_out(**inputs).items()}
    arrays["in_x"] = np.ascontiguousarray(np.asarray(inputs["L0_attn_x"]).reshape(NB * S, D))
    nc = bacc.Bacc("TRN2", target_bir_lowering=False, num_devices=1)
    w = {k[3:]: nc.dram_tensor(k, a.shape, mybir.dt.from_np(a.dtype), kind="ExternalInput").ap() for k, a in arrays.items()}
    out_d = nc.dram_tensor("out_rows", (NB * S, D), F32, kind="ExternalOutput").ap()
    build(nc, w, out_d)
    r = run_bass_kernel_spmd(nc, [arrays], core_ids=[0])
    return r.results[0]["out_rows"].reshape(NB, S, D)
```
